# Optimizing a Trainium2 kernel written in Bass

```python
import numpy as np
import jax
import jax.numpy as jnp

def _softmax(x, axis=-1):
    return jax.nn.softmax(x, axis=axis)

def _gelu(x):
    return jax.nn.gelu(x, approximate=True)

def _silu(x):
    return jax.nn.silu(x)

def _sigmoid(x):
    return jax.nn.sigmoid(x)

def _layernorm(x, axis=-1, eps=1e-05):
    m = jnp.mean(x, axis=axis, keepdims=True)
    v = jnp.var(x, axis=axis, keepdims=True)
    return (x - m) / jnp.sqrt(v + eps)

def _scatter_add(tgt, idx, src, axis=0):
    return tgt.at[idx].add(src)

def _segment_sum(src, seg, n):
    return jax.ops.segment_sum(src, seg, n)
kernel_name = 'mk_gnn_preln_d4_gnn_r32_f88493'

def setup_inputs(seed: int=0):
    np.random.seed(seed)
    _w = jnp.asarray

    def _rec_inputs():
        import jax
        import jax.numpy as jnp
        _gk = jax.random.key(seed)
        x = -0.0003713 + 1 * jax.random.normal(jax.random.fold_in(_gk, 1), (3125, 128), jnp.float32)
        _s = jax.random.randint(jax.random.fold_in(_gk, 2), (50000,), 0, 3125, jnp.int32)
        _d = jax.random.randint(jax.random.fold_in(_gk, 3), (50000,), 0, 3125, jnp.int32)
        _loop = jnp.arange(3125, dtype=jnp.int32)
        src = jnp.concatenate([_s, _d, _loop])
        dst = jnp.concatenate([_d, _s, _loop])
        _o = jnp.argsort(dst, stable=True)
        src = src[_o]
        dst = dst[_o]
        edge_attr_32 = jax.random.uniform(jax.random.fold_in(_gk, 12), (103125, 32), jnp.float32, 0.0, 1)
        edge_weight = jax.random.uniform(jax.random.fold_in(_gk, 14), (103125,), jnp.float32, 0.0, 0.999999)
        return (x, src, dst, edge_attr_32, edge_weight)
    x, src, dst, edge_attr_32, edge_weight = _rec_inputs()

    def _L0_gnn_setup():
        import jax, jax.numpy as jnp
        import numpy as np
        N = 3125
        E = 50000
        IN_D = 128
        OUT_D = 32
        H = 4
        NEG_SLOPE = 0.2
        key = jax.random.key(seed)
        k0, k1, k2, k3, k4 = jax.random.split(key, 5)
        features = jax.random.normal(k0, (N, IN_D), dtype=jnp.float32)
        edge_index = jax.random.randint(k1, (2, E), 0, N, dtype=jnp.int32)
        W = jax.random.normal(k2, (OUT_D, IN_D), dtype=jnp.float32) * 0.05
        b = jnp.zeros((OUT_D,), dtype=jnp.float32)
        att_src = jax.random.normal(k3, (H, OUT_D), dtype=jnp.float32) * 0.05
        att_dst = jax.random.normal(k4, (H, OUT_D), dtype=jnp.float32) * 0.05
        return {'features': features, 'W': W, 'b': b, 'att_src': att_src, 'att_dst': att_dst, 'edge_index': edge_index}
    _L0_gnn_all = _L0_gnn_setup()
    _L0_gnn_in = {k: v for k, v in _L0_gnn_all.items() if k in ('W', 'b', 'att_src', 'att_dst')}
    del _L0_gnn_all

    def _L1_gnn_setup():
        import jax, jax.numpy as jnp
        import numpy as np
        N_NODES = 3125
        key = jax.random.key(seed)
        k1, k2, k3 = jax.random.split(key, 3)
        x = jax.random.normal(k1, (N_NODES, 128), dtype=jnp.float32)
        edge_src = jax.random.randint(k2, (20000,), 0, N_NODES, dtype=jnp.int64)
        edge_dst = jax.random.randint(k3, (20000,), 0, N_NODES, dtype=jnp.int64)
        return {'x': x, 'edge_src': edge_src, 'edge_dst': edge_dst}
    _L1_gnn_all = _L1_gnn_setup()
    _L1_gnn_in = {k: v for k, v in _L1_gnn_all.items() if k in ()}
    del _L1_gnn_all

    def _L2_gnn_setup():
        import jax, jax.numpy as jnp
        import numpy as np
        LOG2 = float(np.log(2.0))

        def ssp(v):
            return jax.nn.softplus(v) - jnp.asarray(LOG2, v.dtype)
        key = jax.random.key(seed)
        ks = jax.random.split(key, 16)
        N, B, F, R, P = (3125, 128, 64, 32, 50000)
        inp = {'x': jax.random.normal(ks[0], (N, B), jnp.float32), 'f_ij': jax.random.uniform(ks[1], (P, R), jnp.float32), 'rcut_ij': jax.random.uniform(ks[2], (P,), jnp.float32), 'pairlist': jax.random.randint(ks[3], (2, P), 0, N, jnp.int64), 'w_in': jax.random.normal(ks[4], (B, F), jnp.float32) * (1.0 / np.sqrt(B)), 'b_in': jnp.zeros((F,), jnp.float32), 'w_f1': jax.random.normal(ks[5], (R, F), jnp.float32) * (1.0 / np.sqrt(R)), 'b_f1': jnp.zeros((F,), jnp.float32), 'w_f2': jax.random.normal(ks[6], (F, F), jnp.float32) * (1.0 / np.sqrt(F)), 'b_f2': jnp.zeros((F,), jnp.float32), 'w_o1': jax.random.normal(ks[7], (F, B), jnp.float32) * (1.0 / np.sqrt(F)), 'b_o1': jnp.zeros((B,), jnp.float32), 'w_o2': jax.random.normal(ks[8], (B, B), jnp.float32) * (1.0 / np.sqrt(B)), 'b_o2': jnp.zeros((B,), jnp.float32)}
        return inp
    _L2_gnn_all = _L2_gnn_setup()
    _L2_gnn_in = {k: v for k, v in _L2_gnn_all.items() if k in ('w_in', 'b_in', 'w_f1', 'b_f1', 'w_f2', 'b_f2', 'w_o1', 'b_o1', 'w_o2', 'b_o2')}
    del _L2_gnn_all

    def _L3_gnn_setup():
        import jax, jax.numpy as jnp
        import numpy as np
        N = 50000
        E = 25000
        HID = 128
        NH = 8
        HD = HID // NH
        EPS = 1e-05

        def _layernorm(x, g, b):
            mu = jnp.mean(x, axis=-1, keepdims=True)
            var = jnp.mean(jnp.square(x - mu), axis=-1, keepdims=True)
            return (x - mu) * jax.lax.rsqrt(var + EPS) * g + b

        def _gmha(edge_index, h, WQ, bQ, WK, bK, WV, bV):
            Q = (h @ WQ + bQ).reshape(-1, NH, HD)
            K = (h @ WK + bK).reshape(-1, NH, HD)
            V = (h @ WV + bV).reshape(-1, NH, HD)
            src, dst = (edge_index[0], edge_index[1])
            q_dst = Q[dst]
            k_src = K[src]
            v_src = V[src]
            score = jnp.sum(q_dst * k_src, axis=-1) / np.sqrt(HD)
            score = jnp.clip(score, -5.0, 5.0)
            attn = jax.nn.softmax(score, axis=0)
            msg = attn[..., None] * v_src
            h_out = jnp.zeros_like(Q).at[dst].add(msg)
            return h_out.reshape(-1, NH * HD)
        key = jax.random.key(seed)
        ks = jax.random.split(key, 16)
        s = 1.0 / np.sqrt(HID)

        def lin(k):
            kw, kb = jax.random.split(k)
            W = jax.random.uniform(kw, (HID, HID), jnp.float32, -s, s)
            b = jax.random.uniform(kb, (HID,), jnp.float32, -s, s)
            return (W, b)
        WQ, bQ = lin(ks[0])
        WK, bK = lin(ks[1])
        WV, bV = lin(ks[2])
        WO, bO = lin(ks[3])
        W1, b1 = lin(ks[4])
        W2, b2 = lin(ks[5])
        return {'h': jax.random.normal(ks[6], (N, HID), jnp.float32), 'edge_index': jax.random.randint(ks[7], (2, E), 0, N, jnp.int32), 'WQ': WQ, 'bQ': bQ, 'WK': WK, 'bK': bK, 'WV': WV, 'bV': bV, 'WO': WO, 'bO': bO, 'W1': W1, 'b1': b1, 'W2': W2, 'b2': b2, 'ln1_g': jnp.ones((HID,), jnp.float32), 'ln1_b': jnp.zeros((HID,), jnp.float32), 'ln2_g': jnp.ones((HID,), jnp.float32), 'ln2_b': jnp.zeros((HID,), jnp.float32)}
    _L3_gnn_all = _L3_gnn_setup()
    _L3_gnn_in = {k: v for k, v in _L3_gnn_all.items() if k in ('WQ', 'bQ', 'WK', 'bK', 'WV', 'bV', 'WO', 'bO', 'W1', 'b1', 'W2', 'b2', 'ln1_g', 'ln1_b', 'ln2_g', 'ln2_b')}
    del _L3_gnn_all
    return {'x': x, 'src': src, 'dst': dst, 'edge_attr_32': edge_attr_32, 'edge_weight': edge_weight, 'L0_gnn_W': _L0_gnn_in['W'], 'L0_gnn_b': _L0_gnn_in['b'], 'L0_gnn_att_src': _L0_gnn_in['att_src'], 'L0_gnn_att_dst': _L0_gnn_in['att_dst'], 'L2_gnn_w_in': _L2_gnn_in['w_in'], 'L2_gnn_b_in': _L2_gnn_in['b_in'], 'L2_gnn_w_f1': _L2_gnn_in['w_f1'], 'L2_gnn_b_f1': _L2_gnn_in['b_f1'], 'L2_gnn_w_f2': _L2_gnn_in['w_f2'], 'L2_gnn_b_f2': _L2_gnn_in['b_f2'], 'L2_gnn_w_o1': _L2_gnn_in['w_o1'], 'L2_gnn_b_o1': _L2_gnn_in['b_o1'], 'L2_gnn_w_o2': _L2_gnn_in['w_o2'], 'L2_gnn_b_o2': _L2_gnn_in['b_o2'], 'L3_gnn_WQ': _L3_gnn_in['WQ'], 'L3_gnn_bQ': _L3_gnn_in['bQ'], 'L3_gnn_WK': _L3_gnn_in['WK'], 'L3_gnn_bK': _L3_gnn_in['bK'], 'L3_gnn_WV': _L3_gnn_in['WV'], 'L3_gnn_bV': _L3_gnn_in['bV'], 'L3_gnn_WO': _L3_gnn_in['WO'], 'L3_gnn_bO': _L3_gnn_in['bO'], 'L3_gnn_W1': _L3_gnn_in['W1'], 'L3_gnn_b1': _L3_gnn_in['b1'], 'L3_gnn_W2': _L3_gnn_in['W2'], 'L3_gnn_b2': _L3_gnn_in['b2'], 'L3_gnn_ln1_g': _L3_gnn_in['ln1_g'], 'L3_gnn_ln1_b': _L3_gnn_in['ln1_b'], 'L3_gnn_ln2_g': _L3_gnn_in['ln2_g'], 'L3_gnn_ln2_b': _L3_gnn_in['ln2_b']}

def reference(x, src, dst, edge_attr_32, edge_weight, L0_gnn_W, L0_gnn_b, L0_gnn_att_src, L0_gnn_att_dst, L2_gnn_w_in, L2_gnn_b_in, L2_gnn_w_f1, L2_gnn_b_f1, L2_gnn_w_f2, L2_gnn_b_f2, L2_gnn_w_o1, L2_gnn_b_o1, L2_gnn_w_o2, L2_gnn_b_o2, L3_gnn_WQ, L3_gnn_bQ, L3_gnn_WK, L3_gnn_bK, L3_gnn_WV, L3_gnn_bV, L3_gnn_WO, L3_gnn_bO, L3_gnn_W1, L3_gnn_b1, L3_gnn_W2, L3_gnn_b2, L3_gnn_ln1_g, L3_gnn_ln1_b, L3_gnn_ln2_g, L3_gnn_ln2_b):
    import jax
    import jax.numpy as jnp

    def _L0_gnn_ref(features, W, b, att_src, att_dst, edge_index):
        import jax, jax.numpy as jnp
        import numpy as np
        N = 3125
        E = 50000
        IN_D = 128
        OUT_D = 32
        H = 4
        NEG_SLOPE = 0.2
        src = edge_index[0]
        dst = edge_index[1]
        Wh = features @ W.T + b
        a_src = Wh @ att_src.T
        a_dst = Wh @ att_dst.T
        e = a_src[src] + a_dst[dst]
        e = jnp.where(e > 0, e, NEG_SLOPE * e)
        e = e - jnp.max(e)
        exp_e = jnp.exp(e)
        denom = jax.ops.segment_sum(exp_e, src, num_segments=N)
        alpha = exp_e / (denom[src] + 1e-16)
        msg = Wh[src][:, None, :] * alpha[:, :, None]
        out = jax.ops.segment_sum(msg, dst, num_segments=N)
        return out.reshape(N, H * OUT_D)

    def _L1_gnn_ref(x, edge_src, edge_dst):
        import jax, jax.numpy as jnp
        import numpy as np
        N_NODES = 3125
        n = x.shape[0]
        gathered = x[edge_src]
        sums = jax.ops.segment_sum(gathered, edge_dst, num_segments=n)
        counts = jax.ops.segment_sum(jnp.ones(edge_dst.shape, dtype=x.dtype), edge_dst, num_segments=n)
        denom = jnp.maximum(counts, 1.0)[:, None]
        return sums / denom

    def _L2_gnn_ref(x, f_ij, rcut_ij, pairlist, w_in, b_in, w_f1, b_f1, w_f2, b_f2, w_o1, b_o1, w_o2, b_o2):
        import jax, jax.numpy as jnp
        import numpy as np
        LOG2 = float(np.log(2.0))

        def ssp(v):
            return jax.nn.softplus(v) - jnp.asarray(LOG2, v.dtype)
        n_atoms = x.shape[0]
        h = x @ w_in + b_in
        Wij = ssp(f_ij @ w_f1 + b_f1) @ w_f2 + b_f2
        Wij = Wij * rcut_ij[:, None]
        idx_i, idx_j = (pairlist[0], pairlist[1])
        x_ij = h[idx_j] * Wij
        agg = jax.ops.segment_sum(x_ij, idx_i, num_segments=n_atoms)
        out = ssp(agg @ w_o1 + b_o1) @ w_o2 + b_o2
        return out

    def _L3_gnn_ref(h, edge_index, WQ, bQ, WK, bK, WV, bV, WO, bO, W1, b1, W2, b2, ln1_g, ln1_b, ln2_g, ln2_b):
        import jax, jax.numpy as jnp
        import numpy as np
        N = 50000
        E = 25000
        HID = 128
        NH = 8
        HD = HID // NH
        EPS = 1e-05

        def _layernorm(x, g, b):
            mu = jnp.mean(x, axis=-1, keepdims=True)
            var = jnp.mean(jnp.square(x - mu), axis=-1, keepdims=True)
            return (x - mu) * jax.lax.rsqrt(var + EPS) * g + b

        def _gmha(edge_index, h, WQ, bQ, WK, bK, WV, bV):
            Q = (h @ WQ + bQ).reshape(-1, NH, HD)
            K = (h @ WK + bK).reshape(-1, NH, HD)
            V = (h @ WV + bV).reshape(-1, NH, HD)
            src, dst = (edge_index[0], edge_index[1])
            q_dst = Q[dst]
            k_src = K[src]
            v_src = V[src]
            score = jnp.sum(q_dst * k_src, axis=-1) / np.sqrt(HD)
            score = jnp.clip(score, -5.0, 5.0)
            attn = jax.nn.softmax(score, axis=0)
            msg = attn[..., None] * v_src
            h_out = jnp.zeros_like(Q).at[dst].add(msg)
            return h_out.reshape(-1, NH * HD)
        h_rc = h
        a = _gmha(edge_index, h, WQ, bQ, WK, bK, WV, bV)
        a = a @ WO + bO
        x = _layernorm(h_rc + a, ln1_g, ln1_b)
        f = jax.nn.relu(x @ W1 + b1) @ W2 + b2
        return _layernorm(x + f, ln2_g, ln2_b)
    edge_index = jnp.stack([src, dst])
    h = jnp.maximum(_layernorm(x, axis=-1), 0.0)
    x = x + _L0_gnn_ref(h, L0_gnn_W, L0_gnn_b, L0_gnn_att_src, L0_gnn_att_dst, edge_index)
    h = jnp.maximum(_layernorm(x, axis=-1), 0.0)
    x = x + _L1_gnn_ref(h, src, dst)
    h = jnp.maximum(_layernorm(x, axis=-1), 0.0)
    x = x + _L2_gnn_ref(h, edge_attr_32, edge_weight, edge_index, L2_gnn_w_in, L2_gnn_b_in, L2_gnn_w_f1, L2_gnn_b_f1, L2_gnn_w_f2, L2_gnn_b_f2, L2_gnn_w_o1, L2_gnn_b_o1, L2_gnn_w_o2, L2_gnn_b_o2)
    h = jnp.maximum(_layernorm(x, axis=-1), 0.0)
    x = x + _L3_gnn_ref(h, edge_index, L3_gnn_WQ, L3_gnn_bQ, L3_gnn_WK, L3_gnn_bK, L3_gnn_WV, L3_gnn_bV, L3_gnn_WO, L3_gnn_bO, L3_gnn_W1, L3_gnn_b1, L3_gnn_W2, L3_gnn_b2, L3_gnn_ln1_g, L3_gnn_ln1_b, L3_gnn_ln2_g, L3_gnn_ln2_b)
    return x

_drawn_inputs = setup_inputs


def setup_inputs(seed=0):
    import zlib

    import numpy as np

    out = dict(_drawn_inputs(seed))
    spreads = {'L0_gnn_b': (0.0, 0.1),
     'L2_gnn_b_in': (0.0, 0.1),
     'L2_gnn_b_f1': (0.0, 0.1),
     'L2_gnn_b_f2': (0.0, 0.1),
     'L2_gnn_b_o1': (0.0, 0.1),
     'L2_gnn_b_o2': (0.0, 0.1),
     'L3_gnn_ln1_g': (1.0, 0.2),
     'L3_gnn_ln1_b': (0.0, 0.1),
     'L3_gnn_ln2_g': (1.0, 0.2),
     'L3_gnn_ln2_b': (0.0, 0.1)}
    factors = {'L0_gnn_att_src': 104.8,
     'L0_gnn_att_dst': 5.546,
     'L3_gnn_WQ': 64.0,
     'L3_gnn_bQ': 200.0,
     'L3_gnn_WK': 64.0,
     'L3_gnn_bK': 192.952,
     'L3_gnn_WV': 64.0,
     'L3_gnn_bV': 64.0,
     'L3_gnn_WO': 64.0,
     'L3_gnn_b1': 6.772,
     'L3_gnn_b2': 2.788}
    for name, (base, spread) in spreads.items():
        noise = np.random.default_rng([zlib.crc32(name.encode()), seed]).standard_normal(out[name].shape)
        drawn = base * np.exp(spread * noise) if base else spread * noise
        out[name] = jnp.asarray(drawn.astype(out[name].dtype))
    for name, factor in factors.items():
        out[name] = (out[name] * factor).astype(out[name].dtype)
    return out
```

```python
from contextlib import ExitStack
import math

import concourse.bass as bass
from concourse import mybir

F32 = mybir.dt.float32
BF16 = mybir.dt.bfloat16
F16 = mybir.dt.float16
I32 = mybir.dt.int32
U32 = mybir.dt.uint32
ALU = mybir.AluOpType
ACT = mybir.ActivationFunctionType
RMAX = bass.bass_isa.ReduceOp.max
RADD = bass.bass_isa.ReduceOp.add
AXX = mybir.AxisListType.X

P = 128
N = 3125
D = 128
E = 103125
NCH = 7
CH = 448
NP = NCH * CH
HALF = NP // 2
NB = 112
NBLK = NP // NB
BPC = CH // NB
TILES = -(-E // P)
LASTE = E - (TILES - 1) * P
G = 13
BODY = 2 * G
ITERS = TILES // BODY
IB = -(-TILES // P)
H0 = 4
O0 = 32
R = 32
F2 = 64
NH = 8
HD = D // NH
SUB = 4
SUBS = [(k, min(SUB, G - k)) for k in range(0, G, SUB)]
NSUB = len(SUBS)
EPS = 1e-5
LOG2 = float(math.log(2.0))
BIG = 1e30
CREDIT = BODY

assert TILES == ITERS * BODY

STEPS = [
    "iota", "iota_h", "x_T", "x_copy",
    "dst_f", "dst_T", "dst_copy", "src_f", "src_T", "src_copy", "w_f", "w_T", "w_copy",
    "keys", "wT_T", "wT_copy",
]


def ln_steps(n):
    return [f"{n}_mean", f"{n}_center", f"{n}_square", f"{n}_var", f"{n}_std", f"{n}_recip", f"{n}_out"]


def table_steps(n):
    return [f"{n}_{s}{q}" for q in range(NBLK // NCH) for s in ("mm", "cp")]


STEPS += ln_steps("ln0") + ["whT_mm", "whT_cp"] + table_steps("ta") + table_steps("tw")
STEPS += ["passA", "cnt_cp", "logit_pad", "logit_leaky", "logit_max", "logit_all", "logit_neg", "logit_exp",
          "exp_b1", "exp_r1", "exp_b2", "exp_b3"]
STEPS += ["passB", "den_cp", "den_mm", "den_eps", "den_recip", "passC", "x1"]
STEPS += ln_steps("ln1") + table_steps("th") + ["passD", "mean_max", "mean_recip", "mean_mul", "x2"]
STEPS += ln_steps("ln2") + table_steps("t2") + ["passE", "agg_cp", "o1_mm"]
STEPS += ["o1_relu", "o1_abs", "o1_exp", "o1_ln", "o1_sum", "o2_mm", "x3"]
STEPS += ln_steps("ln3") + table_steps("tq") + table_steps("tk") + table_steps("tv") + ["passF"]
STEPS += ["z_sum", "z_all", "z_recip", "z_head", "z_red", "att_cp", "wo_mm", "wo_add"]
STEPS += ln_steps("ln4") + ["g1", "w1_mm", "w1_relu", "w2_mm", "w2_add"] + ln_steps("ln5") + ["g2", "x4"]
STEPS += [f"fin_{s}{q}" for q in range(NBLK // NCH) for s in ("mm", "cp")]
AT = {name: n + 1 for n, name in enumerate(STEPS)}


def build(nc, t, out):
    ctx = ExitStack()
    with ctx:
        def sb(name, shape, dt):
            return ctx.enter_context(nc.sbuf_tensor(name, shape, dt))

        def sem(name):
            return ctx.enter_context(nc.semaphore(name))

        tab_a = nc.dram_tensor("tab_a", (NP, 2 * H0), F32).ap()
        tab_w = nc.dram_tensor("tab_w", (NP, O0 + H0), F32).ap()
        tab_h = nc.dram_tensor("tab_h", (NP, D), F32).ap()
        tab_2 = nc.dram_tensor("tab_2", (NP, F2), F32).ap()
        tab_q = nc.dram_tensor("tab_q", (NP, D), F32).ap()
        tab_kv = nc.dram_tensor("tab_kv", (NP, 2 * D), F32).ap()

        acc = ctx.enter_context(nc.psum_tensor("acc", [P, NCH, 512], F32))
        small = ctx.enter_context(nc.psum_tensor("small", [P, 512], F32))

        def nodes(ap):
            return ap.rearrange("p (c n) -> p c n", c=NCH)

        xT = sb("xT", [P, NP], F32)
        hT = sb("hT", [P, NP], F32)
        va = sb("va", [P, NP], F32)
        vb = sb("vb", [P, NP], F32)
        cnt = sb("cnt", [P, NP], F32)
        tabs = sb("tabs", [NB, NBLK, D], F32)

        EC = IB * P
        ew = sb("ew", [P, EC], F32)
        dst_key = sb("dst_key", [P, TILES], F32)
        src_key = sb("src_key", [P, TILES], F32)
        dst_idx = sb("dst_idx", [P, TILES], I32)
        src_idx = sb("src_idx", [P, TILES], I32)
        padneg = sb("padneg", [P, 1], F32)
        ed = sb("ed", [P, TILES * H0], F32)
        e4 = ed[:, :]

        ga = sb("ga", [P, 2, G, 2 * D], F32)
        gb = sb("gb", [P, 2, G, D], F32)
        msg = sb("msg", [P, G * D], F32)
        res = sb("res", [P, G * D], F32)
        parts = sb("parts", [P, 2, 3, G * D], BF16)
        sc = sb("sc", [P, G, NH], F32)
        stage_i = parts[:, :, :, :].rearrange("p a s f -> p (a s f)")[:, 0:2 * EC].bitcast(I32)\
            .rearrange("p (b e) -> p b e", e=P)
        stage_f = cnt[:, 0:EC].rearrange("p (b e) -> p b e", e=P)
        dstf = msg[:, 0:EC]
        srcf = res[:, 0:EC]
        exp_parts = ga[:, :, :, :].rearrange("p a k f -> p (a k f)").bitcast(BF16)[:, 0:TILES * 3 * H0]\
            .rearrange("p (t s) -> p t s", s=3 * H0)
        lk = gb[:, :, :, :].rearrange("p a k f -> p (a k f)")[:, 0:TILES * H0]
        idx_a = sb("idx_a", [P, 2, G], I32)
        idx_b = sb("idx_b", [P, 2, G], I32)
        onehot = sb("onehot", [P, 2, NP], BF16)
        alpha = sb("alpha", [P, G * H0], F32)
        ex = sb("ex", [P, G, NH], F32)
        exv = sb("exv", [P, G, NH], F32)
        zacc = sb("zacc", [P, G, NH], F32)
        attrT, hid, hid_r, hid_e = (vb[0:rows_, n * SUB * P:(n + 1) * SUB * P]
                                    for n, rows_ in enumerate((R, F2, F2, F2)))

        iota_i = vb[:, :].bitcast(I32)
        iota_h = sb("iota_h", [P, NP], F16)
        ident = sb("ident", [P, P], F32)
        avg = sb("avg", [P, P], F32)
        ones_bf = sb("ones_bf", [P, P], BF16)
        ones_row = sb("ones_row", [1, P], F32)
        zero_bf = sb("zero_bf", [P, CH], BF16)
        eps_col = sb("eps_col", [P, 1], F32)
        sel = sb("sel", [3 * H0, H0], F32)
        headm = sb("headm", [P, NH], F32)
        colred = sb("colred", [P, 4], F32)
        zsum = sb("zsum", [P, NH], F32)
        zall = sb("zall", [P, NH], F32)
        zrec = sb("zrec", [P, NH], F32)
        zhm = sb("zhm", [P, NH], F32)

        w0 = sb("w0", [O0, D], F32)
        w0T = sb("w0T", [D, O0], F32)
        att = sb("att", [2 * H0, O0], F32)
        attT = sb("attT", [O0, 2 * H0], F32)
        w_in = sb("w_in", [D, F2], F32)
        w_f1 = sb("w_f1", [R, F2], F32)
        w_f2 = sb("w_f2", [F2, F2], F32)
        w_o1 = sb("w_o1", [2 * F2, D], F32)
        w_o2 = sb("w_o2", [D, D], F32)
        wsq = sb("wsq", [D, 6, D], F32)
        SQ = ["WQ", "WK", "WV", "WO", "W1", "W2"]
        rows = sb("rows", [1, O0 + 2 * F2 + 3 * D], F32)
        ROW = {}
        at = 0
        for name, width in (("L0_gnn_b", O0), ("L2_gnn_b_in", F2), ("L2_gnn_b_f2", F2),
                            ("L3_gnn_bQ", D), ("L3_gnn_bK", D), ("L3_gnn_bV", D)):
            ROW[name] = rows[0:1, at:at + width]
            at += width
        COLS = ["L0_gnn_b", "L2_gnn_b_f1", "L2_gnn_b_o1", "L2_gnn_b_o2", "L3_gnn_bO", "L3_gnn_b1", "L3_gnn_b2",
                "L3_gnn_ln1_g", "L3_gnn_ln1_b", "L3_gnn_ln2_g", "L3_gnn_ln2_b"]
        cols = sb("cols", [P, len(COLS)], F32)

        def col(name):
            n = COLS.index(name)
            k = t[name].shape[0]
            return cols[0:k, n:n + 1]

        node_step = sem("node_step")
        loaded = sem("loaded")
        idx_loaded = sem("idx_loaded")
        pads_set = sem("pads_set")
        tab_done = sem("tab_done")
        out_done = sem("out_done")
        const_step = sem("const_step")
        const_v = sem("const_v")
        z_part = sem("z_part")
        z_ready = sem("z_ready")
        attr_in = [sem("attr_in0"), sem("attr_in1")]
        attr_used = sem("attr_used")
        flt_T = sem("flt_T")
        flt_Tc = sem("flt_Tc")
        flt_h = sem("flt_h")
        flt_abs = sem("flt_abs")
        flt_exp = sem("flt_exp")
        flt_ln = sem("flt_ln")
        flt_hid = sem("flt_hid")
        flt_W = sem("flt_W")
        flt_m = sem("flt_m")

        def heads(ap):
            return ap.rearrange("p (t h) -> p t h", h=H0)

        e4h, lkh = heads(e4), heads(lk)

        def e4h_at(tile):
            return heads(ed[:, bass.ds(tile * H0, G * H0)])

        def exp_group(b):
            return parts[:, b, 0, 0:G * 3 * H0].rearrange("p (k h) -> p k h", k=G)

        def msg_wide(b):
            return msg[:, :].rearrange("p (k f) -> p k f", f=D)

        def msg_narrow(b):
            return msg[:, 0:G * F2].rearrange("p (k f) -> p k f", f=F2)

        def res_of(m):
            f = m.shape[2]
            return res[:, 0:G * f].rearrange("p (k f) -> p k f", f=f)

        def parts_wide(b):
            return [parts[:, b, s, :].rearrange("p (k f) -> p k f", f=D) for s in range(3)]

        def parts_narrow(b):
            both = parts[:, b, 0, :].rearrange("p (k f) -> p k f", f=D)
            return [both[:, :, 0:F2], both[:, :, F2:D], parts[:, b, 1, 0:G * F2].rearrange("p (k f) -> p k f", f=F2)]

        class Pass:

            def __init__(self, q, gathers):
                self.gathers = gathers
                self.idx_staged = sem(f"idx_staged_{q}")
                self.gathered = [sem(f"gathered0_{q}"), sem(f"gathered1_{q}")]
                self.taken = sem(f"taken_{q}")
                self.msg = sem(f"msg_{q}")
                self.part1 = sem(f"part1_{q}")
                self.rest1 = sem(f"rest1_{q}")
                self.part2 = sem(f"part2_{q}")
                self.part3 = sem(f"part3_{q}")
                self.oh_ready = sem(f"oh_ready_{q}")
                self.oh_used = sem(f"oh_used_{q}")
                self.score = [sem(f"score{n}_{q}") for n in range(4)]
                self.weight = sem(f"weight_{q}")

            def have_rows(self, i):
                return (i + 1) * (16 * G * self.gathers)

        pA, pB, pC, pD, pE, pF = (Pass(q, n) for q, n in zip("ABCDEF", (2, 0, 1, 1, 1, 2)))

        block = ctx.enter_context(nc.Block())
        FULL = N // NB
        REST = N - FULL * NB
        LASTQ = NBLK // NCH - 1

        def begin(eng, name):
            if AT[name] > 1:
                eng.wait_ge(node_step, AT[name] - 1)

        def dram_tab(table):
            return table.rearrange("(b p) f -> p b f", p=NB)

        xv = t["x"]
        loads = [(tabs[:, 0:FULL, :], xv[0:FULL * NB, :].rearrange("(b p) f -> p b f", p=NB)),
                 (tabs[0:REST, FULL, :], xv[FULL * NB:N, :]),
                 (w0[:, :], t["L0_gnn_W"]), (att[0:H0, :], t["L0_gnn_att_src"]),
                 (att[H0:2 * H0, :], t["L0_gnn_att_dst"]), (w_in[:, :], t["L2_gnn_w_in"]),
                 (w_f1[:, :], t["L2_gnn_w_f1"]), (w_f2[:, :], t["L2_gnn_w_f2"]),
                 (w_o1[0:F2, :], t["L2_gnn_w_o1"]), (w_o1[F2:2 * F2, :], t["L2_gnn_w_o1"]),
                 (w_o2[:, :], t["L2_gnn_w_o2"])]
        loads += [(wsq[:, n, :], t["L3_gnn_" + name]) for n, name in enumerate(SQ)]
        loads += [(ap, t[name].rearrange("(o f) -> o f", o=1)) for name, ap in ROW.items()]
        loads += [(col(name), t[name].rearrange("(f o) -> f o", o=1)) for name in COLS]
        LOADED = 16 * len(loads)

        @block.sync
        def _(sp):
            sp.wait_ge(pads_set, 2)
            for dst_ap, src_ap in loads:
                sp.dma_start(dst_ap, src_ap).then_inc(loaded, 16)

            whole = (IB - 1) * P
            last = TILES - 1 - whole
            for name, staged, after, pads in (("dst", stage_i, None, 2), ("src", stage_i, "dst_f", 3),
                                              ("edge_weight", stage_f, "src_copy", 4)):
                if after:
                    sp.wait_ge(node_step, AT[after])
                    sp.wait_ge(pads_set, pads)
                v = t[name]
                sp.dma_start(staged[:, 0:IB - 1, :], v[0:whole * P].rearrange("(b r e) -> r b e", r=P, e=P))\
                    .then_inc(idx_loaded, 16)
                sp.dma_start(staged[0:last, IB - 1, :], v[whole * P:(whole + last) * P].rearrange("(r e) -> r e", e=P))\
                    .then_inc(idx_loaded, 16)
                sp.dma_start(staged[last:last + 1, IB - 1, 0:LASTE],
                             v[(whole + last) * P:E].rearrange("(r e) -> r e", r=1)).then_inc(idx_loaded, 16)

            def store(table, width, stage, c0=0):
                sp.wait_ge(node_step, AT[stage])
                sp.dma_start(dram_tab(table)[:, :, c0:c0 + width], tabs[:, :, 0:width]).then_inc(tab_done, 16)

            store(tab_a, 2 * H0, f"ta_cp{LASTQ}")
            store(tab_w, O0 + H0, "den_recip")
            store(tab_h, D, f"th_cp{LASTQ}")
            store(tab_2, F2, f"t2_cp{LASTQ}")

            begin(sp, "passE")
            av = t["edge_attr_32"]

            def attributes(b, first, edges):
                if b == 0:
                    sp.dma_start(gb[:, b, :, 0:R], av[bass.ds(first, G * P), :].rearrange("(k e) f -> e k f", e=P))\
                        .then_inc(attr_in[b], 16)
                else:
                    sp.dma_start(gb[:, b, 0:G - 1, 0:R],
                                 av[bass.ds(first, (G - 1) * P), :].rearrange("(k e) f -> e k f", e=P))\
                        .then_inc(attr_in[b], 16)
                    sp.dma_start(gb[0:edges, b, G - 1, 0:R], av[bass.ds(first + (G - 1) * P, edges), :])\
                        .then_inc(attr_in[b], 16)

            attributes(0, 0, P)
            attributes(1, G * P, P)
            with sp.Fori(1, ITERS - 1) as i:
                for b in range(2):
                    sp.wait_ge(attr_used, i * 2 + (b - 1))
                    attributes(b, i * (BODY * P) + b * G * P, P)
            for b in range(2):
                sp.wait_ge(attr_used, (ITERS - 1) * 2 + b - 1)
                attributes(b, (ITERS - 1) * BODY * P + b * G * P, LASTE)

            store(tab_q, D, f"tq_cp{LASTQ}")
            store(tab_kv, D, f"tk_cp{LASTQ}", 0)
            store(tab_kv, D, f"tv_cp{LASTQ}", D)

            sp.wait_ge(node_step, AT[f"fin_cp{LASTQ}"])
            sp.dma_start(out[0:FULL * NB, :].rearrange("(b p) f -> p b f", p=NB), tabs[:, 0:FULL, :])\
                .then_inc(out_done, 16)
            sp.dma_start(out[FULL * NB:N, :], tabs[0:REST, FULL, :]).then_inc(out_done, 16)
            sp.wait_ge(out_done, 32)

        @block.gpsimd
        def _(pool):
            count = [0]

            def link(ins):
                count[0] += 1
                ins.then_inc(const_step, 1)
                pool.wait_ge(const_step, count[0])

            link(nc.gpsimd.memset(ident[:, :], 0.0))
            link(nc.gpsimd.affine_select(out=ident[:, :], in_=ident[:, :], compare_op=ALU.not_equal, fill=1.0,
                                         base=0, pattern=[[-1, P]], channel_multiplier=1))
            link(nc.gpsimd.memset(sel[:, :], 0.0))
            for m in range(3):
                link(nc.gpsimd.affine_select(out=sel[:, :], in_=sel[:, :], compare_op=ALU.not_equal, fill=1.0,
                                             base=-H0 * m, pattern=[[-1, H0]], channel_multiplier=1))
            link(nc.gpsimd.memset(headm[:, :], 1.0))
            link(nc.gpsimd.affine_select(out=headm[:, :], in_=headm[:, :], compare_op=ALU.is_ge, fill=0.0,
                                         base=0, pattern=[[-HD, NH]], channel_multiplier=1))
            link(nc.gpsimd.affine_select(out=headm[:, :], in_=headm[:, :], compare_op=ALU.is_ge, fill=0.0,
                                         base=HD - 1, pattern=[[HD, NH]], channel_multiplier=-1))
            nc.gpsimd.iota(iota_i, pattern=[[1, NP]], base=-HALF, channel_multiplier=0).then_inc(node_step, 1)

            def gather(q, tables):
                pool.sem_inc(q.taken, 2)
                with pool.Fori(0, ITERS) as i:
                    for b in range(2):
                        pool.wait_ge(q.taken, i * 2 + (b + 1))
                        pool.nop(nofuse=True)
                        for table, idx, staged, buf, width in tables:
                            nc.gpsimd.tensor_copy(staged[:, b, :], idx[:, bass.ds(i * BODY + b * G, G)])\
                                .then_inc(q.idx_staged, 1)
                        pool.wait_ge(q.idx_staged, (i * 2 + (b + 1)) * len(tables))
                        pool.nop(nofuse=True)
                        for k in range(G):
                            for table, idx, staged, buf, width in tables:
                                nc.gpsimd.indirect_dma_start(
                                    buf[:, b, k, 0:width], None, table[:, :],
                                    bass.IndirectOffsetOnAxis(ap=staged[:, b, k:k + 1].bitcast(U32), axis=0))\
                                    .then_inc(q.gathered[b], 16)

            by_src, by_dst = (src_idx, idx_a), (dst_idx, idx_b)
            pool.wait_ge(tab_done, 16)
            pool.wait_ge(node_step, AT["keys"])
            gather(pA, [(tab_a, *by_src, ga, 2 * H0), (tab_a, *by_dst, gb, 2 * H0)])
            begin(pool, "logit_all")
            nc.gpsimd.partition_all_reduce(colred[:, 1:2], colred[:, 0:1], P, RMAX).then_inc(node_step, 1)
            pool.wait_ge(tab_done, 32)
            gather(pC, [(tab_w, *by_src, ga, O0 + H0)])
            pool.wait_ge(tab_done, 48)
            gather(pD, [(tab_h, *by_src, ga, D)])
            pool.wait_ge(tab_done, 64)
            gather(pE, [(tab_2, *by_dst, ga, F2)])
            pool.wait_ge(tab_done, 16 * 7)
            gather(pF, [(tab_kv, *by_src, ga, 2 * D), (tab_q, *by_dst, gb, D)])
            begin(pool, "z_all")
            nc.gpsimd.partition_all_reduce(zall[:, :], zsum[:, :], P, RADD).then_inc(node_step, 1)

        @block.scalar
        def _(act):
            def stage(name, *args, **kw):
                begin(act, name)
                nc.scalar.activation(*args, **kw).then_inc(node_step, 1)

            def layernorm(n):
                stage(f"{n}_square", vb[:, :], va[:, :], ACT.Square)
                stage(f"{n}_std", nodes(vb[:, :]), acc[:, :, 0:CH], ACT.Sqrt, bias=eps_col[:, 0:1])

            def table(n, width, done):
                for r in range(LASTQ + 1):
                    begin(act, f"{n}_cp{r}")
                    if r == 0:
                        act.wait_ge(tab_done, 16 * done)
                    nc.scalar.activation(tabs[:, r * NCH:(r + 1) * NCH, 0:width], acc[0:NB, :, 0:width], ACT.Copy)\
                        .then_inc(node_step, 1)

            def split(q, i, b, source, widths):
                g1 = i * 2 + (b + 1)
                first, second = widths(b)[0:2]
                act.wait_ge(q.msg, g1)
                act.wait_ge(q.oh_used, i * BODY + (b * G + CREDIT - G))
                nc.scalar.activation(first, source(b), ACT.Copy).then_inc(q.part1, 1)
                act.wait_ge(q.rest1, g1)
                nc.scalar.activation(second, res_of(source(b)), ACT.Copy).then_inc(q.part2, 1)

            layernorm("ln0")
            stage("whT_cp", nodes(va[0:O0, :]), acc[0:O0, :, 0:CH], ACT.Identity, bias=col("L0_gnn_b"))
            table("ta", 2 * H0, 0)
            table("tw", O0, 1)
            stage("cnt_cp", nodes(cnt[:, :]), acc[:, :, 0:CH], ACT.Copy)
            stage("logit_exp", e4, e4, ACT.Exp, bias=colred[:, 2:3])
            stage("exp_b1", exp_parts[:, :, 0:H0], e4h, ACT.Copy)
            stage("exp_b2", exp_parts[:, :, H0:2 * H0], lkh, ACT.Copy)

            begin(act, "passB")
            with act.Fori(0, ITERS) as i:
                for b in range(2):
                    act.wait_ge(pB.oh_used, i * BODY + (b * G + CREDIT - G))
                    act.nop(nofuse=True)
                    nc.scalar.activation(exp_group(b), exp_parts[:, bass.ds(i * BODY + b * G, G), :], ACT.Copy)\
                        .then_inc(pB.part3, 1)
            stage("den_cp", nodes(va[0:3 * H0, :]), acc[0:3 * H0, :, 0:CH], ACT.Copy)

            begin(act, "passC")
            with act.Fori(0, ITERS) as i:
                for b in range(2):
                    split(pC, i, b, msg_wide, parts_wide)
            layernorm("ln1")
            table("th", D, 2)
            begin(act, "passD")
            with act.Fori(0, ITERS) as i:
                for b in range(2):
                    act.wait_ge(pD.gathered[b], pD.have_rows(i))
                    act.wait_ge(pD.oh_used, i * BODY + (b * G + CREDIT - G))
                    nc.scalar.activation(parts_wide(b)[0], ga[:, b, :, 0:D], ACT.Copy).then_inc(pD.part1, 1)
                    act.wait_ge(pD.rest1, i * 2 + (b + 1))
                    nc.scalar.activation(parts_wide(b)[1], res_of(msg_wide(b)), ACT.Copy).then_inc(pD.part2, 1)
            layernorm("ln2")
            table("t2", F2, 3)

            begin(act, "passE")
            with act.Fori(0, ITERS) as i:
                for b in range(2):
                    for s, (k0, k) in enumerate(SUBS):
                        n1 = i * (2 * NSUB) + (b * NSUB + s + 1)
                        act.wait_ge(flt_T, n1)
                        nc.scalar.activation(attrT[:, 0:k * P], small[0:R, 0:k * P], ACT.Copy).then_inc(flt_Tc, 1)
                        act.wait_ge(flt_h, n1)
                        nc.scalar.activation(hid_e[:, 0:k * P], small[0:F2, 0:k * P], ACT.Abs,
                                             bias=col("L2_gnn_b_f1")).then_inc(flt_abs, 1)
                        nc.scalar.activation(hid_r[:, 0:k * P], small[0:F2, 0:k * P], ACT.Relu,
                                             bias=col("L2_gnn_b_f1"))
                        act.wait_ge(flt_abs, n1)
                        nc.scalar.activation(hid_e[:, 0:k * P], hid_e[:, 0:k * P], ACT.Exp, scale=-1.0)\
                            .then_inc(flt_exp, 1)
                        act.wait_ge(flt_exp, n1)
                        nc.scalar.activation(hid_e[:, 0:k * P], hid_e[:, 0:k * P], ACT.Ln, bias=1.0)\
                            .then_inc(flt_ln, 1)
                    split(pE, i, b, msg_narrow, parts_narrow)
            stage("agg_cp", nodes(va[:, :]), acc[:, :, 0:CH], ACT.Copy)
            b_o1 = col("L2_gnn_b_o1")
            stage("o1_relu", nodes(va[:, :]), acc[:, :, 0:CH], ACT.Relu, bias=b_o1)
            stage("o1_abs", nodes(vb[:, :]), acc[:, :, 0:CH], ACT.Abs, bias=b_o1)
            stage("o1_exp", vb[:, :], vb[:, :], ACT.Exp, scale=-1.0)
            stage("o1_ln", vb[:, :], vb[:, :], ACT.Ln, bias=1.0)
            layernorm("ln3")
            table("tq", D, 4)
            table("tk", D, 5)
            table("tv", D, 6)

            begin(act, "passF")
            with act.Fori(0, ITERS) as i:
                for b in range(2):
                    g1 = i * 2 + (b + 1)
                    act.wait_ge(pF.score[3], g1)
                    nc.scalar.activation(ex[:, :, :], sc[:, :, :], ACT.Exp).then_inc(pF.weight, 1)
                    split(pF, i, b, msg_wide, parts_wide)
            layernorm("ln4")
            stage("w1_relu", nodes(va[:, :]), acc[:, :, 0:CH], ACT.Relu, bias=col("L3_gnn_b1"))
            layernorm("ln5")
            table("fin", D, 7)

        @block.vector
        def _(dve):
            def step(ins):
                ins.then_inc(node_step, 1)

            def split(q, i, b, source, widths, credit=0):
                g1 = i * 2 + (b + 1)
                first, second, third = widths(b)
                dve.wait_ge(q.part1, g1)
                nc.vector.tensor_tensor(res_of(source(b)), source(b), first, ALU.subtract).then_inc(q.rest1, 1)
                dve.wait_ge(q.part2, g1)
                nc.vector.tensor_tensor(third, res_of(source(b)), second, ALU.subtract).then_inc(q.part3, 1)

            def onehots(q, i, b, key):
                for k in range(G):
                    n = b * G + k
                    dve.wait_ge(q.oh_used, i * BODY + (n - 1 + CREDIT))
                    nc.vector.tensor_scalar(onehot[:, n % 2, :], iota_h[:, :], key[:, bass.ds(i * BODY + n, 1)], None,
                                            ALU.is_equal).then_inc(q.oh_ready, 1)

            def layernorm(n, x, relu):
                begin(dve, f"{n}_center")
                step(nc.vector.tensor_tensor(nodes(va[:, :]), nodes(x), acc[:, :, 0:CH], ALU.subtract))
                begin(dve, f"{n}_recip")
                step(nc.vector.reciprocal(vb[:, :], vb[:, :]))
                begin(dve, f"{n}_out")
                if relu:
                    step(nc.vector.scalar_tensor_tensor(out=hT[:, :], in0=va[:, :], scalar=0.0, in1=vb[:, :],
                                                        op0=ALU.max, op1=ALU.mult))
                else:
                    step(nc.vector.tensor_tensor(hT[:, :], va[:, :], vb[:, :], ALU.mult))

            nc.vector.memset(tabs[:, FULL, :], 0.0).then_inc(pads_set, 1)
            nc.vector.memset(stage_i[:, :, :], -1).then_inc(pads_set, 1)
            nc.vector.memset(avg[:, :], 1.0 / D)
            nc.vector.memset(ones_bf[:, :], 1.0)
            nc.vector.memset(ones_row[:, :], 1.0)
            nc.vector.memset(zero_bf[:, :], 0.0)
            nc.vector.memset(gb[:, :, :, :], 0.0)
            nc.vector.memset(eps_col[:, :], EPS).then_inc(const_v, 1)
            begin(dve, "iota_h")
            dve.wait_ge(const_v, 1)
            step(nc.vector.tensor_copy(iota_h[:, :], iota_i))
            begin(dve, "x_copy")
            step(nc.vector.tensor_copy(nodes(xT[:, :]), acc[:, :, 0:CH]))
            for name, array, pads, n_in in (("dst", dstf, 0.0, 1), ("src", srcf, 0.0, 2), ("w", ew[:, :], None, 3)):
                begin(dve, f"{name}_f")
                dve.wait_ge(idx_loaded, 48 * n_in)
                if name == "w":
                    step(nc.vector.memset(zacc[:, :, :], 0.0))
                else:
                    step(nc.vector.tensor_copy(stage_f[:, :, :], stage_i[:, :, :]))
                    if name == "dst":
                        dve.wait_ge(node_step, AT["dst_f"])
                        nc.vector.memset(stage_i[:, :, :], 0).then_inc(pads_set, 1)
                begin(dve, f"{name}_copy")
                step(nc.vector.tensor_copy(array.rearrange("p (b e) -> p b e", e=P), acc[:, 0:IB, 0:P]))
                if name == "src":
                    nc.vector.memset(stage_f[:, :, :], 0.0).then_inc(pads_set, 1)
            begin(dve, "keys")
            nc.vector.tensor_scalar(dst_key[:, :], dstf[:, 0:TILES], -float(HALF), None, ALU.add)
            nc.vector.tensor_scalar(src_key[:, :], srcf[:, 0:TILES], -float(HALF), None, ALU.add)
            nc.vector.tensor_scalar(dst_idx[:, :], dstf[:, 0:TILES], 0.0, None, ALU.max)
            nc.vector.tensor_copy(src_idx[:, :], srcf[:, 0:TILES])
            step(nc.vector.tensor_scalar(padneg[:, :], dstf[:, TILES - 1:TILES], 0.0, -BIG, ALU.is_lt, ALU.mult))
            begin(dve, "wT_copy")
            nc.vector.tensor_copy(attT[:, :], small[0:O0, 0:2 * H0])
            step(nc.vector.tensor_copy(w0T[:, :], small[:, 64:64 + O0]))
            layernorm("ln0", xT[:, :], True)

            begin(dve, "passA")
            with dve.Fori(0, ITERS) as i:
                for b in range(2):
                    dve.wait_ge(pA.gathered[b], pA.have_rows(i))
                    dve.nop(nofuse=True)
                    nc.vector.tensor_tensor(e4h_at(i * BODY + b * G), ga[:, b, :, 0:H0], gb[:, b, :, H0:2 * H0],
                                            ALU.add).then_inc(pA.taken, 1)
                    onehots(pA, i, b, dst_key)
            begin(dve, "logit_pad")
            step(nc.vector.tensor_scalar(e4[:, (TILES - 1) * H0:], e4[:, (TILES - 1) * H0:], padneg[:, 0:1], None, ALU.add))
            begin(dve, "logit_leaky")
            step(nc.vector.scalar_tensor_tensor(out=e4, in0=e4, scalar=0.2, in1=e4, op0=ALU.mult, op1=ALU.max))
            begin(dve, "logit_max")
            step(nc.vector.tensor_reduce(colred[:, 0:1], e4, AXX, ALU.max))
            begin(dve, "logit_neg")
            step(nc.vector.tensor_scalar(colred[:, 2:3], colred[:, 1:2], -1.0, None, ALU.mult))
            begin(dve, "exp_r1")
            step(nc.vector.tensor_tensor(lkh, e4h, exp_parts[:, :, 0:H0], ALU.subtract))
            begin(dve, "exp_b3")
            step(nc.vector.tensor_tensor(exp_parts[:, :, 2 * H0:3 * H0], lkh, exp_parts[:, :, H0:2 * H0], ALU.subtract))

            begin(dve, "passB")
            with dve.Fori(0, ITERS) as i:
                for b in range(2):
                    onehots(pB, i, b, src_key)
            begin(dve, "den_eps")
            step(nc.vector.tensor_scalar(tabs[:, :, O0:O0 + H0], small[0:NB, 0:NBLK * H0]
                                         .rearrange("p (b h) -> p b h", h=H0), 1e-16, None, ALU.add))
            begin(dve, "den_recip")
            step(nc.vector.reciprocal(tabs[:, :, O0:O0 + H0], tabs[:, :, O0:O0 + H0]))

            begin(dve, "passC")
            with dve.Fori(0, ITERS) as i:
                for b in range(2):
                    g1 = i * 2 + (b + 1)
                    dve.wait_ge(pC.gathered[b], pC.have_rows(i))
                    dve.nop(nofuse=True)
                    nc.vector.tensor_tensor(alpha[:, :].rearrange("p (k h) -> p k h", h=H0), e4h_at(i * BODY + b * G),
                                            ga[:, b, :, O0:O0 + H0], ALU.mult).then_inc(pC.weight, 1)
                    dve.wait_ge(pC.weight, g1)
                    dve.nop(nofuse=True)
                    nc.vector.tensor_tensor(
                        msg[:, :].rearrange("p (k h o) -> p k h o", h=H0, o=O0),
                        ga[:, b, :, 0:O0].unsqueeze(2).broadcast_to([P, G, H0, O0]),
                        alpha[:, :].rearrange("p (k h) -> p k h", h=H0).unsqueeze(3).broadcast_to([P, G, H0, O0]),
                        ALU.mult).then_inc(pC.msg, 1)
                    dve.wait_ge(pC.msg, g1)
                    dve.sem_inc(pC.taken, 1)
                    split(pC, i, b, msg_wide, parts_wide)
                    onehots(pC, i, b, dst_key)
            begin(dve, "x1")
            step(nc.vector.tensor_tensor(nodes(xT[:, :]), nodes(xT[:, :]), acc[:, :, 0:CH], ALU.add))
            layernorm("ln1", xT[:, :], True)

            begin(dve, "passD")
            with dve.Fori(0, ITERS) as i:
                for b in range(2):
                    g1 = i * 2 + (b + 1)
                    first, second, third = parts_wide(b)
                    dve.wait_ge(pD.part1, g1)
                    nc.vector.tensor_tensor(res_of(msg_wide(b)), ga[:, b, :, 0:D], first, ALU.subtract)\
                        .then_inc(pD.rest1, 1)
                    dve.wait_ge(pD.part2, g1)
                    dve.sem_inc(pD.taken, 1)
                    nc.vector.tensor_tensor(third, res_of(msg_wide(b)), second, ALU.subtract).then_inc(pD.part3, 1)
                    onehots(pD, i, b, dst_key)
            begin(dve, "mean_max")
            step(nc.vector.tensor_scalar(cnt[:, :], cnt[:, :], 1.0, None, ALU.max))
            begin(dve, "mean_recip")
            step(nc.vector.reciprocal(cnt[:, :], cnt[:, :]))
            begin(dve, "mean_mul")
            step(nc.vector.tensor_tensor(nodes(va[:, :]), nodes(cnt[:, :]), acc[:, :, 0:CH], ALU.mult))
            begin(dve, "x2")
            step(nc.vector.tensor_tensor(xT[:, :], xT[:, :], va[:, :], ALU.add))
            layernorm("ln2", xT[:, :], True)

            begin(dve, "passE")
            with dve.Fori(0, ITERS) as i:
                for b in range(2):
                    for s, (k0, kn) in enumerate(SUBS):
                        n1 = i * (2 * NSUB) + (b * NSUB + s + 1)
                        dve.wait_ge(flt_ln, n1)
                        nc.vector.scalar_tensor_tensor(out=hid[:, 0:kn * P], in0=hid_r[:, 0:kn * P], scalar=-LOG2,
                                                       in1=hid_e[:, 0:kn * P], op0=ALU.add, op1=ALU.add)\
                            .then_inc(flt_hid, 1)
                        if s == 0:
                            dve.wait_ge(pE.gathered[b], pE.have_rows(i))
                        dve.wait_ge(flt_W, n1)
                        dve.nop(nofuse=True)
                        for j in range(kn):
                            k = k0 + j
                            ins = nc.vector.scalar_tensor_tensor(
                                out=msg[:, k * F2:(k + 1) * F2], in0=small[:, j * F2:(j + 1) * F2],
                                scalar=ew[:, bass.ds(i * BODY + (b * G + k), 1)], in1=ga[:, b, k, 0:F2],
                                op0=ALU.mult, op1=ALU.mult)
                        ins.then_inc(flt_m, 1)
                    dve.wait_ge(flt_m, i * (2 * NSUB) + ((b + 1) * NSUB + 1))
                    dve.sem_inc(pE.msg, 1)
                    dve.sem_inc(pE.taken, 1)
                    split(pE, i, b, msg_narrow, parts_narrow)
                    onehots(pE, i, b, src_key)
            begin(dve, "o1_sum")
            step(nc.vector.scalar_tensor_tensor(out=va[:, :], in0=va[:, :], scalar=-LOG2, in1=vb[:, :],
                                                op0=ALU.add, op1=ALU.add))
            begin(dve, "x3")
            step(nc.vector.scalar_tensor_tensor(out=nodes(xT[:, :]), in0=acc[:, :, 0:CH], scalar=col("L2_gnn_b_o2"),
                                                in1=nodes(xT[:, :]), op0=ALU.add, op1=ALU.add))
            layernorm("ln3", xT[:, :], True)

            begin(dve, "passF")
            with dve.Fori(0, ITERS) as i:
                for b in range(2):
                    g1 = i * 2 + (b + 1)
                    dve.wait_ge(pF.gathered[b], pF.have_rows(i))
                    nc.vector.tensor_tensor(msg[:, :].rearrange("p (k f) -> p k f", f=D), gb[:, b, :, :],
                                            ga[:, b, :, 0:D], ALU.mult).then_inc(pF.score[0], 1)
                    dve.wait_ge(pF.score[0], g1)
                    nc.vector.tensor_reduce(sc[:, :, :].rearrange("p k h -> p (k h)"),
                                            msg[:, :].rearrange("p (k f) -> p k f", f=HD), AXX, ALU.add)\
                        .then_inc(pF.score[1], 1)
                    dve.wait_ge(pF.score[1], g1)
                    nc.vector.tensor_scalar(sc[:, :, :], sc[:, :, :], 1.0 / math.sqrt(HD), 5.0, ALU.mult, ALU.min)\
                        .then_inc(pF.score[2], 1)
                    dve.wait_ge(pF.score[2], g1)
                    nc.vector.tensor_scalar(sc[:, :, :], sc[:, :, :], -5.0, None, ALU.max).then_inc(pF.score[3], 1)
                    dve.wait_ge(pF.weight, g1)
                    nc.vector.tensor_tensor(
                        msg[:, :].rearrange("p (k h o) -> p k h o", h=NH, o=HD),
                        ga[:, b, :, D:2 * D].rearrange("p k (h o) -> p k h o", o=HD),
                        ex[:, :, :].unsqueeze(3).broadcast_to([P, G, NH, HD]), ALU.mult).then_inc(pF.msg, 1)
                    nc.vector.scalar_tensor_tensor(
                        out=exv[:, :, :],
                        in0=dst_key[:, bass.ds(i * BODY + b * G, G)].unsqueeze(2).broadcast_to([P, G, NH]),
                        scalar=-HALF - 0.5, in1=ex[:, :, :], op0=ALU.is_gt, op1=ALU.mult).then_inc(z_part, 1)
                    dve.wait_ge(z_part, g1)
                    nc.vector.tensor_tensor(zacc[:, :, :], zacc[:, :, :], exv[:, :, :], ALU.add).then_inc(z_ready, 1)
                    dve.wait_ge(pF.msg, g1)
                    dve.sem_inc(pF.taken, 1)
                    split(pF, i, b, msg_wide, parts_wide)
                    onehots(pF, i, b, dst_key)
            begin(dve, "z_sum")
            dve.wait_ge(z_ready, 2 * ITERS)
            step(nc.vector.tensor_reduce(zsum[:, :], zacc[:, :, :].rearrange("p k h -> p h k"), AXX, ALU.add))
            begin(dve, "z_recip")
            step(nc.vector.reciprocal(zrec[:, :], zall[:, :]))
            begin(dve, "z_head")
            step(nc.vector.tensor_tensor(zhm[:, :], headm[:, :], zrec[:, :], ALU.mult))
            begin(dve, "z_red")
            step(nc.vector.tensor_reduce(colred[:, 3:4], zhm[:, :], AXX, ALU.add))
            begin(dve, "att_cp")
            step(nc.vector.tensor_scalar(nodes(va[:, :]), acc[:, :, 0:CH], colred[:, 3:4], None, ALU.mult))
            begin(dve, "wo_add")
            step(nc.vector.scalar_tensor_tensor(out=nodes(hT[:, :]), in0=acc[:, :, 0:CH], scalar=col("L3_gnn_bO"),
                                                in1=nodes(hT[:, :]), op0=ALU.add, op1=ALU.add))
            layernorm("ln4", hT[:, :], False)
            begin(dve, "g1")
            step(nc.vector.tensor_scalar(hT[:, :], hT[:, :], col("L3_gnn_ln1_g"), col("L3_gnn_ln1_b"), ALU.mult, ALU.add))
            begin(dve, "w2_add")
            step(nc.vector.scalar_tensor_tensor(out=nodes(hT[:, :]), in0=acc[:, :, 0:CH], scalar=col("L3_gnn_b2"),
                                                in1=nodes(hT[:, :]), op0=ALU.add, op1=ALU.add))
            layernorm("ln5", hT[:, :], False)
            begin(dve, "g2")
            step(nc.vector.tensor_scalar(hT[:, :], hT[:, :], col("L3_gnn_ln2_g"), col("L3_gnn_ln2_b"), ALU.mult, ALU.add))
            begin(dve, "x4")
            step(nc.vector.tensor_tensor(xT[:, :], xT[:, :], hT[:, :], ALU.add))

        @block.tensor
        def _(pe):
            mm = nc.tensor.matmul

            def dense(name, w, x):
                begin(pe, name)
                for c in range(NCH):
                    ins = mm(acc[0:w.shape[1], c, 0:CH], w, x[:, c * CH:(c + 1) * CH], start=True, stop=True)
                ins.then_inc(node_step, 1)

            def layernorm(n, x):
                dense(f"{n}_mean", avg[:, :], x)
                dense(f"{n}_var", avg[:, :], vb[:, :])

            def table(n, x, w, bias=None):
                for r in range(LASTQ + 1):
                    begin(pe, f"{n}_mm{r}")
                    for j in range(NCH):
                        xb = x[:, (r * NCH + j) * NB:(r * NCH + j + 1) * NB]
                        if w is None:
                            ins = nc.tensor.transpose(acc[0:NB, j, 0:D], xb, ident[:, :])
                            continue
                        o = acc[0:NB, j, 0:w.shape[1]]
                        if bias is not None:
                            mm(o, ones_row[0:1, 0:NB], bias, start=True, stop=False)
                        ins = mm(o, xb, w, start=bias is None, stop=True)
                    ins.then_inc(node_step, 1)

            def scatter(q, name, stationaries, rows_out, wait_parts, before=None):
                begin(pe, name)
                pe.sem_inc(q.oh_used, CREDIT)
                for c in range(NCH):
                    mm(acc[0:rows_out, c, 0:CH], zero_bf[:, 0:rows_out], zero_bf[:, :], start=True, stop=False)
                with pe.Fori(0, ITERS) as i:
                    for b in range(2):
                        if before:
                            before(i, b)
                        if wait_parts:
                            pe.wait_ge(q.part3, i * 2 + (b + 1))
                        for k in range(G):
                            n = b * G + k
                            pe.wait_ge(q.oh_ready, i * BODY + (n + 1))
                            for st in stationaries(b, k):
                                for c in range(NCH):
                                    ins = mm(acc[0:st.shape[1], c, 0:CH], st, onehot[:, n % 2, c * CH:(c + 1) * CH],
                                             start=False, stop=False)
                            ins.then_inc(q.oh_used, 1)
                for c in range(NCH):
                    ins = mm(acc[0:rows_out, c, 0:CH], zero_bf[:, 0:rows_out], zero_bf[:, :], start=False, stop=True)
                ins.then_inc(node_step, 1)

            def wide(b, k):
                return [parts[:, b, s, k * D:(k + 1) * D] for s in range(3)]

            def narrow(b, k):
                return [parts[:, b, 0, k * D:(k + 1) * D], parts[:, b, 1, k * F2:(k + 1) * F2]]

            begin(pe, "x_T")
            pe.wait_ge(loaded, LOADED)
            for blk in range(NBLK):
                j = blk % BPC
                ins = nc.tensor.transpose(acc[:, blk // BPC, j * NB:(j + 1) * NB], tabs[:, blk, :], ident[0:NB, 0:NB])
            ins.then_inc(node_step, 1)
            for name in ("dst_T", "src_T", "w_T"):
                begin(pe, name)
                for j in range(IB):
                    ins = nc.tensor.transpose(acc[:, j, 0:P], stage_f[:, j, :], ident[:, :])
                ins.then_inc(node_step, 1)
            begin(pe, "wT_T")
            nc.tensor.transpose(small[0:O0, 0:2 * H0], att[:, :], ident[0:2 * H0, 0:2 * H0])
            nc.tensor.transpose(small[:, 64:64 + O0], w0[:, :], ident[0:O0, 0:O0]).then_inc(node_step, 1)

            layernorm("ln0", xT)
            dense("whT_mm", w0T[:, :], hT)
            table("ta", va[0:O0, :], attT[:, :])
            table("tw", hT, w0T[:, :], ROW["L0_gnn_b"])
            scatter(pA, "passA", lambda b, k: [ones_bf[:, :]], P, False)
            scatter(pB, "passB", lambda b, k: [exp_group(b)[:, k, :]], 3 * H0, True)
            begin(pe, "den_mm")
            for blk in range(NBLK):
                ins = mm(small[0:NB, blk * H0:(blk + 1) * H0], va[0:3 * H0, blk * NB:(blk + 1) * NB], sel[:, :],
                         start=True, stop=True)
            ins.then_inc(node_step, 1)
            scatter(pC, "passC", wide, P, True)
            layernorm("ln1", xT)
            table("th", hT, None)
            scatter(pD, "passD", wide, P, True)
            layernorm("ln2", xT)
            table("t2", hT, w_in[:, :], ROW["L2_gnn_b_in"])

            def filters(i, b):
                for s, (k0, kn) in enumerate(SUBS):
                    n1 = i * (2 * NSUB) + (b * NSUB + s + 1)
                    if s == 0:
                        pe.wait_ge(attr_in[b], (i + 1) * (16 * (b + 1)))
                    pe.wait_ge(flt_m, n1)
                    for j in range(kn):
                        ins = nc.tensor.transpose(small[0:R, j * P:(j + 1) * P], gb[:, b, k0 + j, 0:R], ident[:, :])
                    ins.then_inc(flt_T, 1)
                    pe.wait_ge(flt_Tc, n1)
                    if s == NSUB - 1:
                        pe.sem_inc(attr_used, 1)
                    mm(small[0:F2, 0:kn * P], w_f1[:, :], attrT[:, 0:kn * P], start=True, stop=True).then_inc(flt_h, 1)
                    pe.wait_ge(flt_hid, n1)
                    for j in range(kn):
                        o = small[:, j * F2:(j + 1) * F2]
                        mm(o, ones_row[0:1, :], ROW["L2_gnn_b_f2"], start=True, stop=False)
                        ins = mm(o, hid[:, j * P:(j + 1) * P], w_f2[:, :], start=False, stop=True)
                    ins.then_inc(flt_W, 1)

            begin(pe, "passE")
            pe.sem_inc(flt_m, 1)
            scatter(pE, "passE", narrow, P, True, filters)
            dense("o1_mm", w_o1[:, :], va)
            dense("o2_mm", w_o2[:, :], va)
            layernorm("ln3", xT)
            for n, name in ((0, "tq"), (1, "tk"), (2, "tv")):
                table(name, hT, wsq[:, n, :], ROW["L3_gnn_b" + "QKV"[n]])
            scatter(pF, "passF", wide, P, True)
            dense("wo_mm", wsq[:, 3, :], va)
            layernorm("ln4", hT)
            dense("w1_mm", wsq[:, 4, :], hT)
            dense("w2_mm", wsq[:, 5, :], va)
            layernorm("ln5", hT)
            table("fin", xT, None)


_INS = ['x', 'src', 'dst', 'edge_attr_32', 'edge_weight', 'L0_gnn_W', 'L0_gnn_b', 'L0_gnn_att_src', 'L0_gnn_att_dst',
 'L2_gnn_w_in', 'L2_gnn_b_in', 'L2_gnn_w_f1', 'L2_gnn_b_f1', 'L2_gnn_w_f2', 'L2_gnn_b_f2', 'L2_gnn_w_o1',
 'L2_gnn_b_o1', 'L2_gnn_w_o2', 'L2_gnn_b_o2', 'L3_gnn_WQ', 'L3_gnn_bQ', 'L3_gnn_WK', 'L3_gnn_bK', 'L3_gnn_WV',
 'L3_gnn_bV', 'L3_gnn_WO', 'L3_gnn_bO', 'L3_gnn_W1', 'L3_gnn_b1', 'L3_gnn_W2', 'L3_gnn_b2', 'L3_gnn_ln1_g',
 'L3_gnn_ln1_b', 'L3_gnn_ln2_g', 'L3_gnn_ln2_b']


def kernel(**inputs):
    import numpy as _np
    import concourse.bacc as _bacc
    from concourse import mybir as _mybir
    from concourse.bass_utils import run_bass_kernel_spmd as _run

    nc = _bacc.Bacc("TRN2", target_bir_lowering=False, num_devices=1)
    arrays, args = {}, {}
    for name in _INS:
        a = _np.ascontiguousarray(inputs[name])
        arrays[f"in_{name}_dram"] = a
        args[name] = nc.dram_tensor(f"in_{name}_dram", a.shape, _mybir.dt.from_np(a.dtype), kind="ExternalInput").ap()
    out = nc.dram_tensor("out_0_dram", (3125, 128), _mybir.dt.float32, kind="ExternalOutput").ap()
    build(nc, args, out)
    r = _run(nc, [arrays], core_ids=[0])
    return r.results[0]["out_0_dram"]
```

```python
from contextlib import ExitStack
import math

import concourse.bass as bass
from concourse import mybir

F32 = mybir.dt.float32
BF16 = mybir.dt.bfloat16
F16 = mybir.dt.float16
I16 = mybir.dt.int16
I32 = mybir.dt.int32
U32 = mybir.dt.uint32
ALU = mybir.AluOpType
ACT = mybir.ActivationFunctionType
RMAX = bass.bass_isa.ReduceOp.max
RADD = bass.bass_isa.ReduceOp.add
AXX = mybir.AxisListType.X
SP_ENGINE = mybir.EngineType.SP
PE_ENGINE = mybir.EngineType.PE

P = 128
N = 3125
D = 128
E = 103125
NCH = 7
CH = 448
NP = NCH * CH
HALF = NP // 2
NB = 112
NBLK = NP // NB
BPC = CH // NB
TILES = -(-E // P)
LASTE = E - (TILES - 1) * P
G = 13
BODY = 2 * G
ITERS = TILES // BODY
IB = -(-TILES // P)
H0 = 4
O0 = 32
R = 32
F2 = 64
NH = 8
HD = D // NH
SUB = 4
SUBS = [(k, min(SUB, G - k)) for k in range(0, G, SUB)]
NSUB = len(SUBS)
ROWM = F2 + 1
GE = G * P
EPS = 1e-5
LOG2 = float(math.log(2.0))
BIG = 1e30
WIN = 64
BPSUM = 512
FAR = 10000.0
CREDIT = BODY

assert TILES == ITERS * BODY

STEPS = [
    "iota", "iota_h", "x_T", "x_copy",
    "dst_f", "dst_T", "dst_copy", "win", "win_flag", "ka_T", "ka_copy", "kb_T", "kb_copy", "src_f", "src_T", "src_copy", "w_f", "w_T", "w_copy",
    "keys", "wT_T", "wT_copy",
]


def ln_steps(n):
    return [f"{n}_mean", f"{n}_center", f"{n}_square", f"{n}_var", f"{n}_std", f"{n}_recip", f"{n}_out"]


def table_steps(n):
    return [f"{n}_{s}{q}" for q in range(NBLK // NCH) for s in ("mm", "cp")]


STEPS += ln_steps("ln0") + ["whT_mm", "whT_cp"] + table_steps("ta") + table_steps("tw")
STEPS += ["passA", "cnt_cp", "logit_pad", "logit_leaky", "logit_max", "logit_all", "logit_neg", "logit_exp",
          "exp_b1", "exp_r1", "exp_b2", "exp_b3"]
STEPS += ["passB", "den_cp", "den_mm", "den_eps", "den_recip", "passC", "x1"]
STEPS += ln_steps("ln1") + table_steps("th") + ["passD", "mean_max", "mean_recip", "mean_mul", "x2"]
STEPS += ln_steps("ln2") + table_steps("t2") + ["before", "counts", "counts_mm", "places", "filters", "passE", "agg_cp", "o1_mm"]
STEPS += ["o1_relu", "o1_abs", "o1_exp", "o1_ln", "o1_sum", "o2_mm", "x3"]
STEPS += ln_steps("ln3") + table_steps("tq") + table_steps("tk") + table_steps("tv") + ["passF"]
STEPS += ["z_sum", "z_all", "z_recip", "z_head", "z_red", "att_cp", "wo_mm", "wo_add"]
STEPS += ln_steps("ln4") + ["g1", "w1_mm", "w1_relu", "w2_mm", "w2_add"] + ln_steps("ln5") + ["g2", "x4"]
STEPS += [f"fin_{s}{q}" for q in range(NBLK // NCH) for s in ("mm", "cp")]
AT = {name: n + 1 for n, name in enumerate(STEPS)}


def build(nc, t, out):
    ctx = ExitStack()
    with ctx:
        def sb(name, shape, dt):
            return ctx.enter_context(nc.sbuf_tensor(name, shape, dt))

        def sem(name):
            return ctx.enter_context(nc.semaphore(name))

        tab_a = nc.dram_tensor("tab_a", (NP, 2 * H0), F32).ap()
        tab_w = nc.dram_tensor("tab_w", (NP, O0 + H0), F32).ap()
        tab_h = nc.dram_tensor("tab_h", (NP, D), F32).ap()
        tab_2 = nc.dram_tensor("tab_2", (NP, F2), F32).ap()
        tab_q = nc.dram_tensor("tab_q", (NP, D), F32).ap()
        win_d = nc.dram_tensor("win_d", (IB * P, 2), I16).ap()
        tab_kv = nc.dram_tensor("tab_kv", (NP, 2 * D), F32).ap()
        tab_m = nc.dram_tensor("tab_m", (TILES * P, ROWM), F32).ap()

        acc = ctx.enter_context(nc.psum_tensor("acc", [P, NCH, 512], F32))
        small = ctx.enter_context(nc.psum_tensor("small", [P, 512], F32))

        def nodes(ap):
            return ap.rearrange("p (c n) -> p c n", c=NCH)

        xT = sb("xT", [P, NP], F32)
        hT = sb("hT", [P, NP], F32)
        va = sb("va", [P, NP], F32)
        vb = sb("vb", [P, NP], F32)
        cnt = sb("cnt", [P, NP], F32)
        tabs = sb("tabs", [NB, NBLK, D], F32)

        EC = IB * P
        ew = sb("ew", [P, EC], F32)
        dst_key = sb("dst_key", [P, TILES], F16)
        src_key = sb("src_key", [P, TILES], F16)
        dst_idx = sb("dst_idx", [P, TILES], I16)
        src_idx = sb("src_idx", [P, TILES], I16)
        padneg = sb("padneg", [P, 1], F32)
        ed = sb("ed", [P, TILES * H0], F32)
        e4 = ed[:, :]

        ga = sb("ga", [P, 2, G, 2 * D], F32)
        gb = sb("gb", [P, 2, G, D], F32)
        msg = sb("msg", [P, G * D], F32)
        res = sb("res", [P, G * D], F32)
        parts = sb("parts", [P, 2, 3, G * D], BF16)
        sc = sb("sc", [P, G, NH], F32)
        stage_i = parts[:, :, :, :].rearrange("p a s f -> p (a s f)")[:, 0:2 * EC].bitcast(I32)\
            .rearrange("p (b e) -> p b e", e=P)
        stage_f = cnt[:, 0:EC].rearrange("p (b e) -> p b e", e=P)
        dstf = msg[:, 0:EC]
        srcf = res[:, 0:EC]
        exp_parts = ga[:, :, :, :].rearrange("p a k f -> p (a k f)").bitcast(BF16)[:, 0:TILES * 3 * H0]\
            .rearrange("p (t s) -> p t s", s=3 * H0)
        lk = gb[:, :, :, :].rearrange("p a k f -> p (a k f)")[:, 0:TILES * H0]
        key_a = sb("key_a", [P, EC], BF16)
        key_b = sb("key_b", [P, EC], BF16)
        win_off = sb("win_off", [1, 2 * TILES], I16)
        covered = sb("covered", [1, 1], I32)
        iota_w = sb("iota_w", [P, WIN], BF16)
        wtmp = sb("wtmp", [P, 8, IB], F32)
        win_st = sb("win_st", [P, IB, 2], I16)
        idx_a = sb("idx_a", [P, 2, G], I32)
        idx_b = sb("idx_b", [P, 2, G], I32)
        onehot = sb("onehot", [P, 2, NP], BF16)
        alpha = sb("alpha", [P, G * H0], F32)
        ex = sb("ex", [P, G, NH], F32)
        exv = sb("exv", [P, G, NH], F32)
        zacc = sb("zacc", [P, G, NH], F32)
        attrT, hid, hid_r, hid_e = ([v[0:rows_, n * SUB * P:(n + 1) * SUB * P] for v in (va, vb)]
                                    for n, rows_ in enumerate((R, F2, F2, F2)))
        mrows = cnt[:, 0:2 * G * ROWM].rearrange("p (a k f) -> p a k f", a=2, f=ROWM)
        before = cnt[:, 2 * G * ROWM:2 * G * ROWM + P]
        place_i = ed[:, 0:TILES].bitcast(I32)
        place_f = ed[:, TILES:2 * TILES]
        halves = ed[:, 2 * TILES:4 * TILES].bitcast(F16)
        blk_of, rank, mask, sums = (halves[:, n * TILES:(n + 1) * TILES] for n in range(4))
        mask_off = ed[:, 3 * TILES:4 * TILES]
        blk_at = cnt[:, 2 * G * ROWM + P:]
        counts, offs, total, first_of = (blk_at[:, n * NBLK:(n + 1) * NBLK] for n in range(4))
        NG = 2 * ITERS
        glim, blk_a, blk_b, blk_ch, blk_off, base_sa, base_sb = (
            blk_at[:, 4 * NBLK + n * NG:4 * NBLK + (n + 1) * NG] for n in range(7))
        place_g = idx_b
        srows = ga[:, :, :, :].rearrange("p a k f -> p a (k f)")[:, :, 0:G * ROWM].rearrange("p a (k f) -> p a k f", f=ROWM)
        more = blk_at[:, 4 * NBLK + 7 * NG:]
        blk_offs = more[0:1, 0:NG].bitcast(I16)
        covered_s = sb("covered_s", [1, 1], I32)
        key_s = more[:, NG:NG + G].bitcast(F16).rearrange("p (w k) -> p w k", w=2)

        oh_flat = onehot[:, :, :].rearrange("p a n -> p (a n)")

        def onehot_wins(b):
            return oh_flat[:, b * G * 2 * WIN:(b + 1) * G * 2 * WIN].rearrange("p (k w n) -> p k w n", w=2, n=WIN)

        def onehot_win(b, w):
            return onehot_wins(b)[:, :, w, :]

        def onehot_blks(b, w):
            return oh_flat[:, (b * 2 + w) * G * NB:(b * 2 + w + 1) * G * NB].rearrange("p (k n) -> p k n", n=NB)

        ohT = va[:, 0:G * P]
        win_rows = gb
        WB = G // 2 + 1

        def small_bf():
            return small[:, :].bitcast(BF16)

        iota_i = vb[:, :].bitcast(I32)
        iota_h = sb("iota_h", [P, NP], F16)
        ident = sb("ident", [P, P], F32)
        avg = sb("avg", [P, P], F32)
        ones_bf = sb("ones_bf", [P, P], BF16)
        ident_bf = sb("ident_bf", [P, P], BF16)
        ones_row = sb("ones_row", [1, P], F32)
        zero_bf = sb("zero_bf", [P, CH], BF16)
        eps_col = sb("eps_col", [P, 1], F32)
        sel = sb("sel", [3 * H0, H0], F32)
        headm = sb("headm", [P, NH], F32)
        colred = sb("colred", [P, 4], F32)
        zsum = sb("zsum", [P, NH], F32)
        zall = sb("zall", [P, NH], F32)
        zrec = sb("zrec", [P, NH], F32)
        zhm = sb("zhm", [P, NH], F32)

        w0 = sb("w0", [O0, D], F32)
        w0T = sb("w0T", [D, O0], F32)
        att = sb("att", [2 * H0, O0], F32)
        attT = sb("attT", [O0, 2 * H0], F32)
        w_in = sb("w_in", [D, F2], F32)
        w_f1 = sb("w_f1", [R, F2], F32)
        w_f2 = sb("w_f2", [F2, F2], F32)
        w_o1 = sb("w_o1", [2 * F2, D], F32)
        w_o2 = sb("w_o2", [D, D], F32)
        wsq = sb("wsq", [D, 6, D], F32)
        SQ = ["WQ", "WK", "WV", "WO", "W1", "W2"]
        rows = sb("rows", [1, O0 + 2 * F2 + 3 * D], F32)
        ROW = {}
        at = 0
        for name, width in (("L0_gnn_b", O0), ("L2_gnn_b_in", F2), ("L2_gnn_b_f2", F2),
                            ("L3_gnn_bQ", D), ("L3_gnn_bK", D), ("L3_gnn_bV", D)):
            ROW[name] = rows[0:1, at:at + width]
            at += width
        COLS = ["L0_gnn_b", "L2_gnn_b_f1", "L2_gnn_b_o1", "L2_gnn_b_o2", "L3_gnn_bO", "L3_gnn_b1", "L3_gnn_b2",
                "L3_gnn_ln1_g", "L3_gnn_ln1_b", "L3_gnn_ln2_g", "L3_gnn_ln2_b"]
        cols = sb("cols", [P, len(COLS)], F32)

        def col(name):
            n = COLS.index(name)
            k = t[name].shape[0]
            return cols[0:k, n:n + 1]

        node_step = sem("node_step")
        loaded = sem("loaded")
        idx_loaded = sem("idx_loaded")
        pads_set = sem("pads_set")
        tab_done = sem("tab_done")
        out_done = sem("out_done")
        const_step = sem("const_step")
        const_v = sem("const_v")
        cov_ready = sem("cov_ready")
        win_step = sem("win_step")
        win_dma = sem("win_dma")
        z_part = sem("z_part")
        z_ready = sem("z_ready")
        attr_in = [sem("attr_in0"), sem("attr_in1")]
        attr_used = sem("attr_used")
        flt_T = sem("flt_T")
        flt_Tc = sem("flt_Tc")
        flt_h = sem("flt_h")
        flt_abs = sem("flt_abs")
        flt_exp = sem("flt_exp")
        flt_ln = sem("flt_ln")
        flt_hid = sem("flt_hid")
        flt_W = sem("flt_W")
        flt_m = sem("flt_m")
        place_step = sem("place_step")
        keys_made = sem("keys_made")
        rows_made = sem("rows_made")
        rows_sent = [sem("rows_sent0"), sem("rows_sent1")]
        SENT = 16 * G * ITERS

        def heads(ap):
            return ap.rearrange("p (t h) -> p t h", h=H0)

        e4h, lkh = heads(e4), heads(lk)

        def e4h_at(tile):
            return heads(ed[:, bass.ds(tile * H0, G * H0)])

        def exp_group(b):
            return parts[:, b, 0, 0:G * 3 * H0].rearrange("p (k h) -> p k h", k=G)

        def msg_wide(b):
            return msg[:, :].rearrange("p (k f) -> p k f", f=D)

        def msg_narrow(b):
            return srows[:, b, :, 0:F2]

        def res_of(m):
            f = m.shape[2]
            return res[:, 0:G * f].rearrange("p (k f) -> p k f", f=f)

        def parts_wide(b):
            return [parts[:, b, s, :].rearrange("p (k f) -> p k f", f=D) for s in range(3)]

        def parts_narrow(b):
            both = parts[:, b, 0, :].rearrange("p (k f) -> p k f", f=D)
            return [both[:, :, 0:F2], both[:, :, F2:D], parts[:, b, 1, 0:G * F2].rearrange("p (k f) -> p k f", f=F2)]

        class Pass:

            def __init__(self, q, gathers, parts=True, local=False, scores=0, scatters=True, loads=False):
                if scatters:
                    self.oh_ready = sem(f"oh_ready_{q}")
                    self.oh_used = sem(f"oh_used_{q}")
                    self.part3 = sem(f"part3_{q}")
                self.gathers = gathers
                if gathers or loads:
                    self.gathered = [sem(f"gathered0_{q}"), sem(f"gathered1_{q}")]
                    self.taken = sem(f"taken_{q}")
                if gathers:
                    self.idx_staged = sem(f"idx_staged_{q}")
                if parts:
                    self.msg = sem(f"msg_{q}")
                    self.part1 = sem(f"part1_{q}")
                    self.rest1 = sem(f"rest1_{q}")
                    self.part2 = sem(f"part2_{q}")
                if scores:
                    self.score = [sem(f"score{n}_{q}") for n in range(scores)]
                    self.weight = sem(f"weight_{q}")
                if local:
                    self.rows_in = [sem(f"rows_in0_{q}"), sem(f"rows_in1_{q}")]
                    self.rows_used = sem(f"rows_used_{q}")
                    self.turned = sem(f"turned_{q}")
                    self.turned_sb = sem(f"turned_sb_{q}")
                    self.local = sem(f"local_{q}")

            def have_rows(self, i):
                return (i + 1) * (16 * G * self.gathers)

        pA = Pass("A", 1, parts=False, local=True)
        pB = Pass("B", 0, parts=False)
        pC = Pass("C", 1, scores=1)
        pD = Pass("D", 1)
        pM = Pass("M", 1, parts=False, scatters=False)
        pE = Pass("E", 0, loads=True)
        pA_all = Pass("A_all", 2, parts=False)
        pF_all = Pass("F_all", 2, scores=4)

        block = ctx.enter_context(nc.Block())
        FULL = N // NB
        REST = N - FULL * NB
        LASTQ = NBLK // NCH - 1

        def begin(eng, name):
            if AT[name] > 1:
                eng.wait_ge(node_step, AT[name] - 1)

        def dram_tab(table):
            return table.rearrange("(b p) f -> p b f", p=NB)

        xv = t["x"]
        loads = [(tabs[:, 0:FULL, :], xv[0:FULL * NB, :].rearrange("(b p) f -> p b f", p=NB)),
                 (tabs[0:REST, FULL, :], xv[FULL * NB:N, :]),
                 (w0[:, :], t["L0_gnn_W"]), (att[0:H0, :], t["L0_gnn_att_src"]),
                 (att[H0:2 * H0, :], t["L0_gnn_att_dst"]), (w_in[:, :], t["L2_gnn_w_in"]),
                 (w_f1[:, :], t["L2_gnn_w_f1"]), (w_f2[:, :], t["L2_gnn_w_f2"]),
                 (w_o1[0:F2, :], t["L2_gnn_w_o1"]), (w_o1[F2:2 * F2, :], t["L2_gnn_w_o1"]),
                 (w_o2[:, :], t["L2_gnn_w_o2"])]
        loads += [(wsq[:, n, :], t["L3_gnn_" + name]) for n, name in enumerate(SQ)]
        loads += [(ap, t[name].rearrange("(o f) -> o f", o=1)) for name, ap in ROW.items()]
        loads += [(col(name), t[name].rearrange("(f o) -> f o", o=1)) for name in COLS]
        LOADED = 16 * len(loads)

        WIN_OFFS = 24

        @block.sync
        def _(sp):
            sp.wait_ge(pads_set, 2)
            for dst_ap, src_ap in loads:
                sp.dma_start(dst_ap, src_ap).then_inc(loaded, 16)

            whole = (IB - 1) * P
            last = TILES - 1 - whole
            for name, staged, after, pads in (("dst", stage_i, None, 2), ("src", stage_i, "dst_f", 3),
                                              ("edge_weight", stage_f, "src_copy", 4)):
                if after:
                    sp.wait_ge(node_step, AT[after])
                    sp.wait_ge(pads_set, pads)
                v = t[name]
                sp.dma_start(staged[:, 0:IB - 1, :], v[0:whole * P].rearrange("(b r e) -> r b e", r=P, e=P))\
                    .then_inc(idx_loaded, 16)
                sp.dma_start(staged[0:last, IB - 1, :], v[whole * P:(whole + last) * P].rearrange("(r e) -> r e", e=P))\
                    .then_inc(idx_loaded, 16)
                sp.dma_start(staged[last:last + 1, IB - 1, 0:LASTE],
                             v[(whole + last) * P:E].rearrange("(r e) -> r e", r=1)).then_inc(idx_loaded, 16)

            sp.wait_ge(win_step, WIN_OFFS)
            sp.dma_start(win_d.rearrange("(b r) w -> r b w", r=P), win_st[:, :, :]).then_inc(win_dma, 16)
            sp.wait_ge(win_dma, 16)
            sp.dma_start(win_off[:, :], win_d[0:TILES, :].rearrange("(o t) w -> o (t w)", o=1)).then_inc(win_dma, 16)

            def store(table, width, stage, c0=0):
                sp.wait_ge(node_step, AT[stage])
                sp.dma_start(dram_tab(table)[:, :, c0:c0 + width], tabs[:, :, 0:width]).then_inc(tab_done, 16)

            def window_rows(q, table, c0, width, into):
                with sp.Fori(0, ITERS) as i:
                    for b in range(2):
                        sp.wait_ge(q.rows_used, i * 2 + (b + 1))
                        _, offs = nc.values_load_multi_w_load_instructions(
                            win_off[0:1, bass.ds((i * BODY + b * G) * 2, 2 * G)], engines=[SP_ENGINE],
                            min_val=0, max_val=NCH * BPSUM - WIN,
                            skip_runtime_bounds_check_because="windows() keeps them in the tile's chunk")
                        for k in range(G):
                            for w in range(2):
                                off = offs[2 * k + w]
                                row = nc.s_assert_within(
                                    off - (off // BPSUM) * (BPSUM - CH), 0, NP - WIN,
                                    skip_runtime_bounds_check_because="windows() keeps them among the nodes")
                                sp.dma_start(win_rows[w * WIN:(w + 1) * WIN, b, k, into:into + width],
                                             table[bass.ds(row, WIN), c0:c0 + width]).then_inc(q.rows_in[b], 16)

            store(tab_a, 2 * H0, f"ta_cp{LASTQ}")
            sp.wait_ge(cov_ready, 1)
            sp.wait_ge(tab_done, 16)
            with sp.If(sp.value_load(covered[0:1, 0:1], min_val=0, max_val=1)):
                window_rows(pA, tab_a, H0, H0, 0)
            store(tab_w, O0 + H0, "den_recip")
            store(tab_h, D, f"th_cp{LASTQ}")
            store(tab_2, F2, f"t2_cp{LASTQ}")

            begin(sp, "filters")
            av = t["edge_attr_32"]

            def attributes(b, first, edges):
                if b == 0:
                    sp.dma_start(gb[:, b, :, 0:R], av[bass.ds(first, G * P), :].rearrange("(k e) f -> e k f", e=P))\
                        .then_inc(attr_in[b], 16)
                else:
                    sp.dma_start(gb[:, b, 0:G - 1, 0:R],
                                 av[bass.ds(first, (G - 1) * P), :].rearrange("(k e) f -> e k f", e=P))\
                        .then_inc(attr_in[b], 16)
                    sp.dma_start(gb[0:edges, b, G - 1, 0:R], av[bass.ds(first + (G - 1) * P, edges), :])\
                        .then_inc(attr_in[b], 16)

            attributes(0, 0, P)
            attributes(1, G * P, P)
            with sp.Fori(1, ITERS - 1) as i:
                for b in range(2):
                    sp.wait_ge(attr_used, i * 2 + (b - 1))
                    attributes(b, i * (BODY * P) + b * G * P, P)
            for b in range(2):
                sp.wait_ge(attr_used, (ITERS - 1) * 2 + b - 1)
                attributes(b, (ITERS - 1) * BODY * P + b * G * P, LASTE)

            begin(sp, "passE")
            for b in range(2):
                sp.wait_ge(rows_sent[b], SENT)
            with sp.Fori(0, ITERS) as i:
                for b in range(2):
                    sp.wait_ge(pE.taken, i * 2 + (b + 1))
                    sp.dma_start(srows[:, b, :, :].rearrange("p k f -> p (k f)"),
                                 tab_m[bass.ds(i * (BODY * P) + b * GE, GE), :].rearrange("(p k) f -> p (k f)", k=G))\
                        .then_inc(pE.gathered[b], 16)

            store(tab_q, D, f"tq_cp{LASTQ}")
            store(tab_kv, D, f"tk_cp{LASTQ}", 0)
            store(tab_kv, D, f"tv_cp{LASTQ}", D)

            sp.wait_ge(node_step, AT[f"fin_cp{LASTQ}"])
            sp.dma_start(out[0:FULL * NB, :].rearrange("(b p) f -> p b f", p=NB), tabs[:, 0:FULL, :])\
                .then_inc(out_done, 16)
            sp.dma_start(out[FULL * NB:N, :], tabs[0:REST, FULL, :]).then_inc(out_done, 16)
            sp.wait_ge(out_done, 32)

        @block.gpsimd
        def _(pool):
            count = [0]

            def link(ins):
                count[0] += 1
                ins.then_inc(const_step, 1)
                pool.wait_ge(const_step, count[0])

            link(nc.gpsimd.memset(ident[:, :], 0.0))
            link(nc.gpsimd.affine_select(out=ident[:, :], in_=ident[:, :], compare_op=ALU.not_equal, fill=1.0,
                                         base=0, pattern=[[-1, P]], channel_multiplier=1))
            link(nc.gpsimd.memset(sel[:, :], 0.0))
            for m in range(3):
                link(nc.gpsimd.affine_select(out=sel[:, :], in_=sel[:, :], compare_op=ALU.not_equal, fill=1.0,
                                             base=-H0 * m, pattern=[[-1, H0]], channel_multiplier=1))
            link(nc.gpsimd.memset(headm[:, :], 1.0))
            link(nc.gpsimd.affine_select(out=headm[:, :], in_=headm[:, :], compare_op=ALU.is_ge, fill=0.0,
                                         base=0, pattern=[[-HD, NH]], channel_multiplier=1))
            link(nc.gpsimd.affine_select(out=headm[:, :], in_=headm[:, :], compare_op=ALU.is_ge, fill=0.0,
                                         base=HD - 1, pattern=[[HD, NH]], channel_multiplier=-1))
            nc.gpsimd.iota(iota_i, pattern=[[1, NP]], base=-HALF, channel_multiplier=0).then_inc(node_step, 1)

            def gather(q, tables):
                pool.sem_inc(q.taken, 2)
                with pool.Fori(0, ITERS) as i:
                    for b in range(2):
                        pool.wait_ge(q.taken, i * 2 + (b + 1))
                        pool.nop(nofuse=True)
                        for table, idx, staged, buf, width in tables:
                            nc.gpsimd.tensor_copy(staged[:, b, :], idx[:, bass.ds(i * BODY + b * G, G)])\
                                .then_inc(q.idx_staged, 1)
                        pool.wait_ge(q.idx_staged, (i * 2 + (b + 1)) * len(tables))
                        pool.nop(nofuse=True)
                        for k in range(G):
                            for table, idx, staged, buf, width in tables:
                                nc.gpsimd.indirect_dma_start(
                                    buf[:, b, k, 0:width], None, table[:, :],
                                    bass.IndirectOffsetOnAxis(ap=staged[:, b, k:k + 1].bitcast(U32), axis=0))\
                                    .then_inc(q.gathered[b], 16)

            begin(pool, "win_flag")
            nc.gpsimd.partition_all_reduce(colred[:, 1:2], colred[:, 0:1], P, RMAX).then_inc(node_step, 1)

            by_src, by_dst = (src_idx, idx_a), (dst_idx, idx_b)
            pool.wait_ge(tab_done, 16)
            pool.wait_ge(node_step, AT["keys"])
            pool.wait_ge(cov_ready, 1)
            with pool.If(pool.value_load(covered[0:1, 0:1], min_val=0, max_val=1)):
                gather(pA, [(tab_a, *by_src, ga, 2 * H0)])
            with pool.Else():
                gather(pA_all, [(tab_a, *by_src, ga, 2 * H0), (tab_a, *by_dst, gb, 2 * H0)])
            begin(pool, "logit_all")
            nc.gpsimd.partition_all_reduce(colred[:, 1:2], colred[:, 0:1], P, RMAX).then_inc(node_step, 1)
            pool.wait_ge(tab_done, 32)
            gather(pC, [(tab_w, *by_src, ga, O0 + H0)])
            pool.wait_ge(tab_done, 48)
            gather(pD, [(tab_h, *by_src, ga, D)])
            pool.wait_ge(tab_done, 64)
            begin(pool, "before")
            link(nc.gpsimd.memset(before, 1.0))
            nc.gpsimd.affine_select(out=before, in_=before, compare_op=ALU.is_ge, fill=0.0, base=-1,
                                    pattern=[[1, P]], channel_multiplier=-1).then_inc(node_step, 1)

            def fetch(i, b, staged):
                pool.wait_ge(pM.taken, i * 2 + (b + 1))
                pool.nop(nofuse=True)
                nc.gpsimd.tensor_copy(idx_a[:, b, :], dst_idx[:, bass.ds(i * BODY + b * G, G)])\
                    .then_inc(pM.idx_staged, 1)
                pool.wait_ge(pM.idx_staged, staged)
                pool.nop(nofuse=True)
                for k in range(G):
                    nc.gpsimd.indirect_dma_start(
                        ga[:, b, k, 0:F2], None, tab_2[:, :],
                        bass.IndirectOffsetOnAxis(ap=idx_a[:, b, k:k + 1].bitcast(U32), axis=0))\
                        .then_inc(pM.gathered[b], 16)

            def send(i, b, staged):
                pool.wait_ge(rows_made, i * 2 + (b + 1))
                pool.nop(nofuse=True)
                nc.gpsimd.tensor_copy(place_g[:, b, :], place_i[:, bass.ds(i * BODY + b * G, G)])\
                    .then_inc(pM.idx_staged, 1)
                pool.wait_ge(pM.idx_staged, staged)
                pool.nop(nofuse=True)
                for k in range(G):
                    nc.gpsimd.indirect_dma_start(
                        tab_m[:, :], bass.IndirectOffsetOnAxis(ap=place_g[:, b, k:k + 1].bitcast(U32), axis=0),
                        mrows[:, b, k, :], None).then_inc(rows_sent[b], 16)

            begin(pool, "filters")
            pool.sem_inc(pM.taken, 2)
            fetch(0, 0, 1)
            with pool.Fori(0, ITERS - 1) as i:
                fetch(i, 1, i * 4 + 2)
                send(i, 0, i * 4 + 3)
                fetch(i + 1, 0, i * 4 + 4)
                send(i, 1, i * 4 + 5)
            fetch(ITERS - 1, 1, ITERS * 4 - 2)
            send(ITERS - 1, 0, ITERS * 4 - 1)
            send(ITERS - 1, 1, ITERS * 4)
            begin(pool, "passE")
            pool.sem_inc(pE.taken, 2)
            pool.wait_ge(tab_done, 16 * 7)
            gather(pF_all, [(tab_kv, *by_src, ga, 2 * D), (tab_q, *by_dst, gb, D)])
            begin(pool, "z_all")
            nc.gpsimd.partition_all_reduce(zall[:, :], zsum[:, :], P, RADD).then_inc(node_step, 1)

        @block.scalar
        def _(act):
            def stage(name, *args, **kw):
                begin(act, name)
                nc.scalar.activation(*args, **kw).then_inc(node_step, 1)

            def layernorm(n):
                stage(f"{n}_square", vb[:, :], va[:, :], ACT.Square)
                stage(f"{n}_std", nodes(vb[:, :]), acc[:, :, 0:CH], ACT.Sqrt, bias=eps_col[:, 0:1])

            def table(n, width, done):
                for r in range(LASTQ + 1):
                    begin(act, f"{n}_cp{r}")
                    if r == 0:
                        act.wait_ge(tab_done, 16 * done)
                    nc.scalar.activation(tabs[:, r * NCH:(r + 1) * NCH, 0:width], acc[0:NB, :, 0:width], ACT.Copy)\
                        .then_inc(node_step, 1)

            def turn_copy(q, i, b, s):
                k0, k1 = (0, WB) if s == 0 else (WB, G)
                act.wait_ge(q.turned, i * 4 + (b * 2 + s + 1))
                act.wait_ge(q.rows_used, i * 2 + (b + 2))
                nc.scalar.activation(ohT[:, k0 * P:k1 * P], small_bf()[:, 0:(k1 - k0) * P], ACT.Copy)\
                    .then_inc(q.turned_sb, 1)

            def split(q, i, b, source, widths):
                g1 = i * 2 + (b + 1)
                first, second = widths(b)[0:2]
                act.wait_ge(q.msg, g1)
                act.wait_ge(q.oh_used, i * BODY + (b * G + CREDIT - G))
                nc.scalar.activation(first, source(b), ACT.Copy).then_inc(q.part1, 1)
                act.wait_ge(q.rest1, g1)
                nc.scalar.activation(second, res_of(source(b)), ACT.Copy).then_inc(q.part2, 1)

            layernorm("ln0")
            stage("whT_cp", nodes(va[0:O0, :]), acc[0:O0, :, 0:CH], ACT.Identity, bias=col("L0_gnn_b"))
            table("ta", 2 * H0, 0)
            table("tw", O0, 1)
            begin(act, "passA")
            act.wait_ge(cov_ready, 1)
            with act.If(act.value_load(covered[0:1, 0:1], min_val=0, max_val=1)):
                with act.Fori(0, ITERS) as i:
                    for b in range(2):
                        for s in range(2):
                            turn_copy(pA, i, b, s)
            stage("cnt_cp", nodes(cnt[:, :]), acc[:, :, 0:CH], ACT.Copy)
            stage("logit_exp", e4, e4, ACT.Exp, bias=colred[:, 2:3])
            stage("exp_b1", exp_parts[:, :, 0:H0], e4h, ACT.Copy)
            stage("exp_b2", exp_parts[:, :, H0:2 * H0], lkh, ACT.Copy)

            begin(act, "passB")
            with act.Fori(0, ITERS) as i:
                for b in range(2):
                    act.wait_ge(pB.oh_used, i * BODY + (b * G + CREDIT - G))
                    act.nop(nofuse=True)
                    nc.scalar.activation(exp_group(b), exp_parts[:, bass.ds(i * BODY + b * G, G), :], ACT.Copy)\
                        .then_inc(pB.part3, 1)
            stage("den_cp", nodes(va[0:3 * H0, :]), acc[0:3 * H0, :, 0:CH], ACT.Copy)

            begin(act, "passC")
            with act.Fori(0, ITERS) as i:
                for b in range(2):
                    split(pC, i, b, msg_wide, parts_wide)
            layernorm("ln1")
            table("th", D, 2)
            begin(act, "passD")
            with act.Fori(0, ITERS) as i:
                for b in range(2):
                    act.wait_ge(pD.gathered[b], pD.have_rows(i))
                    act.wait_ge(pD.oh_used, i * BODY + (b * G + CREDIT - G))
                    nc.scalar.activation(parts_wide(b)[0], ga[:, b, :, 0:D], ACT.Copy).then_inc(pD.part1, 1)
                    act.wait_ge(pD.rest1, i * 2 + (b + 1))
                    nc.scalar.activation(parts_wide(b)[1], res_of(msg_wide(b)), ACT.Copy).then_inc(pD.part2, 1)
            layernorm("ln2")
            table("t2", F2, 3)

            begin(act, "filters")
            with act.Fori(0, ITERS) as i:
                for b in range(2):
                    def attr_copy(s):
                        n1 = i * (2 * NSUB) + (b * NSUB + s + 1)
                        k = SUBS[s][1]
                        act.wait_ge(flt_T, n1)
                        nc.scalar.activation(attrT[s % 2][:, 0:k * P], acc[0:R, s % 2, 0:k * P], ACT.Copy)\
                            .then_inc(flt_Tc, 1)

                    attr_copy(0)
                    for s, (k0, k) in enumerate(SUBS):
                        n1 = i * (2 * NSUB) + (b * NSUB + s + 1)
                        relu, e = hid_r[s % 2][:, 0:k * P], hid_e[s % 2][:, 0:k * P]
                        act.wait_ge(flt_h, n1)
                        hidden = acc[0:F2, 2 + s % 2, 0:k * P]
                        nc.scalar.activation(e, hidden, ACT.Abs, bias=col("L2_gnn_b_f1")).then_inc(flt_abs, 1)
                        nc.scalar.activation(relu, hidden, ACT.Relu, bias=col("L2_gnn_b_f1"))
                        if s + 1 < NSUB:
                            attr_copy(s + 1)
                        act.wait_ge(flt_abs, n1)
                        nc.scalar.activation(e, e, ACT.Exp, scale=-1.0).then_inc(flt_exp, 1)
                        act.wait_ge(flt_exp, n1)
                        nc.scalar.activation(e, e, ACT.Ln, bias=1.0).then_inc(flt_ln, 1)

            begin(act, "passE")
            with act.Fori(0, ITERS) as i:
                for b in range(2):
                    act.wait_ge(pE.gathered[b], (i + 1) * 16)
                    act.wait_ge(pE.oh_used, i * BODY + (b * G + CREDIT - G))
                    nc.scalar.activation(parts_narrow(b)[0], msg_narrow(b), ACT.Copy).then_inc(pE.part1, 1)
                    act.wait_ge(pE.rest1, i * 2 + (b + 1))
                    nc.scalar.activation(parts_narrow(b)[1], res_of(msg_narrow(b)), ACT.Copy).then_inc(pE.part2, 1)
            stage("agg_cp", nodes(va[:, :]), acc[:, :, 0:CH], ACT.Copy)
            b_o1 = col("L2_gnn_b_o1")
            stage("o1_relu", nodes(va[:, :]), acc[:, :, 0:CH], ACT.Relu, bias=b_o1)
            stage("o1_abs", nodes(vb[:, :]), acc[:, :, 0:CH], ACT.Abs, bias=b_o1)
            stage("o1_exp", vb[:, :], vb[:, :], ACT.Exp, scale=-1.0)
            stage("o1_ln", vb[:, :], vb[:, :], ACT.Ln, bias=1.0)
            layernorm("ln3")
            table("tq", D, 4)
            table("tk", D, 5)
            table("tv", D, 6)

            begin(act, "passF")
            with act.Fori(0, ITERS) as i:
                for b in range(2):
                    g1 = i * 2 + (b + 1)
                    act.wait_ge(pF_all.score[3], g1)
                    nc.scalar.activation(ex[:, :, :], sc[:, :, :], ACT.Exp).then_inc(pF_all.weight, 1)
                    split(pF_all, i, b, msg_wide, parts_wide)
            layernorm("ln4")
            stage("w1_relu", nodes(va[:, :]), acc[:, :, 0:CH], ACT.Relu, bias=col("L3_gnn_b1"))
            layernorm("ln5")
            table("fin", D, 7)

        @block.vector
        def _(dve):
            def step(ins):
                ins.then_inc(node_step, 1)

            def split(q, i, b, source, widths, credit=0):
                g1 = i * 2 + (b + 1)
                first, second, third = widths(b)
                dve.wait_ge(q.part1, g1)
                nc.vector.tensor_tensor(res_of(source(b)), source(b), first, ALU.subtract).then_inc(q.rest1, 1)
                dve.wait_ge(q.part2, g1)
                nc.vector.tensor_tensor(third, res_of(source(b)), second, ALU.subtract).then_inc(q.part3, 1)
                dve.wait_ge(q.part3, g1)

            def onehots(q, i, b, key):
                for k in range(G):
                    onehot_tile(q, i, b * G + k, key)

            def onehot_tile(q, i, n, key):
                dve.wait_ge(q.oh_used, i * BODY + (n - 1 + CREDIT))
                nc.vector.tensor_scalar(onehot[:, n % 2, :], iota_h[:, :], key[:, bass.ds(i * BODY + n, 1)], None,
                                        ALU.is_equal).then_inc(q.oh_ready, 1)

            def both_ways(run):
                dve.wait_ge(cov_ready, 1)
                with dve.If(dve.value_load(covered[0:1, 0:1], min_val=0, max_val=1)):
                    run(onehots_win)
                with dve.Else():
                    run(lambda q, i, b: onehots(q, i, b, dst_key))

            def onehots_win(q, i, b):
                dve.wait_ge(q.oh_used, i * BODY + (b * G + CREDIT - G))
                for w, key in enumerate((key_a, key_b)):
                    ins = nc.vector.tensor_tensor(
                        onehot_win(b, w), iota_w[:, :].unsqueeze(1).broadcast_to([P, G, WIN]),
                        key[:, bass.ds(i * BODY + b * G, G)].unsqueeze(2).broadcast_to([P, G, WIN]), ALU.is_equal)
                ins.then_inc(q.oh_ready, 1)

            def layernorm(n, x, relu):
                begin(dve, f"{n}_center")
                step(nc.vector.tensor_tensor(nodes(va[:, :]), nodes(x), acc[:, :, 0:CH], ALU.subtract))
                begin(dve, f"{n}_recip")
                step(nc.vector.reciprocal(vb[:, :], vb[:, :]))
                begin(dve, f"{n}_out")
                if relu:
                    step(nc.vector.scalar_tensor_tensor(out=hT[:, :], in0=va[:, :], scalar=0.0, in1=vb[:, :],
                                                        op0=ALU.max, op1=ALU.mult))
                else:
                    step(nc.vector.tensor_tensor(hT[:, :], va[:, :], vb[:, :], ALU.mult))

            def windows():
                n = [0]

                def link(ins):
                    n[0] += 1
                    ins.then_inc(win_step, 1)
                    dve.wait_ge(win_step, n[0])

                first, last, ca, cb, lim, base_a, base_b, off = (wtmp[:, j, :] for j in range(8))
                ka, kb = (v[:, 0:EC].rearrange("p (b e) -> p b e", e=P) for v in (va, vb))

                def each(x):
                    return x.unsqueeze(2).broadcast_to([P, IB, P])

                begin(dve, "win")
                link(nc.vector.tensor_scalar(ka, stage_f[:, :, :], 0.0, 2.0 * NP, ALU.is_lt, ALU.mult))
                link(nc.vector.tensor_tensor(ka, ka, stage_f[:, :, :], ALU.add))
                link(nc.vector.tensor_reduce(first, ka, AXX, ALU.min))
                link(nc.vector.tensor_reduce(last, stage_f[:, :, :], AXX, ALU.max))
                for node, chunk in ((first, ca), (last, cb)):
                    link(nc.vector.tensor_scalar(chunk, node, float(CH), None, ALU.is_ge))
                    for c in range(2, NCH):
                        link(nc.vector.scalar_tensor_tensor(out=chunk, in0=node, scalar=float(c * CH), in1=chunk,
                                                            op0=ALU.is_ge, op1=ALU.add))
                link(nc.vector.tensor_scalar(lim, ca, float(CH), float(CH - WIN), ALU.mult, ALU.add))
                link(nc.vector.tensor_tensor(base_a, first, lim, ALU.min))
                link(nc.vector.tensor_scalar(lim, cb, float(CH), None, ALU.mult))
                link(nc.vector.scalar_tensor_tensor(out=base_b, in0=last, scalar=1.0 - WIN, in1=lim,
                                                    op0=ALU.add, op1=ALU.max))
                for w, (chunk, base) in enumerate(((ca, base_a), (cb, base_b))):
                    link(nc.vector.scalar_tensor_tensor(out=off, in0=chunk, scalar=float(BPSUM - CH), in1=base,
                                                        op0=ALU.mult, op1=ALU.add))
                    link(nc.vector.tensor_copy(win_st[:, :, w], off))
                assert n[0] == WIN_OFFS
                link(nc.vector.tensor_tensor(ka, stage_f[:, :, :], each(base_a), ALU.subtract))
                link(nc.vector.tensor_scalar(kb, ka, float(WIN), FAR, ALU.is_lt, ALU.mult))
                link(nc.vector.tensor_tensor(kb, kb, stage_f[:, :, :], ALU.add))
                link(nc.vector.tensor_tensor(kb, kb, each(base_b), ALU.subtract))
                link(nc.vector.tensor_reduce(first, kb, AXX, ALU.min))
                link(nc.vector.tensor_reduce(colred[:, 0:1], first, AXX, ALU.min))
                step(nc.vector.tensor_scalar(colred[:, 0:1], colred[:, 0:1], -1.0, None, ALU.mult))
                for half, key in (("ka", key_a), ("kb", key_b)):
                    begin(dve, f"{half}_copy")
                    step(nc.vector.tensor_copy(key[:, :].rearrange("p (b e) -> p b e", e=P), acc[:, 0:IB, 0:P]))
                nc.vector.tensor_scalar(covered[:, :], colred[0:1, 1:2], 0.0, None, ALU.is_le).then_inc(cov_ready, 1)

            nc.vector.memset(tabs[:, FULL, :], 0.0).then_inc(pads_set, 1)
            nc.vector.memset(stage_i[:, :, :], -1).then_inc(pads_set, 1)
            nc.vector.memset(avg[:, :], 1.0 / D)
            nc.vector.memset(ones_bf[:, :], 1.0)
            nc.vector.memset(ones_row[:, :], 1.0)
            nc.vector.memset(zero_bf[:, :], 0.0)
            nc.vector.memset(gb[:, :, :, :], 0.0)
            nc.vector.memset(eps_col[:, :], EPS).then_inc(const_v, 1)
            begin(dve, "iota_h")
            dve.wait_ge(const_v, 1)
            nc.vector.tensor_scalar(iota_w[:, :], iota_i[:, 0:WIN], float(HALF), None, ALU.add)
            nc.vector.tensor_copy(ident_bf[:, :], ident[:, :])
            step(nc.vector.tensor_copy(iota_h[:, :], iota_i))
            begin(dve, "x_copy")
            step(nc.vector.tensor_copy(nodes(xT[:, :]), acc[:, :, 0:CH]))
            for name, array, pads, n_in in (("dst", dstf, 0.0, 1), ("src", srcf, 0.0, 2), ("w", ew[:, :], None, 3)):
                begin(dve, f"{name}_f")
                dve.wait_ge(idx_loaded, 48 * n_in)
                if name == "w":
                    step(nc.vector.memset(zacc[:, :, :], 0.0))
                else:
                    step(nc.vector.tensor_copy(stage_f[:, :, :], stage_i[:, :, :]))
                    if name == "dst":
                        dve.wait_ge(node_step, AT["dst_f"])
                        nc.vector.memset(stage_i[:, :, :], 0).then_inc(pads_set, 1)
                begin(dve, f"{name}_copy")
                step(nc.vector.tensor_copy(array.rearrange("p (b e) -> p b e", e=P), acc[:, 0:IB, 0:P]))
                if name == "src":
                    nc.vector.memset(stage_f[:, :, :], 0.0).then_inc(pads_set, 1)
                if name == "dst":
                    windows()
            begin(dve, "keys")
            nc.vector.tensor_scalar(dst_key[:, :], dstf[:, 0:TILES], -float(HALF), None, ALU.add)
            nc.vector.tensor_scalar(src_key[:, :], srcf[:, 0:TILES], -float(HALF), None, ALU.add)
            nc.vector.tensor_scalar(dst_idx[:, :], dstf[:, 0:TILES], 0.0, None, ALU.max)
            nc.vector.tensor_copy(src_idx[:, :], srcf[:, 0:TILES])
            step(nc.vector.tensor_scalar(padneg[:, :], dstf[:, TILES - 1:TILES], 0.0, -BIG, ALU.is_lt, ALU.mult))
            begin(dve, "wT_copy")
            nc.vector.tensor_copy(attT[:, :], small[0:O0, 0:2 * H0])
            step(nc.vector.tensor_copy(w0T[:, :], small[:, 64:64 + O0]))
            layernorm("ln0", xT[:, :], True)

            begin(dve, "passA")

            def edges_A():
                with dve.Fori(0, ITERS) as i:
                    for b in range(2):
                        onehots_win(pA, i, b)
                        dve.wait_ge(pA.gathered[b], pA.have_rows(i))
                        dve.wait_ge(pA.local, i * 2 + (b + 1))
                        dve.nop(nofuse=True)
                        nc.vector.tensor_tensor(e4h_at(i * BODY + b * G), ga[:, b, :, 0:H0], heads(small[:, 0:G * H0]),
                                                ALU.add).then_inc(pA.taken, 1)

            def edges_A_all():
                with dve.Fori(0, ITERS) as i:
                    for b in range(2):
                        dve.wait_ge(pA_all.gathered[b], pA_all.have_rows(i))
                        dve.nop(nofuse=True)
                        nc.vector.tensor_tensor(e4h_at(i * BODY + b * G), ga[:, b, :, 0:H0], gb[:, b, :, H0:2 * H0],
                                                ALU.add).then_inc(pA_all.taken, 1)
                        onehots(pA_all, i, b, dst_key)

            dve.wait_ge(cov_ready, 1)
            with dve.If(dve.value_load(covered[0:1, 0:1], min_val=0, max_val=1)):
                edges_A()
            with dve.Else():
                edges_A_all()
            begin(dve, "logit_pad")
            step(nc.vector.tensor_scalar(e4[:, (TILES - 1) * H0:], e4[:, (TILES - 1) * H0:], padneg[:, 0:1], None, ALU.add))
            begin(dve, "logit_leaky")
            step(nc.vector.scalar_tensor_tensor(out=e4, in0=e4, scalar=0.2, in1=e4, op0=ALU.mult, op1=ALU.max))
            begin(dve, "logit_max")
            step(nc.vector.tensor_reduce(colred[:, 0:1], e4, AXX, ALU.max))
            begin(dve, "logit_neg")
            step(nc.vector.tensor_scalar(colred[:, 2:3], colred[:, 1:2], -1.0, None, ALU.mult))
            begin(dve, "exp_r1")
            step(nc.vector.tensor_tensor(lkh, e4h, exp_parts[:, :, 0:H0], ALU.subtract))
            begin(dve, "exp_b3")
            step(nc.vector.tensor_tensor(exp_parts[:, :, 2 * H0:3 * H0], lkh, exp_parts[:, :, H0:2 * H0], ALU.subtract))

            begin(dve, "passB")
            with dve.Fori(0, ITERS) as i:
                for b in range(2):
                    onehots(pB, i, b, src_key)
            begin(dve, "den_eps")
            step(nc.vector.tensor_scalar(tabs[:, :, O0:O0 + H0], small[0:NB, 0:NBLK * H0]
                                         .rearrange("p (b h) -> p b h", h=H0), 1e-16, None, ALU.add))
            begin(dve, "den_recip")
            step(nc.vector.reciprocal(tabs[:, :, O0:O0 + H0], tabs[:, :, O0:O0 + H0]))

            begin(dve, "passC")

            def edges_C(targets):
                with dve.Fori(0, ITERS) as i:
                    for b in range(2):
                        g1 = i * 2 + (b + 1)
                        dve.wait_ge(pC.gathered[b], pC.have_rows(i))
                        dve.nop(nofuse=True)
                        nc.vector.tensor_tensor(alpha[:, :].rearrange("p (k h) -> p k h", h=H0), e4h_at(i * BODY + b * G),
                                                ga[:, b, :, O0:O0 + H0], ALU.mult).then_inc(pC.weight, 1)
                        dve.wait_ge(pC.weight, g1)
                        dve.nop(nofuse=True)
                        nc.vector.tensor_tensor(
                            msg[:, :].rearrange("p (k h o) -> p k h o", h=H0, o=O0),
                            ga[:, b, :, 0:O0].unsqueeze(2).broadcast_to([P, G, H0, O0]),
                            alpha[:, :].rearrange("p (k h) -> p k h", h=H0).unsqueeze(3).broadcast_to([P, G, H0, O0]),
                            ALU.mult).then_inc(pC.msg, 1)
                        dve.wait_ge(pC.msg, g1)
                        dve.sem_inc(pC.taken, 1)
                        split(pC, i, b, msg_wide, parts_wide)
                        targets(pC, i, b)

            both_ways(edges_C)
            begin(dve, "x1")
            step(nc.vector.tensor_tensor(nodes(xT[:, :]), nodes(xT[:, :]), acc[:, :, 0:CH], ALU.add))
            layernorm("ln1", xT[:, :], True)

            begin(dve, "passD")

            def edges_D(targets):
                with dve.Fori(0, ITERS) as i:
                    for b in range(2):
                        g1 = i * 2 + (b + 1)
                        first, second, third = parts_wide(b)
                        dve.wait_ge(pD.part1, g1)
                        nc.vector.tensor_tensor(res_of(msg_wide(b)), ga[:, b, :, 0:D], first, ALU.subtract)\
                            .then_inc(pD.rest1, 1)
                        dve.wait_ge(pD.part2, g1)
                        dve.sem_inc(pD.taken, 1)
                        nc.vector.tensor_tensor(third, res_of(msg_wide(b)), second, ALU.subtract).then_inc(pD.part3, 1)
                        dve.wait_ge(pD.part3, g1)
                        targets(pD, i, b)

            both_ways(edges_D)
            begin(dve, "mean_max")
            step(nc.vector.tensor_scalar(cnt[:, :], cnt[:, :], 1.0, None, ALU.max))
            begin(dve, "mean_recip")
            step(nc.vector.reciprocal(cnt[:, :], cnt[:, :]))
            begin(dve, "mean_mul")
            step(nc.vector.tensor_tensor(nodes(va[:, :]), nodes(cnt[:, :]), acc[:, :, 0:CH], ALU.mult))
            begin(dve, "x2")
            step(nc.vector.tensor_tensor(xT[:, :], xT[:, :], va[:, :], ALU.add))
            layernorm("ln2", xT[:, :], True)

            placed = [0]

            def link(ins):
                placed[0] += 1
                ins.then_inc(place_step, 1)
                dve.wait_ge(place_step, placed[0])

            link(nc.vector.tensor_scalar(blk_of, src_idx[:, :], float(NB), None, ALU.is_ge))
            for j in range(2, NBLK):
                link(nc.vector.scalar_tensor_tensor(out=blk_of, in0=src_idx[:, :], scalar=float(j * NB), in1=blk_of,
                                                    op0=ALU.is_ge, op1=ALU.add))
            nc.vector.memset(place_f, 1.0)
            link(nc.vector.memset(rank, 0.0))
            for j in range(NBLK):
                link(nc.vector.tensor_scalar(mask, blk_of, float(j), None, ALU.is_equal))
                link(nc.vector.tensor_tensor_scan(sums, place_f, mask, 0.0, ALU.mult, ALU.add))
                link(nc.vector.tensor_tensor(mask, mask, sums, ALU.mult))
                nc.vector.tensor_copy(counts[:, j:j + 1], sums[:, TILES - 1:TILES])
                link(nc.vector.tensor_tensor(rank, rank, mask, ALU.add))
            begin(dve, "counts")
            step(nc.vector.tensor_scalar(place_f, rank, -1.0, None, ALU.add))
            begin(dve, "places")
            link(nc.vector.tensor_scalar(total, small[:, P:P + NBLK], float(D), None, ALU.mult))
            link(nc.vector.memset(mask_off[:, 0:NBLK], 1.0))
            link(nc.vector.tensor_tensor_scan(first_of, mask_off[:, 0:NBLK], total, 0.0, ALU.mult, ALU.add))
            link(nc.vector.tensor_tensor(first_of, first_of, total, ALU.subtract))
            link(nc.vector.tensor_tensor(offs, first_of, small[:, 0:NBLK], ALU.add))
            for j in range(NBLK):
                link(nc.vector.tensor_scalar(mask_off, blk_of, float(j), offs[:, j:j + 1], ALU.is_equal, ALU.mult))
                link(nc.vector.tensor_tensor(place_f, place_f, mask_off, ALU.add))
            link(nc.vector.tensor_copy(place_i, place_f))
            link(nc.vector.tensor_reduce(colred[:, 0:1], total[:, 1:NBLK - 1], AXX, ALU.min))
            link(nc.vector.tensor_scalar(covered_s[:, :], colred[0:1, 0:1], GE - 1.5, None, ALU.is_ge))
            for blk, at_place in ((blk_a, 0), (blk_b, GE - 1)):
                link(nc.vector.tensor_scalar(glim, iota_h[:, 0:NG], float(HALF), float(GE), ALU.add, ALU.mult))
                if at_place:
                    link(nc.vector.tensor_scalar(glim, glim, float(at_place), None, ALU.add))
                link(nc.vector.tensor_scalar(blk, glim, first_of[:, 1:2], None, ALU.is_ge))
                for j in range(2, NBLK):
                    link(nc.vector.scalar_tensor_tensor(out=blk, in0=glim, scalar=first_of[:, j:j + 1], in1=blk,
                                                        op0=ALU.is_ge, op1=ALU.add))
            for w, blk in enumerate((blk_a, blk_b)):
                link(nc.vector.tensor_scalar(blk_ch, blk, float(BPC), None, ALU.is_ge))
                for c in range(2, NCH):
                    link(nc.vector.scalar_tensor_tensor(out=blk_ch, in0=blk, scalar=float(c * BPC), in1=blk_ch,
                                                        op0=ALU.is_ge, op1=ALU.add))
                link(nc.vector.tensor_scalar(blk_off, blk, float(NB), None, ALU.mult))
                link(nc.vector.scalar_tensor_tensor(out=blk_off, in0=blk_ch, scalar=float(BPSUM - CH), in1=blk_off,
                                                    op0=ALU.mult, op1=ALU.add))
                link(nc.vector.tensor_copy(blk_offs[:, :].rearrange("o (g w) -> o g w", w=2)[:, :, w], blk_off[0:1, :]))
            link(nc.vector.tensor_scalar(base_sa, blk_a, float(NB), None, ALU.mult))
            link(nc.vector.tensor_tensor(base_sb, blk_a, blk_b, ALU.is_equal))
            link(nc.vector.tensor_scalar(base_sb, base_sb, 4.0 * NBLK, None, ALU.mult))
            link(nc.vector.tensor_tensor(base_sb, base_sb, blk_b, ALU.add))
            step(nc.vector.tensor_scalar(base_sb, base_sb, float(NB), None, ALU.mult))

            begin(dve, "filters")

            def messages(i, first):
                for b in range(2):
                    if not first:
                        dve.wait_ge(rows_sent[b], i * (16 * G))
                        dve.nop(nofuse=True)
                    nc.vector.tensor_copy(mrows[:, b, :, F2], src_key[:, bass.ds(i * BODY + b * G, G)])
                    for s, (k0, kn) in enumerate(SUBS):
                        n1 = i * (2 * NSUB) + (b * NSUB + s + 1)
                        dve.wait_ge(flt_ln, n1)
                        nc.vector.scalar_tensor_tensor(
                            out=hid[s % 2][:, 0:kn * P], in0=hid_r[s % 2][:, 0:kn * P], scalar=-LOG2,
                            in1=hid_e[s % 2][:, 0:kn * P], op0=ALU.add, op1=ALU.add).then_inc(flt_hid, 1)
                        if s == 0:
                            dve.wait_ge(pM.gathered[b], pM.have_rows(i))
                        dve.wait_ge(flt_W, n1)
                        dve.nop(nofuse=True)
                        for j in range(kn):
                            k = k0 + j
                            ins = nc.vector.scalar_tensor_tensor(
                                out=mrows[:, b, k, 0:F2], in0=acc[:, 4 + s % 2, j * F2:(j + 1) * F2],
                                scalar=ew[:, bass.ds(i * BODY + (b * G + k), 1)], in1=ga[:, b, k, 0:F2],
                                op0=ALU.mult, op1=ALU.mult)
                        ins.then_inc(flt_m, 1)
                    dve.wait_ge(flt_m, i * (2 * NSUB) + (b + 1) * NSUB)
                    dve.sem_inc(rows_made, 1)
                    dve.sem_inc(pM.taken, 1)

            messages(0, True)
            with dve.Fori(1, ITERS) as i:
                messages(i, False)
            dve.wait_ge(rows_made, 2 * ITERS)
            dve.sem_inc(node_step, 1)

            begin(dve, "passE")

            def parts_E(i, b):
                g1 = i * 2 + (b + 1)
                first, second, third = parts_narrow(b)
                dve.wait_ge(pE.part1, g1)
                nc.vector.tensor_tensor(res_of(msg_narrow(b)), msg_narrow(b), first, ALU.subtract)\
                    .then_inc(pE.rest1, 1)
                dve.wait_ge(pE.part2, g1)
                nc.vector.tensor_tensor(third, res_of(msg_narrow(b)), second, ALU.subtract).then_inc(pE.part3, 1)
                dve.wait_ge(pE.part3, g1)

            def edges_E():
                with dve.Fori(0, ITERS) as i:
                    for b in range(2):
                        dve.wait_ge(pE.gathered[b], (i + 1) * 16)
                        for w, base in enumerate((base_sa, base_sb)):
                            ins = nc.vector.tensor_scalar(key_s[:, w, :], srows[:, b, :, F2],
                                                          base[:, bass.ds(i * 2 + b, 1)], None, ALU.subtract)
                        ins.then_inc(keys_made, 1)
                        dve.wait_ge(keys_made, i * 2 + (b + 1))
                        dve.wait_ge(pE.oh_used, i * BODY + (b * G + CREDIT - G))
                        for w in range(2):
                            ins = nc.vector.tensor_tensor(
                                onehot_blks(b, w), iota_h[:, 0:NB].unsqueeze(1).broadcast_to([P, G, NB]),
                                key_s[:, w, :].unsqueeze(2).broadcast_to([P, G, NB]), ALU.is_equal)
                        ins.then_inc(pE.oh_ready, 1)
                        parts_E(i, b)
                        dve.sem_inc(pE.taken, 1)

            def edges_E_all():
                with dve.Fori(0, ITERS) as i:
                    for b in range(2):
                        dve.wait_ge(pE.gathered[b], (i + 1) * 16)
                        parts_E(i, b)
                        for k in range(G):
                            n = b * G + k
                            dve.wait_ge(pE.oh_used, i * BODY + (n - 1 + CREDIT))
                            ins = nc.vector.tensor_scalar(onehot[:, n % 2, :], iota_h[:, :], srows[:, b, k, F2:F2 + 1],
                                                          None, ALU.is_equal).then_inc(pE.oh_ready, 1)
                        dve.wait_ge(pE.oh_ready, i * BODY + (b + 1) * G)
                        dve.sem_inc(pE.taken, 1)

            with dve.If(dve.value_load(covered_s[0:1, 0:1], min_val=0, max_val=1)):
                edges_E()
            with dve.Else():
                edges_E_all()
            begin(dve, "o1_sum")
            step(nc.vector.scalar_tensor_tensor(out=va[:, :], in0=va[:, :], scalar=-LOG2, in1=vb[:, :],
                                                op0=ALU.add, op1=ALU.add))
            begin(dve, "x3")
            step(nc.vector.scalar_tensor_tensor(out=nodes(xT[:, :]), in0=acc[:, :, 0:CH], scalar=col("L2_gnn_b_o2"),
                                                in1=nodes(xT[:, :]), op0=ALU.add, op1=ALU.add))
            layernorm("ln3", xT[:, :], True)

            begin(dve, "passF")

            def edges_F(targets):
                with dve.Fori(0, ITERS) as i:
                    for b in range(2):
                        g1 = i * 2 + (b + 1)
                        dve.wait_ge(pF_all.gathered[b], pF_all.have_rows(i))
                        nc.vector.tensor_tensor(msg[:, :].rearrange("p (k f) -> p k f", f=D), gb[:, b, :, :],
                                                ga[:, b, :, 0:D], ALU.mult).then_inc(pF_all.score[0], 1)
                        dve.wait_ge(pF_all.score[0], g1)
                        nc.vector.tensor_reduce(sc[:, :, :].rearrange("p k h -> p (k h)"),
                                                msg[:, :].rearrange("p (k f) -> p k f", f=HD), AXX, ALU.add)\
                            .then_inc(pF_all.score[1], 1)
                        dve.wait_ge(pF_all.score[1], g1)
                        nc.vector.tensor_scalar(sc[:, :, :], sc[:, :, :], 1.0 / math.sqrt(HD), 5.0, ALU.mult, ALU.min)\
                            .then_inc(pF_all.score[2], 1)
                        dve.wait_ge(pF_all.score[2], g1)
                        nc.vector.tensor_scalar(sc[:, :, :], sc[:, :, :], -5.0, None, ALU.max).then_inc(pF_all.score[3], 1)
                        dve.wait_ge(pF_all.weight, g1)
                        nc.vector.tensor_tensor(
                            msg[:, :].rearrange("p (k h o) -> p k h o", h=NH, o=HD),
                            ga[:, b, :, D:2 * D].rearrange("p k (h o) -> p k h o", o=HD),
                            ex[:, :, :].unsqueeze(3).broadcast_to([P, G, NH, HD]), ALU.mult).then_inc(pF_all.msg, 1)
                        nc.vector.scalar_tensor_tensor(
                            out=exv[:, :, :],
                            in0=dst_key[:, bass.ds(i * BODY + b * G, G)].unsqueeze(2).broadcast_to([P, G, NH]),
                            scalar=-HALF - 0.5, in1=ex[:, :, :], op0=ALU.is_gt, op1=ALU.mult).then_inc(z_part, 1)
                        dve.wait_ge(z_part, g1)
                        nc.vector.tensor_tensor(zacc[:, :, :], zacc[:, :, :], exv[:, :, :], ALU.add).then_inc(z_ready, 1)
                        dve.wait_ge(pF_all.msg, g1)
                        dve.sem_inc(pF_all.taken, 1)
                        split(pF_all, i, b, msg_wide, parts_wide)
                        targets(pF_all, i, b)

            both_ways(edges_F)
            begin(dve, "z_sum")
            dve.wait_ge(z_ready, 2 * ITERS)
            step(nc.vector.tensor_reduce(zsum[:, :], zacc[:, :, :].rearrange("p k h -> p h k"), AXX, ALU.add))
            begin(dve, "z_recip")
            step(nc.vector.reciprocal(zrec[:, :], zall[:, :]))
            begin(dve, "z_head")
            step(nc.vector.tensor_tensor(zhm[:, :], headm[:, :], zrec[:, :], ALU.mult))
            begin(dve, "z_red")
            step(nc.vector.tensor_reduce(colred[:, 3:4], zhm[:, :], AXX, ALU.add))
            begin(dve, "att_cp")
            step(nc.vector.tensor_scalar(nodes(va[:, :]), acc[:, :, 0:CH], colred[:, 3:4], None, ALU.mult))
            begin(dve, "wo_add")
            step(nc.vector.scalar_tensor_tensor(out=nodes(hT[:, :]), in0=acc[:, :, 0:CH], scalar=col("L3_gnn_bO"),
                                                in1=nodes(hT[:, :]), op0=ALU.add, op1=ALU.add))
            layernorm("ln4", hT[:, :], False)
            begin(dve, "g1")
            step(nc.vector.tensor_scalar(hT[:, :], hT[:, :], col("L3_gnn_ln1_g"), col("L3_gnn_ln1_b"), ALU.mult, ALU.add))
            begin(dve, "w2_add")
            step(nc.vector.scalar_tensor_tensor(out=nodes(hT[:, :]), in0=acc[:, :, 0:CH], scalar=col("L3_gnn_b2"),
                                                in1=nodes(hT[:, :]), op0=ALU.add, op1=ALU.add))
            layernorm("ln5", hT[:, :], False)
            begin(dve, "g2")
            step(nc.vector.tensor_scalar(hT[:, :], hT[:, :], col("L3_gnn_ln2_g"), col("L3_gnn_ln2_b"), ALU.mult, ALU.add))
            begin(dve, "x4")
            step(nc.vector.tensor_tensor(xT[:, :], xT[:, :], hT[:, :], ALU.add))

        @block.tensor
        def _(pe):
            mm = nc.tensor.matmul
            acc_row = acc[:, :, :].rearrange("p c n -> p (c n)")

            def dense(name, w, x):
                begin(pe, name)
                for c in range(NCH):
                    ins = mm(acc[0:w.shape[1], c, 0:CH], w, x[:, c * CH:(c + 1) * CH], start=True, stop=True)
                ins.then_inc(node_step, 1)

            def layernorm(n, x):
                dense(f"{n}_mean", avg[:, :], x)
                dense(f"{n}_var", avg[:, :], vb[:, :])

            def table(n, x, w, bias=None):
                for r in range(LASTQ + 1):
                    begin(pe, f"{n}_mm{r}")
                    for j in range(NCH):
                        xb = x[:, (r * NCH + j) * NB:(r * NCH + j + 1) * NB]
                        if w is None:
                            ins = nc.tensor.transpose(acc[0:NB, j, 0:D], xb, ident[:, :])
                            continue
                        o = acc[0:NB, j, 0:w.shape[1]]
                        if bias is not None:
                            mm(o, ones_row[0:1, 0:NB], bias, start=True, stop=False)
                        ins = mm(o, xb, w, start=bias is None, stop=True)
                    ins.then_inc(node_step, 1)

            def open_acc(rows_out):
                for c in range(NCH):
                    mm(acc[0:rows_out, c, 0:CH], zero_bf[:, 0:rows_out], zero_bf[:, :], start=True, stop=False)

            def close_acc(rows_out):
                for c in range(NCH):
                    ins = mm(acc[0:rows_out, c, 0:CH], zero_bf[:, 0:rows_out], zero_bf[:, :], start=False, stop=True)
                ins.then_inc(node_step, 1)

            def scatter_tile(q, stationaries, i, b, k):
                n = b * G + k
                pe.wait_ge(q.oh_ready, i * BODY + (n + 1))
                for st in stationaries(b, k):
                    for c in range(NCH):
                        ins = mm(acc[0:st.shape[1], c, 0:CH], st, onehot[:, n % 2, c * CH:(c + 1) * CH],
                                 start=False, stop=False)
                ins.then_inc(q.oh_used, 1)

            def all_nodes(q, stationaries):
                with pe.Fori(0, ITERS) as i:
                    for b in range(2):
                        if stationaries is not counting:
                            pe.wait_ge(q.part3, i * 2 + (b + 1))
                        for k in range(G):
                            scatter_tile(q, stationaries, i, b, k)

            def window_offsets(i, b):
                _, offs = nc.values_load_multi_w_load_instructions(
                    win_off[0:1, bass.ds((i * BODY + b * G) * 2, 2 * G)], engines=[PE_ENGINE],
                    min_val=0, max_val=NCH * BPSUM - WIN,
                    skip_runtime_bounds_check_because="windows() keeps them in the tile's chunk")
                return offs

            def scatter_windows(q, stationaries, i, b, offs):
                for k in range(G):
                    for st in stationaries(b, k):
                        for w in range(2):
                            ins = mm(acc_row[0:st.shape[1], bass.ds(offs[2 * k + w], WIN)], st,
                                     onehot_win(b, w)[:, k, :], start=False, stop=False)
                ins.then_inc(q.oh_used, G)

            def in_windows(q, stationaries):
                with pe.Fori(0, ITERS) as i:
                    for b in range(2):
                        offs = window_offsets(i, b)
                        pe.wait_ge(q.part3, i * 2 + (b + 1))
                        pe.wait_ge(q.oh_ready, i * 2 + (b + 1))
                        scatter_windows(q, stationaries, i, b, offs)

            def turn(q, i, b):
                for s, (k0, k1) in enumerate(((0, WB), (WB, G))):
                    if s == 1:
                        pe.wait_ge(q.turned_sb, i * 4 + (b * 2 + 1))
                    for k in range(k0, k1):
                        ins = nc.tensor.transpose(small_bf()[:, (k - k0) * P:(k - k0 + 1) * P],
                                                  onehot_wins(b)[:, k, :, :].rearrange("p w n -> p (w n)"), ident_bf[:, :])
                    ins.then_inc(q.turned, 1)

            def counting(b, k):
                return [ones_bf[:, :]]

            def windows_A():
                pe.sem_inc(pA.rows_used, 2)
                with pe.Fori(0, ITERS) as i:
                    for b in range(2):
                        offs = window_offsets(i, b)
                        pe.wait_ge(pA.oh_ready, i * 2 + (b + 1))
                        pe.wait_ge(pA.taken, i * 2 + (b + 2))
                        turn(pA, i, b)
                        pe.wait_ge(pA.turned_sb, i * 4 + (b * 2 + 2))
                        pe.wait_ge(pA.rows_in[b], (i + 1) * (16 * 2 * G))
                        for k in range(G):
                            ins = mm(small[:, k * H0:(k + 1) * H0], ohT[:, k * P:(k + 1) * P],
                                     win_rows[:, b, k, 0:H0], start=True, stop=True)
                        ins.then_inc(pA.local, 1)
                        pe.wait_ge(pA.local, i * 2 + (b + 1))
                        pe.sem_inc(pA.rows_used, 1)
                        scatter_windows(pA, counting, i, b, offs)
                pe.wait_ge(pA.taken, ITERS * 2 + 2)

            def scatter(name, stationaries, rows_out, q, q_all, windows):
                begin(pe, name)
                open_acc(rows_out)
                if windows:
                    pe.wait_ge(cov_ready, 1)
                    pe.wait_ge(win_dma, 32)
                    with pe.If(pe.value_load(covered[0:1, 0:1], min_val=0, max_val=1)):
                        pe.sem_inc(q.oh_used, CREDIT)
                        windows()
                    with pe.Else():
                        pe.sem_inc(q_all.oh_used, CREDIT)
                        all_nodes(q_all, stationaries)
                else:
                    pe.sem_inc(q_all.oh_used, CREDIT)
                    all_nodes(q_all, stationaries)
                close_acc(rows_out)

            def wide(b, k):
                return [parts[:, b, s, k * D:(k + 1) * D] for s in range(3)]

            def narrow(b, k):
                return [parts[:, b, 0, k * D:(k + 1) * D], parts[:, b, 1, k * F2:(k + 1) * F2]]

            begin(pe, "x_T")
            pe.wait_ge(loaded, LOADED)
            for blk in range(NBLK):
                j = blk % BPC
                ins = nc.tensor.transpose(acc[:, blk // BPC, j * NB:(j + 1) * NB], tabs[:, blk, :], ident[0:NB, 0:NB])
            ins.then_inc(node_step, 1)
            for name, staged in (("dst_T", stage_f), ("ka_T", va), ("kb_T", vb), ("src_T", stage_f), ("w_T", stage_f)):
                begin(pe, name)
                if staged is not stage_f:
                    staged = staged[:, 0:EC].rearrange("p (b e) -> p b e", e=P)
                for j in range(IB):
                    ins = nc.tensor.transpose(acc[:, j, 0:P], staged[:, j, :], ident[:, :])
                ins.then_inc(node_step, 1)
            begin(pe, "wT_T")
            nc.tensor.transpose(small[0:O0, 0:2 * H0], att[:, :], ident[0:2 * H0, 0:2 * H0])
            nc.tensor.transpose(small[:, 64:64 + O0], w0[:, :], ident[0:O0, 0:O0]).then_inc(node_step, 1)

            layernorm("ln0", xT)
            dense("whT_mm", w0T[:, :], hT)
            table("ta", va[0:O0, :], attT[:, :])
            table("tw", hT, w0T[:, :], ROW["L0_gnn_b"])
            scatter("passA", counting, P, pA, pA_all, windows_A)
            scatter("passB", lambda b, k: [exp_group(b)[:, k, :]], 3 * H0, None, pB, None)
            begin(pe, "den_mm")
            for blk in range(NBLK):
                ins = mm(small[0:NB, blk * H0:(blk + 1) * H0], va[0:3 * H0, blk * NB:(blk + 1) * NB], sel[:, :],
                         start=True, stop=True)
            ins.then_inc(node_step, 1)
            scatter("passC", wide, P, pC, pC, lambda: in_windows(pC, wide))
            layernorm("ln1", xT)
            table("th", hT, None)
            scatter("passD", wide, P, pD, pD, lambda: in_windows(pD, wide))
            layernorm("ln2", xT)
            table("t2", hT, w_in[:, :], ROW["L2_gnn_b_in"])

            begin(pe, "counts_mm")
            mm(small[:, 0:NBLK], before, counts, start=True, stop=True)
            mm(small[:, P:P + NBLK], avg[:, :], counts, start=True, stop=True).then_inc(node_step, 1)

            def attr_T(b, s):
                k0, kn = SUBS[s]
                for j in range(kn):
                    ins = nc.tensor.transpose(acc[0:R, s % 2, j * P:(j + 1) * P], gb[:, b, k0 + j, 0:R], ident[:, :])
                ins.then_inc(flt_T, 1)

            begin(pe, "filters")
            with pe.Fori(0, ITERS) as i:
                for b in range(2):
                    pe.wait_ge(attr_in[b], (i + 1) * (16 * (b + 1)))
                    attr_T(b, 0)
                    for s, (k0, kn) in enumerate(SUBS):
                        n1 = i * (2 * NSUB) + (b * NSUB + s + 1)
                        pe.wait_ge(flt_Tc, n1)
                        if s == NSUB - 1:
                            pe.sem_inc(attr_used, 1)
                        mm(acc[0:F2, 2 + s % 2, 0:kn * P], w_f1[:, :], attrT[s % 2][:, 0:kn * P], start=True, stop=True)\
                            .then_inc(flt_h, 1)
                        if s + 1 < NSUB:
                            attr_T(b, s + 1)
                        pe.wait_ge(flt_hid, n1)
                        for j in range(kn):
                            o = acc[:, 4 + s % 2, j * F2:(j + 1) * F2]
                            mm(o, ones_row[0:1, :], ROW["L2_gnn_b_f2"], start=True, stop=False)
                            ins = mm(o, hid[s % 2][:, j * P:(j + 1) * P], w_f2[:, :], start=False, stop=True)
                        ins.then_inc(flt_W, 1)

            begin(pe, "passE")
            open_acc(P)
            pe.sem_inc(pE.oh_used, CREDIT)
            with pe.If(pe.value_load(covered_s[0:1, 0:1], min_val=0, max_val=1)):
                with pe.Fori(0, ITERS) as i:
                    _, offs = nc.values_load_multi_w_load_instructions(
                        blk_offs[0:1, bass.ds(i * 4, 4)], engines=[PE_ENGINE], min_val=0, max_val=NCH * BPSUM - NB,
                        skip_runtime_bounds_check_because="blocks of nodes by their number")
                    for b in range(2):
                        pe.wait_ge(pE.oh_ready, i * 2 + (b + 1))
                        pe.wait_ge(pE.part3, i * 2 + (b + 1))
                        for k in range(G):
                            for st in narrow(b, k):
                                for w in range(2):
                                    ins = mm(acc_row[0:st.shape[1], bass.ds(offs[2 * b + w], NB)], st,
                                             onehot_blks(b, w)[:, k, :], start=False, stop=False)
                        ins.then_inc(pE.oh_used, G)
            with pe.Else():
                all_nodes(pE, narrow)
            close_acc(P)
            dense("o1_mm", w_o1[:, :], va)
            dense("o2_mm", w_o2[:, :], va)
            layernorm("ln3", xT)
            for n, name in ((0, "tq"), (1, "tk"), (2, "tv")):
                table(name, hT, wsq[:, n, :], ROW["L3_gnn_b" + "QKV"[n]])
            scatter("passF", wide, P, pF_all, pF_all, lambda: in_windows(pF_all, wide))
            dense("wo_mm", wsq[:, 3, :], va)
            layernorm("ln4", hT)
            dense("w1_mm", wsq[:, 4, :], hT)
            dense("w2_mm", wsq[:, 5, :], va)
            layernorm("ln5", hT)
            table("fin", xT, None)


_INS = ['x', 'src', 'dst', 'edge_attr_32', 'edge_weight', 'L0_gnn_W', 'L0_gnn_b', 'L0_gnn_att_src', 'L0_gnn_att_dst',
 'L2_gnn_w_in', 'L2_gnn_b_in', 'L2_gnn_w_f1', 'L2_gnn_b_f1', 'L2_gnn_w_f2', 'L2_gnn_b_f2', 'L2_gnn_w_o1',
 'L2_gnn_b_o1', 'L2_gnn_w_o2', 'L2_gnn_b_o2', 'L3_gnn_WQ', 'L3_gnn_bQ', 'L3_gnn_WK', 'L3_gnn_bK', 'L3_gnn_WV',
 'L3_gnn_bV', 'L3_gnn_WO', 'L3_gnn_bO', 'L3_gnn_W1', 'L3_gnn_b1', 'L3_gnn_W2', 'L3_gnn_b2', 'L3_gnn_ln1_g',
 'L3_gnn_ln1_b', 'L3_gnn_ln2_g', 'L3_gnn_ln2_b']


def kernel(**inputs):
    import numpy as _np
    import concourse.bacc as _bacc
    from concourse import mybir as _mybir
    from concourse.bass_utils import run_bass_kernel_spmd as _run

    nc = _bacc.Bacc("TRN2", target_bir_lowering=False, num_devices=1)
    arrays, args = {}, {}
    for name in _INS:
        a = _np.ascontiguousarray(inputs[name])
        arrays[f"in_{name}_dram"] = a
        args[name] = nc.dram_tensor(f"in_{name}_dram", a.shape, _mybir.dt.from_np(a.dtype), kind="ExternalInput").ap()
    out = nc.dram_tensor("out_0_dram", (3125, 128), _mybir.dt.float32, kind="ExternalOutput").ap()
    build(nc, args, out)
    r = _run(nc, [arrays], core_ids=[0])
    return r.results[0]["out_0_dram"]
```

```python
from contextlib import ExitStack
import math

import concourse.bass as bass
from concourse import mybir

F32 = mybir.dt.float32
BF16 = mybir.dt.bfloat16
F16 = mybir.dt.float16
I16 = mybir.dt.int16
I32 = mybir.dt.int32
U32 = mybir.dt.uint32
ALU = mybir.AluOpType
ACT = mybir.ActivationFunctionType
RMAX = bass.bass_isa.ReduceOp.max
RADD = bass.bass_isa.ReduceOp.add
AXX = mybir.AxisListType.X
SP_ENGINE = mybir.EngineType.SP
PE_ENGINE = mybir.EngineType.PE

P = 128
N = 3125
D = 128
E = 103125
NCH = 7
CH = 448
NP = NCH * CH
HALF = NP // 2
NB = 112
NBLK = NP // NB
BPC = CH // NB
TILES = -(-E // P)
LASTE = E - (TILES - 1) * P
G = 13
BODY = 2 * G
ITERS = TILES // BODY
IB = -(-TILES // P)
H0 = 4
O0 = 32
R = 32
F2 = 64
NH = 8
HD = D // NH
SUB = 4
SUBS = [(k, min(SUB, G - k)) for k in range(0, G, SUB)]
NSUB = len(SUBS)
BODY_SUBS = [(b, s, k0, kn) for b in range(2) for s, (k0, kn) in enumerate(SUBS)]


def sub_at(i, n):
    return i + n // len(BODY_SUBS), BODY_SUBS[n % len(BODY_SUBS)]


ROWM = F2 + 1
GE = G * P
EPS = 1e-5
LOG2 = float(math.log(2.0))
BIG = 1e30
WIN = 64
BPSUM = 512
FAR = 10000.0
CREDIT = BODY

assert TILES == ITERS * BODY

STEPS = [
    "iota", "iota_h", "x_T", "x_copy",
    "dst_f", "dst_T", "dst_copy", "win", "win_flag", "ka_T", "ka_copy", "kb_T", "kb_copy", "src_f", "src_T", "src_copy", "w_f", "w_T", "w_copy",
    "keys", "grp", "grp_all", "grp_base", "wT_T", "wT_copy",
]


def ln_steps(n):
    return [f"{n}_mean", f"{n}_center", f"{n}_square", f"{n}_var", f"{n}_std", f"{n}_recip", f"{n}_out"]


def table_steps(n):
    return [f"{n}_{s}{q}" for q in range(NBLK // NCH) for s in ("mm", "cp")]


STEPS += ln_steps("ln0") + ["whT_mm", "whT_cp"] + table_steps("ta") + table_steps("tw")
STEPS += ["passA", "cnt_cp", "logit_pad", "logit_leaky", "logit_max", "logit_all", "logit_neg", "logit_exp",
          "exp_b1", "exp_r1", "exp_b2", "exp_b3"]
STEPS += ["passB", "den_1", "den_2", "den_3", "den_recip", "passC", "x1"]
STEPS += ln_steps("ln1") + table_steps("th") + ["passD", "mean_max", "mean_recip", "mean_mul", "x2"]
STEPS += ln_steps("ln2") + table_steps("t2") + ["before", "pair_zero", "counts", "counts_mm", "places", "filters", "passE", "agg_cp", "o1_mm"]
STEPS += ["o1_relu", "o1_abs", "o1_exp", "o1_ln", "o1_sum", "o2_mm", "x3"]
STEPS += ln_steps("ln3") + table_steps("tq") + table_steps("tk") + table_steps("tv") + ["passF"]
STEPS += ["z_sum", "z_all", "z_recip", "z_head", "z_red", "att_cp", "wo_mm", "wo_add"]
STEPS += ln_steps("ln4") + ["g1", "w1_mm", "w1_relu", "w2_mm", "w2_add"] + ln_steps("ln5") + ["g2", "x4"]
STEPS += [f"fin_{s}{q}" for q in range(NBLK // NCH) for s in ("mm", "cp")]
AT = {name: n + 1 for n, name in enumerate(STEPS)}


def build(nc, t, out):
    ctx = ExitStack()
    with ctx:
        def sb(name, shape, dt):
            return ctx.enter_context(nc.sbuf_tensor(name, shape, dt))

        def sem(name):
            return ctx.enter_context(nc.semaphore(name))

        tab_a = nc.dram_tensor("tab_a", (NP, 2 * H0), F32).ap()
        tab_w = nc.dram_tensor("tab_w", (NP, O0 + H0), F32).ap()
        tab_h = nc.dram_tensor("tab_h", (NP, D), F32).ap()
        tab_2 = nc.dram_tensor("tab_2", (NP, F2), F32).ap()
        tab_q = nc.dram_tensor("tab_q", (NP, D), F32).ap()
        win_d = nc.dram_tensor("win_d", (IB * P, 2), I16).ap()
        tab_kv = nc.dram_tensor("tab_kv", (NP, 2 * D), F32).ap()
        tab_m = nc.dram_tensor("tab_m", (TILES * P, ROWM), F32).ap()

        acc = ctx.enter_context(nc.psum_tensor("acc", [P, NCH, 512], F32))
        small = ctx.enter_context(nc.psum_tensor("small", [P, 512], F32))

        def nodes(ap):
            return ap.rearrange("p (c n) -> p c n", c=NCH)

        xT = sb("xT", [P, NP], F32)
        hT = sb("hT", [P, NP], F32)
        va = sb("va", [P, NP], F32)
        vb = sb("vb", [P, NP], F32)
        cnt = sb("cnt", [P, NP], F32)
        tabs = sb("tabs", [NB, NBLK, D], F32)

        EC = IB * P
        ew = sb("ew", [P, EC], F32)
        dst_key = sb("dst_key", [P, TILES], F16)
        src_key = sb("src_key", [P, TILES], F16)
        dst_idx = sb("dst_idx", [P, TILES], I16)
        src_idx = sb("src_idx", [P, TILES], I16)
        padneg = sb("padneg", [P, 1], F32)
        ed = sb("ed", [P, TILES * H0], F32)
        e4 = ed[:, :]

        ga = sb("ga", [P, 2, G, 2 * D], F32)
        gb = sb("gb", [P, 2, G, D], F32)
        msg = sb("msg", [P, G * D], F32)
        res = sb("res", [P, G * D], F32)
        parts = sb("parts", [P, 2, 3, G * D], BF16)
        sc = sb("sc", [P, G, NH], F32)
        stage_i = parts[:, :, :, :].rearrange("p a s f -> p (a s f)")[:, 0:2 * EC].bitcast(I32)\
            .rearrange("p (b e) -> p b e", e=P)
        stage_f = cnt[:, 0:EC].rearrange("p (b e) -> p b e", e=P)
        dstf = msg[:, 0:EC]
        srcf = res[:, 0:EC]
        exp_parts = ga[:, :, :, :].rearrange("p a k f -> p (a k f)").bitcast(BF16)[:, 0:TILES * 3 * H0]\
            .rearrange("p (t s) -> p t s", s=3 * H0)
        src_blk = res[:, 0:TILES // 2].bitcast(F16)
        src_low = res[:, TILES // 2:TILES].bitcast(F16)
        lk = gb[:, :, :, :].rearrange("p a k f -> p (a k f)")[:, 0:TILES * H0]
        key_a = sb("key_a", [P, EC], BF16)
        key_b = sb("key_b", [P, EC], BF16)
        win_off = sb("win_off", [1, 2 * TILES], I16)
        covered = sb("covered", [1, 1], I32)
        iota_w = sb("iota_w", [P, WIN], BF16)
        wtmp = ga[:, 0, 0, 0:8 * IB].rearrange("p (j b) -> p j b", b=IB)
        NG = 2 * ITERS
        grp_base = sb("grp_base", [P, NG], F32)
        grp_row = sb("grp_row", [1, NG], I16)
        grp_dst = ga[:, 1, :, :].rearrange("p k f -> p (k f)")[:, 0:TILES]
        grp_ends, grp_ends_all = (ga[:, 0, n, 0:2 * NG] for n in range(2))
        grp_key = sb("grp_key", [P, G], F16)
        win_st = sb("win_st", [P, IB, 2], I16)
        idx_a = sb("idx_a", [P, 2, G], I32)
        idx_b = sb("idx_b", [P, 2, G], I32)
        onehot = sb("onehot", [P, 2, NP], BF16)
        alpha = sb("alpha", [P, G * H0], F32)
        ex = sb("ex", [P, G, NH], F32)
        exv = sb("exv", [P, G, NH], F32)
        zacc = sb("zacc", [P, G, NH], F32)
        attrT, hid, hid_r, hid_e = ([v[:, n * SUB * P:(n + 1) * SUB * P] for v in (va, vb)] for n in range(4))
        attrs = gb[:, :, :, :].rearrange("p a k f -> p a (k f)")[:, :, SUB * D:SUB * D + G * R]
        w_f1_pairs, w_f2_pair, b_f2_sub = (hT[0:rows_, at_:at_ + w_] for rows_, at_, w_ in
                                           ((P, 4 * SUB * P, SUB * F2), (P, 4 * SUB * P + SUB * F2, 2 * F2),
                                            (1, 4 * SUB * P + (SUB + 2) * F2, SUB * F2)))
        mrows = cnt[:, 0:2 * G * ROWM].rearrange("p (a k f) -> p a k f", a=2, f=ROWM)
        before = cnt[:, 2 * G * ROWM:2 * G * ROWM + P]
        place_i = ed[:, 0:TILES].bitcast(I32)
        place_f = ed[:, TILES:2 * TILES]
        halves = ed[:, 2 * TILES:4 * TILES].bitcast(F16)
        blk_of, rank, mask, sums = (halves[:, n * TILES:(n + 1) * TILES] for n in range(4))
        mask_off = ed[:, 3 * TILES:4 * TILES]
        blk_at = cnt[:, 2 * G * ROWM + P:]
        offs, total, first_of = (blk_at[:, n * NBLK:(n + 1) * NBLK] for n in range(3))
        counts = gb[:, 0, 1, 0:ITERS]
        glim, blk_a, blk_b, blk_ch, blk_off, base_sa, base_sb = (
            blk_at[:, 4 * NBLK + n * NG:4 * NBLK + (n + 1) * NG] for n in range(7))
        place_g = idx_b
        srows = ga[:, :, :, :].rearrange("p a k f -> p a (k f)")[:, :, 0:G * ROWM].rearrange("p a (k f) -> p a k f", f=ROWM)
        more = blk_at[:, 4 * NBLK + 7 * NG:]
        blk_offs = more[0:1, 0:NG].bitcast(I16)
        covered_s = sb("covered_s", [1, 1], I32)
        key_s = more[:, NG:NG + G].bitcast(F16).rearrange("p (w k) -> p w k", w=2)

        oh_flat = onehot[:, :, :].rearrange("p a n -> p (a n)")

        def onehot_wins(b):
            return oh_flat[:, b * G * 2 * WIN:(b + 1) * G * 2 * WIN].rearrange("p (k w n) -> p k w n", w=2, n=WIN)

        def onehot_win(b, w):
            return onehot_wins(b)[:, :, w, :]

        def onehot_blks(b, w):
            return oh_flat[:, (b * 2 + w) * G * NB:(b * 2 + w + 1) * G * NB].rearrange("p (k n) -> p k n", n=NB)

        def onehot_grp(slot):
            return oh_flat[:, slot * G * P:(slot + 1) * G * P].rearrange("p (k n) -> p k n", n=P)

        ohT = va[:, 0:G * P]
        ohT_m = [hT[:, n * SUB * P:(n + 1) * SUB * P] for n in range(4)]
        WB = G // 2 + 1

        def win_rows(b, c0, width):
            return gb[:, b, 0, c0:c0 + width]

        def win_rows_q(b):
            return va[:, G * P + b * D:G * P + (b + 1) * D]

        LB = BPSUM // D
        BODY_LOCALS = [(b, k, min(LB, G - k)) for b in range(2) for k in range(0, G, LB)]
        NLB = len(BODY_LOCALS) // 2

        def local_q(k):
            return small[:, 0:k * D]

        def small_bf():
            return small[:, :].bitcast(BF16)

        def turned_m(n):
            return acc[:, 6, :].bitcast(BF16)[:, n * SUB * P:(n + 1) * SUB * P]

        iota_i = vb[:, :].bitcast(I32)
        iota_h = sb("iota_h", [P, NP], F16)
        ident = sb("ident", [P, P], F32)
        avg = sb("avg", [P, P], F32)
        ones_bf = sb("ones_bf", [P, P], BF16)
        ident_bf = sb("ident_bf", [P, P], BF16)
        ones_row = sb("ones_row", [1, P], F32)
        zero_bf = sb("zero_bf", [P, CH], BF16)
        eps_col = sb("eps_col", [P, 1], F32)
        headm = sb("headm", [P, NH], F32)
        colred = sb("colred", [P, 4], F32)
        zsum = sb("zsum", [P, NH], F32)
        zall = sb("zall", [P, NH], F32)
        zrec = sb("zrec", [P, NH], F32)
        zhm = sb("zhm", [P, NH], F32)

        w0 = sb("w0", [O0, D], F32)
        w0T = sb("w0T", [D, O0], F32)
        att = sb("att", [2 * H0, O0], F32)
        attT = sb("attT", [O0, 2 * H0], F32)
        w_in = sb("w_in", [D, F2], F32)
        w_o1 = sb("w_o1", [2 * F2, D], F32)
        w_o2 = sb("w_o2", [D, D], F32)
        wsq = sb("wsq", [D, 6, D], F32)
        SQ = ["WQ", "WK", "WV", "WO", "W1", "W2"]
        rows = sb("rows", [1, O0 + F2 + 3 * D], F32)
        ROW = {}
        at = 0
        for name, width in (("L0_gnn_b", O0), ("L2_gnn_b_in", F2),
                            ("L3_gnn_bQ", D), ("L3_gnn_bK", D), ("L3_gnn_bV", D)):
            ROW[name] = rows[0:1, at:at + width]
            at += width
        COLS = ["L0_gnn_b", "L2_gnn_b_f1", "L2_gnn_b_o1", "L2_gnn_b_o2", "L3_gnn_bO", "L3_gnn_b1", "L3_gnn_b2",
                "L3_gnn_ln1_g", "L3_gnn_ln1_b", "L3_gnn_ln2_g", "L3_gnn_ln2_b"]
        cols = sb("cols", [P, len(COLS)], F32)

        def col(name):
            n = COLS.index(name)
            k = t[name].shape[0]
            return cols[0:k, n:n + 1]

        node_step = sem("node_step")
        loaded = sem("loaded")
        idx_loaded = sem("idx_loaded")
        pads_set = sem("pads_set")
        tab_done = sem("tab_done")
        out_done = sem("out_done")
        const_step = sem("const_step")
        const_v = sem("const_v")
        cov_ready = sem("cov_ready")
        win_step = sem("win_step")
        win_dma = sem("win_dma")
        z_part = sem("z_part")
        z_ready = sem("z_ready")
        grp_step = sem("grp_step")
        grp_keyed = sem("grp_keyed")
        local_sb = sem("local_sb")
        grp_hot = sem("grp_hot")
        attr_in = [sem("attr_in0"), sem("attr_in1")]
        attr_used = sem("attr_used")
        flt_T = sem("flt_T")
        flt_Tc = sem("flt_Tc")
        flt_h = sem("flt_h")
        flt_abs = sem("flt_abs")
        flt_exp = sem("flt_exp")
        flt_ln = sem("flt_ln")
        flt_hid = sem("flt_hid")
        flt_W = sem("flt_W")
        flt_m = sem("flt_m")
        flt_weighted = sem("flt_weighted")
        place_step = sem("place_step")
        pair_loaded = sem("pair_loaded")
        block_step = sem("block_step")
        keys_made = sem("keys_made")
        rows_made = sem("rows_made")
        rows_sent = [sem("rows_sent0"), sem("rows_sent1")]
        SENT = 16 * G * ITERS

        def heads(ap):
            return ap.rearrange("p (t h) -> p t h", h=H0)

        e4h, lkh = heads(e4), heads(lk)

        def e4h_at(tile):
            return heads(ed[:, bass.ds(tile * H0, G * H0)])

        def exp_by_block(b):
            return parts[:, b, :, :].rearrange("p s f -> p (s f)")[:, 0:G * NBLK * 3 * H0]\
                .rearrange("p (k j s) -> p k j s", k=G, j=NBLK)

        def onehot_low(b):
            return oh_flat[:, b * G * NB:(b + 1) * G * NB].rearrange("p (k n) -> p k n", n=NB)

        onehot_of_blk = oh_flat[:, 2 * G * NB:2 * G * NB + G * NBLK].rearrange("p (k j) -> p k j", j=NBLK)

        def msg_wide(b):
            return msg[:, :].rearrange("p (k f) -> p k f", f=D)

        def msg_narrow(b):
            return srows[:, b, :, 0:F2]

        def res_of(m):
            f = m.shape[2]
            return res[:, 0:G * f].rearrange("p (k f) -> p k f", f=f)

        def parts_wide(b):
            return [parts[:, b, s, :].rearrange("p (k f) -> p k f", f=D) for s in range(3)]

        def parts_narrow(b):
            both = parts[:, b, 0, :].rearrange("p (k f) -> p k f", f=D)
            return [both[:, :, 0:F2], both[:, :, F2:D], parts[:, b, 1, 0:G * F2].rearrange("p (k f) -> p k f", f=F2)]

        class Pass:

            def __init__(self, q, gathers=True, parts=True, local=False, scores=0, weights=False, scatters=True, loads=False):
                if scatters:
                    self.oh_ready = sem(f"oh_ready_{q}")
                    self.oh_used = sem(f"oh_used_{q}")
                    self.part3 = sem(f"part3_{q}")
                if gathers or loads:
                    self.gathered = [sem(f"gathered0_{q}"), sem(f"gathered1_{q}")]
                    self.taken = sem(f"taken_{q}")
                if gathers:
                    self.idx_staged = sem(f"idx_staged_{q}")
                if parts:
                    self.msg = sem(f"msg_{q}")
                    self.part1 = sem(f"part1_{q}")
                    self.rest1 = sem(f"rest1_{q}")
                    self.part2 = sem(f"part2_{q}")
                self.score = [sem(f"score{n}_{q}") for n in range(scores)]
                if weights:
                    self.weight = sem(f"weight_{q}")
                if local:
                    self.rows_in = [sem(f"rows_in0_{q}"), sem(f"rows_in1_{q}")]
                    self.rows_used = sem(f"rows_used_{q}")
                    self.turned = sem(f"turned_{q}")
                    self.turned_sb = sem(f"turned_sb_{q}")
                    self.local = sem(f"local_{q}")

            def have_rows(self, i, gathers=1):
                return (i + 1) * (16 * G * gathers)

        pA = Pass("A", parts=False, local=True)
        pB = Pass("B", gathers=False, parts=False)
        pC = Pass("C", weights=True)
        pD = Pass("D")
        pM = Pass("M", parts=False, scatters=False, local=True)
        pE = Pass("E", gathers=False, loads=True)
        pF = Pass("F", scores=4, weights=True, local=True)
        GRP_A, GRP_M, GRP_F = 0, NG, 2 * NG

        block = ctx.enter_context(nc.Block())
        FULL = N // NB
        REST = N - FULL * NB
        LASTQ = NBLK // NCH - 1

        def begin(eng, name):
            if AT[name] > 1:
                eng.wait_ge(node_step, AT[name] - 1)

        def dram_tab(table):
            return table.rearrange("(b p) f -> p b f", p=NB)

        xv = t["x"]
        loads = [(tabs[:, 0:FULL, :], xv[0:FULL * NB, :].rearrange("(b p) f -> p b f", p=NB)),
                 (tabs[0:REST, FULL, :], xv[FULL * NB:N, :]),
                 (w0[:, :], t["L0_gnn_W"]), (att[0:H0, :], t["L0_gnn_att_src"]),
                 (att[H0:2 * H0, :], t["L0_gnn_att_dst"]), (w_in[:, :], t["L2_gnn_w_in"]),
                 (w_o1[0:F2, :], t["L2_gnn_w_o1"]), (w_o1[F2:2 * F2, :], t["L2_gnn_w_o1"]),
                 (w_o2[:, :], t["L2_gnn_w_o2"])]
        loads += [(wsq[:, n, :], t["L3_gnn_" + name]) for n, name in enumerate(SQ)]
        loads += [(ap, t[name].rearrange("(o f) -> o f", o=1)) for name, ap in ROW.items()]
        loads += [(col(name), t[name].rearrange("(f o) -> f o", o=1)) for name in COLS]
        b_f1 = cols[:, COLS.index("L2_gnn_b_f1"):COLS.index("L2_gnn_b_f1") + 1]
        loads += [(b_f1[F2:2 * F2, :], t["L2_gnn_b_f1"].rearrange("(f o) -> f o", o=1))]
        LOADED = 16 * len(loads)
        pair_loads = [(w_f1_pairs[k * R:(k + 1) * R, k * F2:(k + 1) * F2], t["L2_gnn_w_f1"]) for k in range(SUB)]
        pair_loads += [(w_f2_pair[k * F2:(k + 1) * F2, k * F2:(k + 1) * F2], t["L2_gnn_w_f2"]) for k in range(2)]
        pair_loads += [(b_f2_sub[:, k * F2:(k + 1) * F2], t["L2_gnn_b_f2"].rearrange("(o f) -> o f", o=1))
                       for k in range(SUB)]

        def pairs(kn):
            return [(j, min(2, kn - j)) for j in range(0, kn, 2)]

        def hidden_of(v, kn):
            return v[0:min(kn, 2) * F2, 0:len(pairs(kn)) * P]

        WIN_OFFS = 24

        @block.sync
        def _(sp):
            sp.wait_ge(pads_set, 2)
            for dst_ap, src_ap in loads:
                sp.dma_start(dst_ap, src_ap).then_inc(loaded, 16)

            whole = (IB - 1) * P
            last = TILES - 1 - whole
            for name, staged, after, pads in (("dst", stage_i, None, 2), ("src", stage_i, "dst_f", 3),
                                              ("edge_weight", stage_f, "src_copy", 4)):
                if after:
                    sp.wait_ge(node_step, AT[after])
                    sp.wait_ge(pads_set, pads)
                v = t[name]
                sp.dma_start(staged[:, 0:IB - 1, :], v[0:whole * P].rearrange("(b r e) -> r b e", r=P, e=P))\
                    .then_inc(idx_loaded, 16)
                sp.dma_start(staged[0:last, IB - 1, :], v[whole * P:(whole + last) * P].rearrange("(r e) -> r e", e=P))\
                    .then_inc(idx_loaded, 16)
                sp.dma_start(staged[last:last + 1, IB - 1, 0:LASTE],
                             v[(whole + last) * P:E].rearrange("(r e) -> r e", r=1)).then_inc(idx_loaded, 16)

            sp.wait_ge(win_step, WIN_OFFS)
            sp.dma_start(win_d.rearrange("(b r) w -> r b w", r=P), win_st[:, :, :]).then_inc(win_dma, 16)
            sp.wait_ge(win_dma, 16)
            sp.dma_start(win_off[:, :], win_d[0:TILES, :].rearrange("(o t) w -> o (t w)", o=1)).then_inc(win_dma, 16)

            def store(table, width, stage, c0=0):
                sp.wait_ge(node_step, AT[stage])
                sp.dma_start(dram_tab(table)[:, :, c0:c0 + width], tabs[:, :, 0:width]).then_inc(tab_done, 16)

            def window_bases(i):
                _, bases = nc.values_load_multi_w_load_instructions(
                    grp_row[0:1, bass.ds(i * 2, 2)], engines=[SP_ENGINE], min_val=0, max_val=NP - P,
                    skip_runtime_bounds_check_because="groups() keeps the windows among the nodes")
                return bases

            def window_load(q, i, b, bases, table, c0, width, rows):
                sp.wait_ge(q.rows_used, i * 2 + (b + 1))
                sp.dma_start(rows, table[bass.ds(bases[b], P), c0:c0 + width])\
                    .then_inc(q.rows_in[b], 16)

            def window_rows(q, table, c0, width, rows):
                with sp.Fori(0, ITERS) as i:
                    bases = window_bases(i)
                    for b in range(2):
                        window_load(q, i, b, bases, table, c0, width, rows(b))

            store(tab_a, 2 * H0, f"ta_cp{LASTQ}")
            sp.wait_ge(cov_ready, 1)
            sp.wait_ge(tab_done, 16)
            with sp.If(sp.value_load(covered[0:1, 0:1], min_val=0, max_val=1)):
                window_rows(pA, tab_a, H0, H0, lambda b: win_rows(b, 0, H0))
            store(tab_w, O0 + H0, "den_recip")
            store(tab_h, D, f"th_cp{LASTQ}")
            store(tab_2, F2, f"t2_cp{LASTQ}")

            sp.wait_ge(node_step, AT["pair_zero"])
            for dst_ap, src_ap in pair_loads:
                sp.dma_start(dst_ap, src_ap).then_inc(pair_loaded, 16)
            begin(sp, "filters")
            av = t["edge_attr_32"]

            def attr_tiles(b):
                return attrs[:, b, :].rearrange("p (k f) -> p k f", f=R)

            def attributes(b, first, edges):
                if b == 0:
                    sp.dma_start(attr_tiles(b)[:, :, :], av[bass.ds(first, G * P), :].rearrange("(k e) f -> e k f", e=P))\
                        .then_inc(attr_in[b], 16)
                else:
                    sp.dma_start(attr_tiles(b)[:, 0:G - 1, :],
                                 av[bass.ds(first, (G - 1) * P), :].rearrange("(k e) f -> e k f", e=P))\
                        .then_inc(attr_in[b], 16)
                    sp.dma_start(attr_tiles(b)[0:edges, G - 1, :], av[bass.ds(first + (G - 1) * P, edges), :])\
                        .then_inc(attr_in[b], 16)

            def all_attributes(local):
                def rows(i, b, bases):
                    if local:
                        window_load(pM, i, b, bases, tab_2, 0, F2, win_rows(b, F2, F2))

                bases = window_bases(0) if local else None
                for b in range(2):
                    attributes(b, b * GE, P)
                    rows(0, b, bases)
                with sp.Fori(1, ITERS - 1) as i:
                    bases = window_bases(i) if local else None
                    for b in range(2):
                        sp.wait_ge(attr_used, i * 2 + (b - 1))
                        attributes(b, i * (BODY * P) + b * GE, P)
                        rows(i, b, bases)
                bases = window_bases(ITERS - 1) if local else None
                for b in range(2):
                    sp.wait_ge(attr_used, (ITERS - 1) * 2 + b - 1)
                    attributes(b, (ITERS - 1) * BODY * P + b * GE, LASTE)
                    rows(ITERS - 1, b, bases)

            sp.wait_ge(tab_done, 16 * 4)
            with sp.If(sp.value_load(covered[0:1, 0:1], min_val=0, max_val=1)):
                all_attributes(True)
            with sp.Else():
                all_attributes(False)

            begin(sp, "passE")
            for b in range(2):
                sp.wait_ge(rows_sent[b], SENT)
            with sp.Fori(0, ITERS) as i:
                for b in range(2):
                    sp.wait_ge(pE.taken, i * 2 + (b + 1))
                    sp.dma_start(srows[:, b, :, :].rearrange("p k f -> p (k f)"),
                                 tab_m[bass.ds(i * (BODY * P) + b * GE, GE), :].rearrange("(p k) f -> p (k f)", k=G))\
                        .then_inc(pE.gathered[b], 16)

            store(tab_q, D, f"tq_cp{LASTQ}")
            store(tab_kv, D, f"tk_cp{LASTQ}", 0)
            store(tab_kv, D, f"tv_cp{LASTQ}", D)
            sp.wait_ge(tab_done, 16 * 7)
            with sp.If(sp.value_load(covered[0:1, 0:1], min_val=0, max_val=1)):
                window_rows(pF, tab_q, 0, D, win_rows_q)

            sp.wait_ge(node_step, AT[f"fin_cp{LASTQ}"])
            sp.dma_start(out[0:FULL * NB, :].rearrange("(b p) f -> p b f", p=NB), tabs[:, 0:FULL, :])\
                .then_inc(out_done, 16)
            sp.dma_start(out[FULL * NB:N, :], tabs[0:REST, FULL, :]).then_inc(out_done, 16)
            sp.wait_ge(out_done, 32)

        @block.gpsimd
        def _(pool):
            count = [0]

            def link(ins):
                count[0] += 1
                ins.then_inc(const_step, 1)
                pool.wait_ge(const_step, count[0])

            link(nc.gpsimd.memset(ident[:, :], 0.0))
            link(nc.gpsimd.affine_select(out=ident[:, :], in_=ident[:, :], compare_op=ALU.not_equal, fill=1.0,
                                         base=0, pattern=[[-1, P]], channel_multiplier=1))
            link(nc.gpsimd.memset(headm[:, :], 1.0))
            link(nc.gpsimd.affine_select(out=headm[:, :], in_=headm[:, :], compare_op=ALU.is_ge, fill=0.0,
                                         base=0, pattern=[[-HD, NH]], channel_multiplier=1))
            link(nc.gpsimd.affine_select(out=headm[:, :], in_=headm[:, :], compare_op=ALU.is_ge, fill=0.0,
                                         base=HD - 1, pattern=[[HD, NH]], channel_multiplier=-1))
            nc.gpsimd.iota(iota_i, pattern=[[1, NP]], base=-HALF, channel_multiplier=0).then_inc(node_step, 1)

            def gather(q, tables):
                pool.sem_inc(q.taken, 2)
                with pool.Fori(0, ITERS) as i:
                    for b in range(2):
                        pool.wait_ge(q.taken, i * 2 + (b + 1))
                        pool.nop(nofuse=True)
                        for table, idx, staged, buf, width in tables:
                            nc.gpsimd.tensor_copy(staged[:, b, :], idx[:, bass.ds(i * BODY + b * G, G)])\
                                .then_inc(q.idx_staged, 1)
                        pool.wait_ge(q.idx_staged, (i * 2 + (b + 1)) * len(tables))
                        pool.nop(nofuse=True)
                        for k in range(G):
                            for table, idx, staged, buf, width in tables:
                                nc.gpsimd.indirect_dma_start(
                                    buf[:, b, k, 0:width], None, table[:, :],
                                    bass.IndirectOffsetOnAxis(ap=staged[:, b, k:k + 1].bitcast(U32), axis=0))\
                                    .then_inc(q.gathered[b], 16)

            begin(pool, "win_flag")
            nc.gpsimd.partition_all_reduce(colred[:, 1:2], colred[:, 0:1], P, RMAX).then_inc(node_step, 1)
            begin(pool, "grp_all")
            nc.gpsimd.partition_all_reduce(grp_ends_all, grp_ends, P, RMAX).then_inc(node_step, 1)

            by_src, by_dst = (src_idx, idx_a), (dst_idx, idx_b)
            pool.wait_ge(tab_done, 16)
            pool.wait_ge(node_step, AT["keys"])
            pool.wait_ge(cov_ready, 1)
            with pool.If(pool.value_load(covered[0:1, 0:1], min_val=0, max_val=1)):
                gather(pA, [(tab_a, *by_src, ga, 2 * H0)])
            with pool.Else():
                gather(pA, [(tab_a, *by_src, ga, 2 * H0), (tab_a, *by_dst, gb, 2 * H0)])
            begin(pool, "logit_all")
            nc.gpsimd.partition_all_reduce(colred[:, 1:2], colred[:, 0:1], P, RMAX).then_inc(node_step, 1)
            pool.wait_ge(tab_done, 32)
            gather(pC, [(tab_w, *by_src, ga, O0 + H0)])
            pool.wait_ge(tab_done, 48)
            gather(pD, [(tab_h, *by_src, ga, D)])
            pool.wait_ge(tab_done, 64)
            begin(pool, "before")
            link(nc.gpsimd.memset(before, 1.0))
            nc.gpsimd.affine_select(out=before, in_=before, compare_op=ALU.is_ge, fill=0.0, base=-1,
                                    pattern=[[1, P]], channel_multiplier=-1).then_inc(node_step, 1)

            def fetch(i, b, staged):
                pool.wait_ge(pM.taken, i * 2 + (b + 1))
                pool.nop(nofuse=True)
                nc.gpsimd.tensor_copy(idx_a[:, b, :], dst_idx[:, bass.ds(i * BODY + b * G, G)])\
                    .then_inc(pM.idx_staged, 1)
                pool.wait_ge(pM.idx_staged, staged)
                pool.nop(nofuse=True)
                for k in range(G):
                    nc.gpsimd.indirect_dma_start(
                        ga[:, b, k, 0:F2], None, tab_2[:, :],
                        bass.IndirectOffsetOnAxis(ap=idx_a[:, b, k:k + 1].bitcast(U32), axis=0))\
                        .then_inc(pM.gathered[b], 16)

            def send(i, b, staged):
                pool.wait_ge(flt_m, i * len(BODY_SUBS) + (b * NSUB + 1))
                pool.nop(nofuse=True)
                nc.gpsimd.tensor_copy(place_g[:, b, :], place_i[:, bass.ds(i * BODY + b * G, G)])\
                    .then_inc(pM.idx_staged, 1)
                pool.wait_ge(pM.idx_staged, staged)
                pool.nop(nofuse=True)
                for s, (k0, kn) in enumerate(SUBS):
                    if s > 0:
                        pool.wait_ge(flt_m, i * len(BODY_SUBS) + (b * NSUB + s + 1))
                        pool.nop(nofuse=True)
                    for k in range(k0, k0 + kn):
                        nc.gpsimd.indirect_dma_start(
                            tab_m[:, :], bass.IndirectOffsetOnAxis(ap=place_g[:, b, k:k + 1].bitcast(U32), axis=0),
                            mrows[:, b, k, :], None).then_inc(rows_sent[b], 16)

            begin(pool, "filters")
            pool.sem_inc(pM.taken, 2)
            with pool.If(pool.value_load(covered[0:1, 0:1], min_val=0, max_val=1)):
                with pool.Fori(0, ITERS) as i:
                    for b in range(2):
                        send(i, b, i * 2 + (b + 1))
            with pool.Else():
                fetch(0, 0, 1)
                with pool.Fori(0, ITERS - 1) as i:
                    fetch(i, 1, i * 4 + 2)
                    send(i, 0, i * 4 + 3)
                    fetch(i + 1, 0, i * 4 + 4)
                    send(i, 1, i * 4 + 5)
                fetch(ITERS - 1, 1, ITERS * 4 - 2)
                send(ITERS - 1, 0, ITERS * 4 - 1)
                send(ITERS - 1, 1, ITERS * 4)
            begin(pool, "passE")
            pool.sem_inc(pE.taken, 2)
            pool.wait_ge(tab_done, 16 * 7)
            with pool.If(pool.value_load(covered[0:1, 0:1], min_val=0, max_val=1)):
                gather(pF, [(tab_kv, *by_src, ga, 2 * D)])
            with pool.Else():
                gather(pF, [(tab_kv, *by_src, ga, 2 * D), (tab_q, *by_dst, gb, D)])
            begin(pool, "z_all")
            nc.gpsimd.partition_all_reduce(zall[:, :], zsum[:, :], P, RADD).then_inc(node_step, 1)

        @block.scalar
        def _(act):
            def stage(name, *args, **kw):
                begin(act, name)
                nc.scalar.activation(*args, **kw).then_inc(node_step, 1)

            def layernorm(n):
                stage(f"{n}_square", vb[:, :], va[:, :], ACT.Square)
                stage(f"{n}_std", nodes(vb[:, :]), acc[:, :, 0:CH], ACT.Sqrt, bias=eps_col[:, 0:1])

            def table(n, width, done):
                for r in range(LASTQ + 1):
                    begin(act, f"{n}_cp{r}")
                    if r == 0:
                        act.wait_ge(tab_done, 16 * done)
                    nc.scalar.activation(tabs[:, r * NCH:(r + 1) * NCH, 0:width], acc[0:NB, :, 0:width], ACT.Copy)\
                        .then_inc(node_step, 1)

            def turn_copy(q, i, b, s):
                k0, k1 = (0, WB) if s == 0 else (WB, G)
                act.wait_ge(q.turned, i * 4 + (b * 2 + s + 1))
                act.wait_ge(q.rows_used, i * 2 + (b + 2))
                nc.scalar.activation(ohT[:, k0 * P:k1 * P], small_bf()[:, 0:(k1 - k0) * P], ACT.Copy)\
                    .then_inc(q.turned_sb, 1)

            def split(q, i, b, source, widths):
                g1 = i * 2 + (b + 1)
                first, second = widths(b)[0:2]
                act.wait_ge(q.msg, g1)
                act.wait_ge(q.oh_used, i * BODY + (b * G + CREDIT - G))
                nc.scalar.activation(first, source(b), ACT.Copy).then_inc(q.part1, 1)
                act.wait_ge(q.rest1, g1)
                nc.scalar.activation(second, res_of(source(b)), ACT.Copy).then_inc(q.part2, 1)

            layernorm("ln0")
            stage("whT_cp", nodes(va[0:O0, :]), acc[0:O0, :, 0:CH], ACT.Identity, bias=col("L0_gnn_b"))
            table("ta", 2 * H0, 0)
            table("tw", O0, 1)
            begin(act, "passA")
            act.wait_ge(cov_ready, 1)
            with act.If(act.value_load(covered[0:1, 0:1], min_val=0, max_val=1)):
                with act.Fori(0, ITERS) as i:
                    for b in range(2):
                        for s in range(2):
                            turn_copy(pA, i, b, s)
            stage("cnt_cp", nodes(cnt[:, :]), acc[:, :, 0:CH], ACT.Copy)
            stage("logit_exp", e4, e4, ACT.Exp, bias=colred[:, 2:3])
            stage("exp_b1", exp_parts[:, :, 0:H0], e4h, ACT.Copy)
            stage("exp_b2", exp_parts[:, :, H0:2 * H0], lkh, ACT.Copy)

            begin(act, "passC")
            with act.Fori(0, ITERS) as i:
                for b in range(2):
                    split(pC, i, b, msg_wide, parts_wide)
            layernorm("ln1")
            table("th", D, 2)
            begin(act, "passD")
            with act.Fori(0, ITERS) as i:
                for b in range(2):
                    act.wait_ge(pD.gathered[b], pD.have_rows(i))
                    act.wait_ge(pD.oh_used, i * BODY + (b * G + CREDIT - G))
                    nc.scalar.activation(parts_wide(b)[0], ga[:, b, :, 0:D], ACT.Copy).then_inc(pD.part1, 1)
                    act.wait_ge(pD.rest1, i * 2 + (b + 1))
                    nc.scalar.activation(parts_wide(b)[1], res_of(msg_wide(b)), ACT.Copy).then_inc(pD.part2, 1)
            layernorm("ln2")
            table("t2", F2, 3)

            begin(act, "filters")
            def attr_copy(i, n, local):
                k = sub_at(i, n)[1][3]
                attr_rows = k * R
                act.wait_ge(flt_T, i * len(BODY_SUBS) + (n + 1))
                if local:
                    nc.scalar.activation(ohT_m[n % 4][:, 0:k * P], turned_m(n % 2)[:, 0:k * P], ACT.Copy)
                nc.scalar.activation(attrT[n % 2][0:attr_rows, 0:P], acc[0:attr_rows, n % 2, 0:P], ACT.Copy)\
                    .then_inc(flt_Tc, 1)

            def filters(i, last, local):
                for n, (b, s, k0, k) in enumerate(BODY_SUBS):
                    n1 = i * len(BODY_SUBS) + (n + 1)
                    relu, e = hidden_of(hid_r[n % 2], k), hidden_of(hid_e[n % 2], k)
                    act.wait_ge(flt_h, n1)
                    hidden = hidden_of(acc[:, 2 + n % 2, :], k)
                    bias = b_f1[0:hidden.shape[0], :]
                    nc.scalar.activation(e, hidden, ACT.Abs, bias=bias).then_inc(flt_abs, 1)
                    nc.scalar.activation(relu, hidden, ACT.Relu, bias=bias)
                    act.wait_ge(flt_abs, n1)
                    nc.scalar.activation(e, e, ACT.Exp, scale=-1.0).then_inc(flt_exp, 1)
                    act.wait_ge(flt_exp, n1)
                    nc.scalar.activation(e, e, ACT.Ln, bias=1.0).then_inc(flt_ln, 1)
                    if not last or n + 2 < len(BODY_SUBS):
                        attr_copy(i, n + 2, local)

            def all_filters(local):
                nc.scalar.preload_act_table_set("natural_log_exp_and_others")
                attr_copy(0, 0, local)
                attr_copy(0, 1, local)
                with act.Fori(0, ITERS - 1) as i:
                    filters(i, False, local)
                filters(ITERS - 1, True, local)

            with act.If(act.value_load(covered[0:1, 0:1], min_val=0, max_val=1)):
                all_filters(True)
            with act.Else():
                all_filters(False)

            begin(act, "passE")
            with act.Fori(0, ITERS) as i:
                for b in range(2):
                    act.wait_ge(pE.gathered[b], (i + 1) * 16)
                    act.wait_ge(pE.oh_used, i * BODY + (b * G + CREDIT - G))
                    nc.scalar.activation(parts_narrow(b)[0], msg_narrow(b), ACT.Copy).then_inc(pE.part1, 1)
                    act.wait_ge(pE.rest1, i * 2 + (b + 1))
                    nc.scalar.activation(parts_narrow(b)[1], res_of(msg_narrow(b)), ACT.Copy).then_inc(pE.part2, 1)
            stage("agg_cp", nodes(va[:, :]), acc[:, :, 0:CH], ACT.Copy)
            b_o1 = col("L2_gnn_b_o1")
            stage("o1_relu", nodes(va[:, :]), acc[:, :, 0:CH], ACT.Relu, bias=b_o1)
            stage("o1_abs", nodes(vb[:, :]), acc[:, :, 0:CH], ACT.Abs, bias=b_o1)
            stage("o1_exp", vb[:, :], vb[:, :], ACT.Exp, scale=-1.0)
            stage("o1_ln", vb[:, :], vb[:, :], ACT.Ln, bias=1.0)
            layernorm("ln3")
            table("tq", D, 4)
            table("tk", D, 5)
            table("tv", D, 6)

            begin(act, "passF")
            def local_copies(i, b, first, end):
                for n, (b_, k0, k) in enumerate(BODY_LOCALS):
                    if b * NLB + first <= n < b * NLB + end:
                        act.wait_ge(pF.local, i * len(BODY_LOCALS) + (n + 1))
                        nc.scalar.activation(gb[:, b, k0:k0 + k, :], local_q(k).rearrange("p (k f) -> p k f", f=D),
                                             ACT.Copy).then_inc(local_sb, 1)

            def edges_F(i, last, local):
                for b in range(2):
                    g1 = i * 2 + (b + 1)
                    ahead = (i + 1, b) if local and not last else None
                    act.wait_ge(pF.score[3], g1)
                    nc.scalar.activation(ex[:, :, :], sc[:, :, :], ACT.Exp).then_inc(pF.weight, 1)
                    if ahead:
                        turn_copy(pF, *ahead, 0)
                    first, second, _ = parts_wide(b)
                    act.wait_ge(pF.msg, g1)
                    act.wait_ge(pF.oh_used, i * BODY + (b * G + CREDIT - G))
                    nc.scalar.activation(first, msg_wide(b), ACT.Copy).then_inc(pF.part1, 1)
                    if ahead:
                        turn_copy(pF, *ahead, 1)
                        local_copies(*ahead, 0, 1)
                    act.wait_ge(pF.rest1, g1)
                    nc.scalar.activation(second, res_of(msg_wide(b)), ACT.Copy).then_inc(pF.part2, 1)
                    if ahead:
                        local_copies(*ahead, 1, NLB)

            with act.If(act.value_load(covered[0:1, 0:1], min_val=0, max_val=1)):
                nc.scalar.preload_act_table(ACT.Exp)
                for b in range(2):
                    for s in range(2):
                        turn_copy(pF, 0, b, s)
                    local_copies(0, b, 0, NLB)
                with act.Fori(0, ITERS - 1) as i:
                    edges_F(i, False, True)
                edges_F(ITERS - 1, True, True)
            with act.Else():
                with act.Fori(0, ITERS) as i:
                    edges_F(i, False, False)
            layernorm("ln4")
            stage("w1_relu", nodes(va[:, :]), acc[:, :, 0:CH], ACT.Relu, bias=col("L3_gnn_b1"))
            layernorm("ln5")
            table("fin", D, 7)

        @block.vector
        def _(dve):
            def step(ins):
                ins.then_inc(node_step, 1)

            def split(q, i, b, source, widths, between=None):
                g1 = i * 2 + (b + 1)
                first, second, third = widths(b)
                dve.wait_ge(q.part1, g1)
                nc.vector.tensor_tensor(res_of(source(b)), source(b), first, ALU.subtract).then_inc(q.rest1, 1)
                if between:
                    between()
                dve.wait_ge(q.part2, g1)
                nc.vector.tensor_tensor(third, res_of(source(b)), second, ALU.subtract).then_inc(q.part3, 1)
                dve.wait_ge(q.part3, g1)

            def onehots(q, i, b, key):
                for k in range(G):
                    onehot_tile(q, i, b * G + k, key)

            def onehot_tile(q, i, n, key):
                dve.wait_ge(q.oh_used, i * BODY + (n - 1 + CREDIT))
                nc.vector.tensor_scalar(onehot[:, n % 2, :], iota_h[:, :], key[:, bass.ds(i * BODY + n, 1)], None,
                                        ALU.is_equal).then_inc(q.oh_ready, 1)

            def both_ways(run):
                dve.wait_ge(cov_ready, 1)
                with dve.If(dve.value_load(covered[0:1, 0:1], min_val=0, max_val=1)):
                    run(onehots_win)
                with dve.Else():
                    run(lambda q, i, b: onehots(q, i, b, dst_key))

            def onehot_half(q, i, b, w):
                key = (key_a, key_b)[w]
                if w == 0:
                    dve.wait_ge(q.oh_used, i * BODY + (b * G + CREDIT - G))
                ins = nc.vector.tensor_tensor(
                    onehot_win(b, w), iota_w[:, :].unsqueeze(1).broadcast_to([P, G, WIN]),
                    key[:, bass.ds(i * BODY + b * G, G)].unsqueeze(2).broadcast_to([P, G, WIN]), ALU.is_equal)
                if w == 1:
                    ins.then_inc(q.oh_ready, 1)

            def onehots_win(q, i, b):
                for w in range(2):
                    onehot_half(q, i, b, w)

            def layernorm(n, x, relu):
                begin(dve, f"{n}_center")
                step(nc.vector.tensor_tensor(nodes(va[:, :]), nodes(x), acc[:, :, 0:CH], ALU.subtract))
                begin(dve, f"{n}_recip")
                step(nc.vector.reciprocal(vb[:, :], vb[:, :]))
                begin(dve, f"{n}_out")
                if relu:
                    step(nc.vector.scalar_tensor_tensor(out=hT[:, :], in0=va[:, :], scalar=0.0, in1=vb[:, :],
                                                        op0=ALU.max, op1=ALU.mult))
                else:
                    step(nc.vector.tensor_tensor(hT[:, :], va[:, :], vb[:, :], ALU.mult))

            def windows():
                n = [0]

                def link(ins):
                    n[0] += 1
                    ins.then_inc(win_step, 1)
                    dve.wait_ge(win_step, n[0])

                first, last, ca, cb, lim, base_a, base_b, off = (wtmp[:, j, :] for j in range(8))
                ka, kb = (v[:, 0:EC].rearrange("p (b e) -> p b e", e=P) for v in (va, vb))

                def each(x):
                    return x.unsqueeze(2).broadcast_to([P, IB, P])

                begin(dve, "win")
                link(nc.vector.tensor_scalar(ka, stage_f[:, :, :], 0.0, 2.0 * NP, ALU.is_lt, ALU.mult))
                link(nc.vector.tensor_tensor(ka, ka, stage_f[:, :, :], ALU.add))
                link(nc.vector.tensor_reduce(first, ka, AXX, ALU.min))
                link(nc.vector.tensor_reduce(last, stage_f[:, :, :], AXX, ALU.max))
                for node, chunk in ((first, ca), (last, cb)):
                    link(nc.vector.tensor_scalar(chunk, node, float(CH), None, ALU.is_ge))
                    for c in range(2, NCH):
                        link(nc.vector.scalar_tensor_tensor(out=chunk, in0=node, scalar=float(c * CH), in1=chunk,
                                                            op0=ALU.is_ge, op1=ALU.add))
                link(nc.vector.tensor_scalar(lim, ca, float(CH), float(CH - WIN), ALU.mult, ALU.add))
                link(nc.vector.tensor_tensor(base_a, first, lim, ALU.min))
                link(nc.vector.tensor_scalar(lim, cb, float(CH), None, ALU.mult))
                link(nc.vector.scalar_tensor_tensor(out=base_b, in0=last, scalar=1.0 - WIN, in1=lim,
                                                    op0=ALU.add, op1=ALU.max))
                for w, (chunk, base) in enumerate(((ca, base_a), (cb, base_b))):
                    link(nc.vector.scalar_tensor_tensor(out=off, in0=chunk, scalar=float(BPSUM - CH), in1=base,
                                                        op0=ALU.mult, op1=ALU.add))
                    link(nc.vector.tensor_copy(win_st[:, :, w], off))
                assert n[0] == WIN_OFFS
                link(nc.vector.tensor_tensor(ka, stage_f[:, :, :], each(base_a), ALU.subtract))
                link(nc.vector.tensor_scalar(kb, ka, float(WIN), FAR, ALU.is_lt, ALU.mult))
                link(nc.vector.tensor_tensor(kb, kb, stage_f[:, :, :], ALU.add))
                link(nc.vector.tensor_tensor(kb, kb, each(base_b), ALU.subtract))
                link(nc.vector.tensor_reduce(first, kb, AXX, ALU.min))
                link(nc.vector.tensor_reduce(colred[:, 0:1], first, AXX, ALU.min))
                step(nc.vector.tensor_scalar(colred[:, 0:1], colred[:, 0:1], -1.0, None, ALU.mult))
                for half, key in (("ka", key_a), ("kb", key_b)):
                    begin(dve, f"{half}_copy")
                    step(nc.vector.tensor_copy(key[:, :].rearrange("p (b e) -> p b e", e=P), acc[:, 0:IB, 0:P]))

            def groups():
                n = [0]

                def link(ins):
                    n[0] += 1
                    ins.then_inc(grp_step, 1)
                    dve.wait_ge(grp_step, n[0])

                def by_group(x):
                    return x.rearrange("p (g k) -> p g k", k=G)

                begin(dve, "grp")
                link(nc.vector.tensor_scalar(grp_dst, dstf[:, 0:TILES], 0.0, 2.0 * NP, ALU.is_lt, ALU.mult))
                link(nc.vector.tensor_tensor(grp_dst, grp_dst, dstf[:, 0:TILES], ALU.add))
                link(nc.vector.tensor_reduce(grp_ends[:, 0:NG], by_group(grp_dst), AXX, ALU.min))
                link(nc.vector.tensor_scalar(grp_ends[:, 0:NG], grp_ends[:, 0:NG], -1.0, None, ALU.mult))
                step(nc.vector.tensor_reduce(grp_ends[:, NG:], by_group(dstf[:, 0:TILES]), AXX, ALU.max))
                begin(dve, "grp_base")
                link(nc.vector.tensor_scalar(grp_base[:, :], grp_ends_all[:, 0:NG], -1.0, float(NP - P), ALU.mult, ALU.min))
                nc.vector.tensor_copy(grp_row[:, :], grp_base[0:1, :])
                span = grp_ends[:, 0:NG]
                link(nc.vector.tensor_tensor(span, grp_ends_all[:, NG:], grp_base[:, :], ALU.subtract))
                link(nc.vector.tensor_reduce(colred[:, 2:3], span, AXX, ALU.max))
                link(nc.vector.tensor_scalar(colred[:, 2:3], colred[:, 2:3], P - 0.5, None, ALU.is_le))
                nc.vector.scalar_tensor_tensor(out=covered[:, :], in0=colred[0:1, 1:2], scalar=0.0,
                                               in1=colred[0:1, 2:3], op0=ALU.is_le, op1=ALU.mult).then_inc(cov_ready, 1)
                dve.wait_ge(cov_ready, 1)
                dve.sem_inc(node_step, 1)

            def onehots_grp(before, i, b, slot):
                g1 = i * 2 + (b + 1 + before)
                nc.vector.tensor_scalar(grp_key[:, :], dst_key[:, bass.ds(i * BODY + b * G, G)],
                                        grp_base[:, bass.ds(i * 2 + b, 1)], None, ALU.subtract).then_inc(grp_keyed, 1)
                dve.wait_ge(grp_keyed, g1)
                nc.vector.tensor_tensor(onehot_grp(slot), iota_h[:, 0:P].unsqueeze(1).broadcast_to([P, G, P]),
                                        grp_key[:, :].unsqueeze(2).broadcast_to([P, G, P]), ALU.is_equal)\
                    .then_inc(grp_hot, 1)
                dve.wait_ge(grp_hot, g1)

            nc.vector.memset(tabs[:, FULL, :], 0.0).then_inc(pads_set, 1)
            nc.vector.memset(stage_i[:, :, :], -1).then_inc(pads_set, 1)
            nc.vector.memset(avg[:, :], 1.0 / D)
            nc.vector.memset(ones_bf[:, :], 1.0)
            nc.vector.memset(ones_row[:, :], 1.0)
            nc.vector.memset(zero_bf[:, :], 0.0)
            nc.vector.memset(gb[:, :, :, :], 0.0)
            nc.vector.memset(eps_col[:, :], EPS).then_inc(const_v, 1)
            begin(dve, "iota_h")
            dve.wait_ge(const_v, 1)
            nc.vector.tensor_scalar(iota_w[:, :], iota_i[:, 0:WIN], float(HALF), None, ALU.add)
            nc.vector.tensor_copy(ident_bf[:, :], ident[:, :])
            step(nc.vector.tensor_copy(iota_h[:, :], iota_i))
            begin(dve, "x_copy")
            step(nc.vector.tensor_copy(nodes(xT[:, :]), acc[:, :, 0:CH]))
            for name, array, pads, n_in in (("dst", dstf, 0.0, 1), ("src", srcf, 0.0, 2), ("w", ew[:, :], None, 3)):
                begin(dve, f"{name}_f")
                dve.wait_ge(idx_loaded, 48 * n_in)
                if name == "w":
                    step(nc.vector.memset(zacc[:, :, :], 0.0))
                else:
                    step(nc.vector.tensor_copy(stage_f[:, :, :], stage_i[:, :, :]))
                    if name == "dst":
                        dve.wait_ge(node_step, AT["dst_f"])
                        nc.vector.memset(stage_i[:, :, :], 0).then_inc(pads_set, 1)
                begin(dve, f"{name}_copy")
                step(nc.vector.tensor_copy(array.rearrange("p (b e) -> p b e", e=P), acc[:, 0:IB, 0:P]))
                if name == "src":
                    nc.vector.memset(stage_f[:, :, :], 0.0).then_inc(pads_set, 1)
                if name == "dst":
                    windows()
            begin(dve, "keys")
            nc.vector.tensor_scalar(dst_key[:, :], dstf[:, 0:TILES], -float(HALF), None, ALU.add)
            nc.vector.tensor_scalar(src_key[:, :], srcf[:, 0:TILES], -float(HALF), None, ALU.add)
            nc.vector.tensor_scalar(dst_idx[:, :], dstf[:, 0:TILES], 0.0, None, ALU.max)
            nc.vector.tensor_copy(src_idx[:, :], srcf[:, 0:TILES])
            step(nc.vector.tensor_scalar(padneg[:, :], dstf[:, TILES - 1:TILES], 0.0, -BIG, ALU.is_lt, ALU.mult))
            groups()
            begin(dve, "wT_copy")
            nc.vector.tensor_copy(attT[:, :], small[0:O0, 0:2 * H0])
            step(nc.vector.tensor_copy(w0T[:, :], small[:, 64:64 + O0]))
            layernorm("ln0", xT[:, :], True)

            def low_and_block():
                n = [0]

                def link(ins):
                    n[0] += 1
                    ins.then_inc(block_step, 1)
                    dve.wait_ge(block_step, n[0])

                link(nc.vector.tensor_scalar(src_blk, src_idx[:, :], float(NB), None, ALU.is_ge))
                for j in range(2, NBLK):
                    link(nc.vector.scalar_tensor_tensor(out=src_blk, in0=src_idx[:, :], scalar=float(j * NB),
                                                        in1=src_blk, op0=ALU.is_ge, op1=ALU.add))
                link(nc.vector.scalar_tensor_tensor(out=src_low, in0=src_blk, scalar=-float(NB), in1=src_key[:, :],
                                                    op0=ALU.mult, op1=ALU.add))

            low_and_block()
            begin(dve, "passA")

            def edges_A():
                with dve.Fori(0, ITERS) as i:
                    for b in range(2):
                        onehots_grp(GRP_A, i, b, 2)
                        onehots_win(pA, i, b)
                        dve.wait_ge(pA.gathered[b], pA.have_rows(i))
                        dve.wait_ge(pA.local, i * 2 + (b + 1))
                        dve.nop(nofuse=True)
                        nc.vector.tensor_tensor(e4h_at(i * BODY + b * G), ga[:, b, :, 0:H0], heads(small[:, 0:G * H0]),
                                                ALU.add).then_inc(pA.taken, 1)

            def edges_A_all():
                with dve.Fori(0, ITERS) as i:
                    for b in range(2):
                        dve.wait_ge(pA.gathered[b], pA.have_rows(i, 2))
                        dve.nop(nofuse=True)
                        nc.vector.tensor_tensor(e4h_at(i * BODY + b * G), ga[:, b, :, 0:H0], gb[:, b, :, H0:2 * H0],
                                                ALU.add).then_inc(pA.taken, 1)
                        onehots(pA, i, b, dst_key)

            dve.wait_ge(cov_ready, 1)
            with dve.If(dve.value_load(covered[0:1, 0:1], min_val=0, max_val=1)):
                edges_A()
            with dve.Else():
                edges_A_all()
            begin(dve, "logit_pad")
            step(nc.vector.tensor_scalar(e4[:, (TILES - 1) * H0:], e4[:, (TILES - 1) * H0:], padneg[:, 0:1], None, ALU.add))
            begin(dve, "logit_leaky")
            step(nc.vector.scalar_tensor_tensor(out=e4, in0=e4, scalar=0.2, in1=e4, op0=ALU.mult, op1=ALU.max))
            begin(dve, "logit_max")
            step(nc.vector.tensor_reduce(colred[:, 0:1], e4, AXX, ALU.max))
            begin(dve, "logit_neg")
            step(nc.vector.tensor_scalar(colred[:, 2:3], colred[:, 1:2], -1.0, None, ALU.mult))
            begin(dve, "exp_r1")
            step(nc.vector.tensor_tensor(lkh, e4h, exp_parts[:, :, 0:H0], ALU.subtract))
            begin(dve, "exp_b3")
            step(nc.vector.tensor_tensor(exp_parts[:, :, 2 * H0:3 * H0], lkh, exp_parts[:, :, H0:2 * H0], ALU.subtract))

            begin(dve, "passB")
            with dve.Fori(0, ITERS) as i:
                for b in range(2):
                    g1 = i * 2 + (b + 1)
                    first = i * BODY + b * G
                    dve.wait_ge(pB.oh_used, i * 2 + (b + 1))
                    dve.nop(nofuse=True)
                    nc.vector.tensor_tensor(onehot_of_blk, iota_w[:, 0:NBLK].unsqueeze(1).broadcast_to([P, G, NBLK]),
                                            src_blk[:, bass.ds(first, G)].unsqueeze(2).broadcast_to([P, G, NBLK]),
                                            ALU.is_equal).then_inc(pB.part3, 1)
                    nc.vector.tensor_tensor(onehot_low(b), iota_h[:, 0:NB].unsqueeze(1).broadcast_to([P, G, NB]),
                                            src_low[:, bass.ds(first, G)].unsqueeze(2).broadcast_to([P, G, NB]),
                                            ALU.is_equal)
                    dve.wait_ge(pB.part3, g1)
                    dve.nop(nofuse=True)
                    nc.vector.tensor_tensor(
                        exp_by_block(b), onehot_of_blk.unsqueeze(3).broadcast_to([P, G, NBLK, 3 * H0]),
                        exp_parts[:, bass.ds(first, G), :].unsqueeze(2).broadcast_to([P, G, NBLK, 3 * H0]),
                        ALU.mult).then_inc(pB.oh_ready, 1)
                    dve.wait_ge(pB.oh_ready, g1)
            den_parts = acc[0:NB, 0, 0:NBLK * 3 * H0].rearrange("p (j s h) -> p j s h", s=3, h=H0)
            den = tabs[:, :, O0:O0 + H0]
            begin(dve, "den_1")
            step(nc.vector.tensor_copy(den, den_parts[:, :, 0, :]))
            begin(dve, "den_2")
            step(nc.vector.tensor_tensor(den, den, den_parts[:, :, 1, :], ALU.add))
            begin(dve, "den_3")
            step(nc.vector.scalar_tensor_tensor(out=den, in0=den_parts[:, :, 2, :], scalar=1e-16, in1=den,
                                                op0=ALU.add, op1=ALU.add))
            begin(dve, "den_recip")
            step(nc.vector.reciprocal(tabs[:, :, O0:O0 + H0], tabs[:, :, O0:O0 + H0]))

            begin(dve, "passC")

            def edges_C(targets):
                with dve.Fori(0, ITERS) as i:
                    for b in range(2):
                        g1 = i * 2 + (b + 1)
                        dve.wait_ge(pC.gathered[b], pC.have_rows(i))
                        dve.nop(nofuse=True)
                        nc.vector.tensor_tensor(alpha[:, :].rearrange("p (k h) -> p k h", h=H0), e4h_at(i * BODY + b * G),
                                                ga[:, b, :, O0:O0 + H0], ALU.mult).then_inc(pC.weight, 1)
                        dve.wait_ge(pC.weight, g1)
                        dve.nop(nofuse=True)
                        nc.vector.tensor_tensor(
                            msg[:, :].rearrange("p (k h o) -> p k h o", h=H0, o=O0),
                            ga[:, b, :, 0:O0].unsqueeze(2).broadcast_to([P, G, H0, O0]),
                            alpha[:, :].rearrange("p (k h) -> p k h", h=H0).unsqueeze(3).broadcast_to([P, G, H0, O0]),
                            ALU.mult).then_inc(pC.msg, 1)
                        dve.wait_ge(pC.msg, g1)
                        dve.sem_inc(pC.taken, 1)
                        split(pC, i, b, msg_wide, parts_wide)
                        targets(pC, i, b)

            both_ways(edges_C)
            begin(dve, "x1")
            step(nc.vector.tensor_tensor(nodes(xT[:, :]), nodes(xT[:, :]), acc[:, :, 0:CH], ALU.add))
            layernorm("ln1", xT[:, :], True)

            assert NBLK <= ITERS
            placed = [0]

            def link(ins):
                placed[0] += 1
                ins.then_inc(place_step, 1)
                dve.wait_ge(place_step, placed[0])

            link(nc.vector.tensor_scalar(blk_of, src_idx[:, :], float(NB), None, ALU.is_ge))
            for j in range(2, NBLK):
                link(nc.vector.scalar_tensor_tensor(out=blk_of, in0=src_idx[:, :], scalar=float(j * NB), in1=blk_of,
                                                    op0=ALU.is_ge, op1=ALU.add))
            link(nc.vector.tensor_scalar(blk_of, blk_of, -float(HALF), None, ALU.add))
            nc.vector.memset(place_f, 1.0)
            link(nc.vector.memset(rank, 0.0))
            RANKED = placed[0]

            def rank_block(i):
                def link(step, ins):
                    ins.then_inc(place_step, 1)
                    dve.wait_ge(place_step, i * 4 + (RANKED + step))

                link(1, nc.vector.tensor_scalar(mask, blk_of, iota_h[:, bass.ds(i, 1)], None, ALU.is_equal))
                link(2, nc.vector.tensor_tensor_scan(sums, place_f, mask, 0.0, ALU.mult, ALU.add))
                dve.nop(nofuse=True)
                nc.vector.tensor_copy(counts[:, bass.ds(i, 1)], sums[:, TILES - 1:TILES])
                link(3, nc.vector.tensor_tensor(mask, mask, sums, ALU.mult))
                link(4, nc.vector.tensor_tensor(rank, rank, mask, ALU.add))

            begin(dve, "passD")

            def edges_D(targets):
                with dve.Fori(0, ITERS) as i:
                    for b in range(2):
                        g1 = i * 2 + (b + 1)
                        first, second, third = parts_wide(b)
                        dve.wait_ge(pD.part1, g1)
                        nc.vector.tensor_tensor(res_of(msg_wide(b)), ga[:, b, :, 0:D], first, ALU.subtract)\
                            .then_inc(pD.rest1, 1)
                        dve.wait_ge(pD.part2, g1)
                        dve.sem_inc(pD.taken, 1)
                        nc.vector.tensor_tensor(third, res_of(msg_wide(b)), second, ALU.subtract).then_inc(pD.part3, 1)
                        dve.wait_ge(pD.part3, g1)
                        targets(pD, i, b)
                    rank_block(i)

            both_ways(edges_D)
            begin(dve, "mean_max")
            step(nc.vector.tensor_scalar(cnt[:, :], cnt[:, :], 1.0, None, ALU.max))
            begin(dve, "mean_recip")
            step(nc.vector.reciprocal(cnt[:, :], cnt[:, :]))
            begin(dve, "mean_mul")
            step(nc.vector.tensor_tensor(nodes(va[:, :]), nodes(cnt[:, :]), acc[:, :, 0:CH], ALU.mult))
            begin(dve, "x2")
            step(nc.vector.tensor_tensor(xT[:, :], xT[:, :], va[:, :], ALU.add))
            layernorm("ln2", xT[:, :], True)

            begin(dve, "pair_zero")
            nc.vector.memset(w_f1_pairs, 0.0)
            step(nc.vector.memset(w_f2_pair, 0.0))
            placed[0] += 4 * ITERS
            begin(dve, "counts")
            step(nc.vector.tensor_scalar(place_f, rank, -1.0, None, ALU.add))
            begin(dve, "places")
            link(nc.vector.tensor_scalar(total, small[:, P:P + NBLK], float(D), None, ALU.mult))
            link(nc.vector.memset(mask_off[:, 0:NBLK], 1.0))
            link(nc.vector.tensor_tensor_scan(first_of, mask_off[:, 0:NBLK], total, 0.0, ALU.mult, ALU.add))
            link(nc.vector.tensor_tensor(first_of, first_of, total, ALU.subtract))
            link(nc.vector.tensor_tensor(offs, first_of, small[:, 0:NBLK], ALU.add))
            for j in range(NBLK):
                link(nc.vector.tensor_scalar(mask_off, blk_of, float(j - HALF), offs[:, j:j + 1], ALU.is_equal, ALU.mult))
                link(nc.vector.tensor_tensor(place_f, place_f, mask_off, ALU.add))
            link(nc.vector.tensor_copy(place_i, place_f))
            link(nc.vector.tensor_reduce(colred[:, 0:1], total[:, 1:NBLK - 1], AXX, ALU.min))
            link(nc.vector.tensor_scalar(covered_s[:, :], colred[0:1, 0:1], GE - 1.5, None, ALU.is_ge))
            for blk, at_place in ((blk_a, 0), (blk_b, GE - 1)):
                link(nc.vector.tensor_scalar(glim, iota_h[:, 0:NG], float(HALF), float(GE), ALU.add, ALU.mult))
                if at_place:
                    link(nc.vector.tensor_scalar(glim, glim, float(at_place), None, ALU.add))
                link(nc.vector.tensor_scalar(blk, glim, first_of[:, 1:2], None, ALU.is_ge))
                for j in range(2, NBLK):
                    link(nc.vector.scalar_tensor_tensor(out=blk, in0=glim, scalar=first_of[:, j:j + 1], in1=blk,
                                                        op0=ALU.is_ge, op1=ALU.add))
            for w, blk in enumerate((blk_a, blk_b)):
                link(nc.vector.tensor_scalar(blk_ch, blk, float(BPC), None, ALU.is_ge))
                for c in range(2, NCH):
                    link(nc.vector.scalar_tensor_tensor(out=blk_ch, in0=blk, scalar=float(c * BPC), in1=blk_ch,
                                                        op0=ALU.is_ge, op1=ALU.add))
                link(nc.vector.tensor_scalar(blk_off, blk, float(NB), None, ALU.mult))
                link(nc.vector.scalar_tensor_tensor(out=blk_off, in0=blk_ch, scalar=float(BPSUM - CH), in1=blk_off,
                                                    op0=ALU.mult, op1=ALU.add))
                link(nc.vector.tensor_copy(blk_offs[:, :].rearrange("o (g w) -> o g w", w=2)[:, :, w], blk_off[0:1, :]))
            link(nc.vector.tensor_scalar(base_sa, blk_a, float(NB), None, ALU.mult))
            link(nc.vector.tensor_tensor(base_sb, blk_a, blk_b, ALU.is_equal))
            link(nc.vector.tensor_scalar(base_sb, base_sb, 4.0 * NBLK, None, ALU.mult))
            link(nc.vector.tensor_tensor(base_sb, base_sb, blk_b, ALU.add))
            step(nc.vector.tensor_scalar(base_sb, base_sb, float(NB), None, ALU.mult))

            begin(dve, "filters")

            def messages(i, first, last, local):
                for b in range(2):
                    if not first:
                        dve.wait_ge(rows_sent[b], i * (16 * G))
                        dve.nop(nofuse=True)
                    nc.vector.tensor_copy(mrows[:, b, :, F2], src_key[:, bass.ds(i * BODY + b * G, G)])
                    for s, (k0, kn) in enumerate(SUBS):
                        n1 = i * (2 * NSUB) + (b * NSUB + s + 1)
                        dve.wait_ge(flt_ln, n1)
                        nc.vector.scalar_tensor_tensor(
                            out=hidden_of(hid[s % 2], kn), in0=hidden_of(hid_r[s % 2], kn), scalar=-LOG2,
                            in1=hidden_of(hid_e[s % 2], kn), op0=ALU.add, op1=ALU.add).then_inc(flt_hid, 1)
                        if local and s == 1 and not (last and b == 1):
                            onehots_grp(GRP_M, i + b, 1 - b, 1 - b)
                        if s == 0 and not local:
                            dve.wait_ge(pM.gathered[b], pM.have_rows(i))
                        dve.wait_ge(flt_W, n1)
                        dve.nop(nofuse=True)
                        if local:
                            def by_tile(x):
                                return x.rearrange("p (k f) -> p k f", f=F2)

                            rows = mrows[:, b, k0:k0 + kn, 0:F2]
                            nc.vector.tensor_tensor(
                                rows, by_tile(small[:, s % 2 * SUB * F2:(s % 2 * SUB + kn) * F2]),
                                ew[:, bass.ds(i * BODY + (b * G + k0), kn)].unsqueeze(2).broadcast_to([P, kn, F2]),
                                ALU.mult).then_inc(flt_weighted, 1)
                            dve.wait_ge(flt_weighted, n1 + 1)
                            nc.vector.tensor_tensor(rows, rows, by_tile(acc[:, 4 + s % 2, 0:kn * F2]), ALU.mult)\
                                .then_inc(flt_m, 1)
                            continue
                        for j in range(kn):
                            k = k0 + j
                            ins = nc.vector.scalar_tensor_tensor(
                                out=mrows[:, b, k, 0:F2], in0=acc[:, 4 + s % 2, j * F2:(j + 1) * F2],
                                scalar=ew[:, bass.ds(i * BODY + (b * G + k), 1)], in1=ga[:, b, k, 0:F2],
                                op0=ALU.mult, op1=ALU.mult)
                        ins.then_inc(flt_m, 1)
                    dve.wait_ge(flt_m, i * (2 * NSUB) + (b + 1) * NSUB)
                    dve.sem_inc(rows_made, 1)
                    dve.sem_inc(pM.taken, 1)

            def all_messages(local):
                if local:
                    dve.sem_inc(flt_weighted, 1)
                    onehots_grp(GRP_M, 0, 0, 0)
                messages(0, True, False, local)
                with dve.Fori(1, ITERS - 1) as i:
                    messages(i, False, False, local)
                messages(ITERS - 1, False, True, local)

            with dve.If(dve.value_load(covered[0:1, 0:1], min_val=0, max_val=1)):
                all_messages(True)
            with dve.Else():
                all_messages(False)
            dve.wait_ge(rows_made, 2 * ITERS)
            dve.sem_inc(node_step, 1)

            begin(dve, "passE")

            def parts_E(i, b):
                g1 = i * 2 + (b + 1)
                first, second, third = parts_narrow(b)
                dve.wait_ge(pE.part1, g1)
                nc.vector.tensor_tensor(res_of(msg_narrow(b)), msg_narrow(b), first, ALU.subtract)\
                    .then_inc(pE.rest1, 1)
                dve.wait_ge(pE.part2, g1)
                nc.vector.tensor_tensor(third, res_of(msg_narrow(b)), second, ALU.subtract).then_inc(pE.part3, 1)
                dve.wait_ge(pE.part3, g1)

            def edges_E():
                with dve.Fori(0, ITERS) as i:
                    for b in range(2):
                        dve.wait_ge(pE.gathered[b], (i + 1) * 16)
                        for w, base in enumerate((base_sa, base_sb)):
                            ins = nc.vector.tensor_scalar(key_s[:, w, :], srows[:, b, :, F2],
                                                          base[:, bass.ds(i * 2 + b, 1)], None, ALU.subtract)
                        ins.then_inc(keys_made, 1)
                        dve.wait_ge(keys_made, i * 2 + (b + 1))
                        dve.wait_ge(pE.oh_used, i * BODY + (b * G + CREDIT - G))
                        for w in range(2):
                            ins = nc.vector.tensor_tensor(
                                onehot_blks(b, w), iota_h[:, 0:NB].unsqueeze(1).broadcast_to([P, G, NB]),
                                key_s[:, w, :].unsqueeze(2).broadcast_to([P, G, NB]), ALU.is_equal)
                        ins.then_inc(pE.oh_ready, 1)
                        parts_E(i, b)
                        dve.sem_inc(pE.taken, 1)

            def edges_E_all():
                with dve.Fori(0, ITERS) as i:
                    for b in range(2):
                        dve.wait_ge(pE.gathered[b], (i + 1) * 16)
                        parts_E(i, b)
                        for k in range(G):
                            n = b * G + k
                            dve.wait_ge(pE.oh_used, i * BODY + (n - 1 + CREDIT))
                            ins = nc.vector.tensor_scalar(onehot[:, n % 2, :], iota_h[:, :], srows[:, b, k, F2:F2 + 1],
                                                          None, ALU.is_equal).then_inc(pE.oh_ready, 1)
                        dve.wait_ge(pE.oh_ready, i * BODY + (b + 1) * G)
                        dve.sem_inc(pE.taken, 1)

            with dve.If(dve.value_load(covered_s[0:1, 0:1], min_val=0, max_val=1)):
                edges_E()
            with dve.Else():
                edges_E_all()
            begin(dve, "o1_sum")
            step(nc.vector.scalar_tensor_tensor(out=va[:, :], in0=va[:, :], scalar=-LOG2, in1=vb[:, :],
                                                op0=ALU.add, op1=ALU.add))
            begin(dve, "x3")
            step(nc.vector.scalar_tensor_tensor(out=nodes(xT[:, :]), in0=acc[:, :, 0:CH], scalar=col("L2_gnn_b_o2"),
                                                in1=nodes(xT[:, :]), op0=ALU.add, op1=ALU.add))
            layernorm("ln3", xT[:, :], True)

            begin(dve, "passF")

            def products(i, b, local):
                dve.wait_ge(pF.gathered[b], pF.have_rows(i, 1 if local else 2))
                if local:
                    dve.wait_ge(local_sb, i * len(BODY_LOCALS) + ((b + 1) * NLB + 1))
                nc.vector.tensor_tensor(msg[:, :].rearrange("p (k f) -> p k f", f=D), gb[:, b, :, :],
                                        ga[:, b, :, 0:D], ALU.mult).then_inc(pF.score[0], 1)
                dve.wait_ge(pF.score[0], i * 2 + (b + 1))

            def edges_F(i, last, local):
                for b in range(2):
                    g1 = i * 2 + (b + 1)
                    products(i, b, local)
                    nc.vector.tensor_reduce(sc[:, :, :].rearrange("p k h -> p (k h)"),
                                            msg[:, :].rearrange("p (k f) -> p k f", f=HD), AXX, ALU.add)\
                        .then_inc(pF.score[1], 1)
                    dve.wait_ge(pF.score[1], g1)
                    nc.vector.tensor_scalar(sc[:, :, :], sc[:, :, :], 1.0 / math.sqrt(HD), 5.0, ALU.mult, ALU.min)\
                        .then_inc(pF.score[2], 1)
                    dve.wait_ge(pF.score[2], g1)
                    nc.vector.tensor_scalar(sc[:, :, :], sc[:, :, :], -5.0, None, ALU.max).then_inc(pF.score[3], 1)
                    if local and not last:
                        dve.wait_ge(pF.turned, i * 4 + (b * 2 + 4))
                        onehots_grp(GRP_F, i + 1, b, 2)
                    dve.wait_ge(pF.weight, g1)
                    nc.vector.tensor_tensor(
                        msg[:, :].rearrange("p (k h o) -> p k h o", h=NH, o=HD),
                        ga[:, b, :, D:2 * D].rearrange("p k (h o) -> p k h o", o=HD),
                        ex[:, :, :].unsqueeze(3).broadcast_to([P, G, NH, HD]), ALU.mult).then_inc(pF.msg, 1)
                    nc.vector.scalar_tensor_tensor(
                        out=exv[:, :, :],
                        in0=dst_key[:, bass.ds(i * BODY + b * G, G)].unsqueeze(2).broadcast_to([P, G, NH]),
                        scalar=-HALF - 0.5, in1=ex[:, :, :], op0=ALU.is_gt, op1=ALU.mult).then_inc(z_part, 1)
                    if local:
                        onehot_half(pF, i, b, 0)
                    dve.wait_ge(z_part, g1)
                    nc.vector.tensor_tensor(zacc[:, :, :], zacc[:, :, :], exv[:, :, :], ALU.add).then_inc(z_ready, 1)
                    dve.wait_ge(pF.msg, g1)
                    dve.sem_inc(pF.taken, 1)
                    split(pF, i, b, msg_wide, parts_wide, (lambda: onehot_half(pF, i, b, 1)) if local else None)
                    if not local:
                        onehots(pF, i, b, dst_key)

            with dve.If(dve.value_load(covered[0:1, 0:1], min_val=0, max_val=1)):
                onehots_grp(GRP_F, 0, 0, 2)
                dve.wait_ge(pF.turned, 2)
                onehots_grp(GRP_F, 0, 1, 2)
                with dve.Fori(0, ITERS - 1) as i:
                    edges_F(i, False, True)
                edges_F(ITERS - 1, True, True)
            with dve.Else():
                with dve.Fori(0, ITERS) as i:
                    edges_F(i, False, False)
            begin(dve, "z_sum")
            dve.wait_ge(z_ready, 2 * ITERS)
            step(nc.vector.tensor_reduce(zsum[:, :], zacc[:, :, :].rearrange("p k h -> p h k"), AXX, ALU.add))
            begin(dve, "z_recip")
            step(nc.vector.reciprocal(zrec[:, :], zall[:, :]))
            begin(dve, "z_head")
            step(nc.vector.tensor_tensor(zhm[:, :], headm[:, :], zrec[:, :], ALU.mult))
            begin(dve, "z_red")
            step(nc.vector.tensor_reduce(colred[:, 3:4], zhm[:, :], AXX, ALU.add))
            begin(dve, "att_cp")
            step(nc.vector.tensor_scalar(nodes(va[:, :]), acc[:, :, 0:CH], colred[:, 3:4], None, ALU.mult))
            begin(dve, "wo_add")
            step(nc.vector.scalar_tensor_tensor(out=nodes(hT[:, :]), in0=acc[:, :, 0:CH], scalar=col("L3_gnn_bO"),
                                                in1=nodes(hT[:, :]), op0=ALU.add, op1=ALU.add))
            layernorm("ln4", hT[:, :], False)
            begin(dve, "g1")
            step(nc.vector.tensor_scalar(hT[:, :], hT[:, :], col("L3_gnn_ln1_g"), col("L3_gnn_ln1_b"), ALU.mult, ALU.add))
            begin(dve, "w2_add")
            step(nc.vector.scalar_tensor_tensor(out=nodes(hT[:, :]), in0=acc[:, :, 0:CH], scalar=col("L3_gnn_b2"),
                                                in1=nodes(hT[:, :]), op0=ALU.add, op1=ALU.add))
            layernorm("ln5", hT[:, :], False)
            begin(dve, "g2")
            step(nc.vector.tensor_scalar(hT[:, :], hT[:, :], col("L3_gnn_ln2_g"), col("L3_gnn_ln2_b"), ALU.mult, ALU.add))
            begin(dve, "x4")
            step(nc.vector.tensor_tensor(xT[:, :], xT[:, :], hT[:, :], ALU.add))

        @block.tensor
        def _(pe):
            mm = nc.tensor.matmul
            acc_row = acc[:, :, :].rearrange("p c n -> p (c n)")

            def dense(name, w, x):
                begin(pe, name)
                for c in range(NCH):
                    ins = mm(acc[0:w.shape[1], c, 0:CH], w, x[:, c * CH:(c + 1) * CH], start=True, stop=True)
                ins.then_inc(node_step, 1)

            def layernorm(n, x):
                dense(f"{n}_mean", avg[:, :], x)
                dense(f"{n}_var", avg[:, :], vb[:, :])

            def table(n, x, w, bias=None):
                for r in range(LASTQ + 1):
                    begin(pe, f"{n}_mm{r}")
                    for j in range(NCH):
                        xb = x[:, (r * NCH + j) * NB:(r * NCH + j + 1) * NB]
                        if w is None:
                            ins = nc.tensor.transpose(acc[0:NB, j, 0:D], xb, ident[:, :])
                            continue
                        o = acc[0:NB, j, 0:w.shape[1]]
                        if bias is not None:
                            mm(o, ones_row[0:1, 0:NB], bias, start=True, stop=False)
                        ins = mm(o, xb, w, start=bias is None, stop=True)
                    ins.then_inc(node_step, 1)

            def open_acc(rows_out):
                for c in range(NCH):
                    mm(acc[0:rows_out, c, 0:CH], zero_bf[:, 0:rows_out], zero_bf[:, :], start=True, stop=False)

            def close_acc(rows_out):
                for c in range(NCH):
                    ins = mm(acc[0:rows_out, c, 0:CH], zero_bf[:, 0:rows_out], zero_bf[:, :], start=False, stop=True)
                ins.then_inc(node_step, 1)

            def scatter_tile(q, stationaries, i, b, k):
                n = b * G + k
                pe.wait_ge(q.oh_ready, i * BODY + (n + 1))
                for st in stationaries(b, k):
                    for c in range(NCH):
                        ins = mm(acc[0:st.shape[1], c, 0:CH], st, onehot[:, n % 2, c * CH:(c + 1) * CH],
                                 start=False, stop=False)
                ins.then_inc(q.oh_used, 1)

            def all_nodes(q, stationaries):
                with pe.Fori(0, ITERS) as i:
                    for b in range(2):
                        if stationaries is not counting:
                            pe.wait_ge(q.part3, i * 2 + (b + 1))
                        for k in range(G):
                            scatter_tile(q, stationaries, i, b, k)

            def window_offsets(i, b):
                _, offs = nc.values_load_multi_w_load_instructions(
                    win_off[0:1, bass.ds((i * BODY + b * G) * 2, 2 * G)], engines=[PE_ENGINE],
                    min_val=0, max_val=NCH * BPSUM - WIN,
                    skip_runtime_bounds_check_because="windows() keeps them in the tile's chunk")
                return offs

            def scatter_windows(q, stationaries, i, b, offs):
                for k in range(G):
                    for st in stationaries(b, k):
                        for w in range(2):
                            ins = mm(acc_row[0:st.shape[1], bass.ds(offs[2 * k + w], WIN)], st,
                                     onehot_win(b, w)[:, k, :], start=False, stop=False)
                ins.then_inc(q.oh_used, G)

            def in_windows(q, stationaries):
                with pe.Fori(0, ITERS) as i:
                    for b in range(2):
                        offs = window_offsets(i, b)
                        pe.wait_ge(q.part3, i * 2 + (b + 1))
                        pe.wait_ge(q.oh_ready, i * 2 + (b + 1))
                        scatter_windows(q, stationaries, i, b, offs)

            def turn(q, before, i, b):
                pe.wait_ge(grp_hot, i * 2 + (b + 1 + before))
                for s, (k0, k1) in enumerate(((0, WB), (WB, G))):
                    if s == 1:
                        pe.wait_ge(q.turned_sb, i * 4 + (b * 2 + 1))
                    for k in range(k0, k1):
                        ins = nc.tensor.transpose(small_bf()[:, (k - k0) * P:(k - k0 + 1) * P],
                                                  onehot_grp(2)[:, k, :], ident_bf[:, :])
                    ins.then_inc(q.turned, 1)

            def counting(b, k):
                return [ones_bf[:, :]]

            def windows_A():
                pe.sem_inc(pA.rows_used, 2)
                with pe.Fori(0, ITERS) as i:
                    for b in range(2):
                        offs = window_offsets(i, b)
                        pe.wait_ge(pA.taken, i * 2 + (b + 2))
                        turn(pA, GRP_A, i, b)
                        pe.wait_ge(pA.turned_sb, i * 4 + (b * 2 + 2))
                        pe.wait_ge(pA.rows_in[b], (i + 1) * 16)
                        for k in range(G):
                            ins = mm(small[:, k * H0:(k + 1) * H0], ohT[:, k * P:(k + 1) * P],
                                     win_rows(b, 0, H0), start=True, stop=True)
                        ins.then_inc(pA.local, 1)
                        pe.wait_ge(pA.local, i * 2 + (b + 1))
                        pe.sem_inc(pA.rows_used, 1)
                        pe.wait_ge(pA.oh_ready, i * 2 + (b + 1))
                        scatter_windows(pA, counting, i, b, offs)
                pe.wait_ge(pA.taken, ITERS * 2 + 2)

            def windows_F():
                def q_of_dst(i, b):
                    pe.wait_ge(local_sb, i * len(BODY_LOCALS) + (b * NLB + 1))
                    turn(pF, GRP_F, i, b)
                    pe.wait_ge(pF.turned_sb, i * 4 + (b * 2 + 2))
                    pe.wait_ge(pF.rows_in[b], (i + 1) * 16)
                    for n, (b_, k0, kn) in enumerate(BODY_LOCALS):
                        if b_ != b:
                            continue
                        pe.wait_ge(local_sb, i * len(BODY_LOCALS) + (n + 1))
                        for k in range(k0, k0 + kn):
                            ins = mm(local_q(LB)[:, (k - k0) * D:(k - k0 + 1) * D], ohT[:, k * P:(k + 1) * P],
                                     win_rows_q(b), start=True, stop=True)
                        ins.then_inc(pF.local, 1)
                    pe.wait_ge(pF.local, i * len(BODY_LOCALS) + (b + 1) * NLB)
                    pe.sem_inc(pF.rows_used, 1)

                def edges_F(i, last):
                    for b in range(2):
                        if not last:
                            q_of_dst(i + 1, b)
                        offs = window_offsets(i, b)
                        pe.wait_ge(pF.oh_ready, i * 2 + (b + 1))
                        pe.wait_ge(pF.part3, i * 2 + (b + 1))
                        scatter_windows(pF, wide, i, b, offs)

                pe.sem_inc(pF.rows_used, 2)
                pe.sem_inc(local_sb, 1)
                for b in range(2):
                    q_of_dst(0, b)
                with pe.Fori(0, ITERS - 1) as i:
                    edges_F(i, False)
                edges_F(ITERS - 1, True)

            def scatter(name, stationaries, q, windows):
                begin(pe, name)
                open_acc(P)
                pe.wait_ge(cov_ready, 1)
                pe.wait_ge(win_dma, 32)
                pe.sem_inc(q.oh_used, CREDIT)
                with pe.If(pe.value_load(covered[0:1, 0:1], min_val=0, max_val=1)):
                    windows()
                with pe.Else():
                    all_nodes(q, stationaries)
                close_acc(P)

            def wide(b, k):
                return [parts[:, b, s, k * D:(k + 1) * D] for s in range(3)]

            def narrow(b, k):
                return [parts[:, b, 0, k * D:(k + 1) * D], parts[:, b, 1, k * F2:(k + 1) * F2]]

            begin(pe, "x_T")
            pe.wait_ge(loaded, LOADED)
            for blk in range(NBLK):
                j = blk % BPC
                ins = nc.tensor.transpose(acc[:, blk // BPC, j * NB:(j + 1) * NB], tabs[:, blk, :], ident[0:NB, 0:NB])
            ins.then_inc(node_step, 1)
            for name, staged in (("dst_T", stage_f), ("ka_T", va), ("kb_T", vb), ("src_T", stage_f), ("w_T", stage_f)):
                begin(pe, name)
                if staged is not stage_f:
                    staged = staged[:, 0:EC].rearrange("p (b e) -> p b e", e=P)
                for j in range(IB):
                    ins = nc.tensor.transpose(acc[:, j, 0:P], staged[:, j, :], ident[:, :])
                ins.then_inc(node_step, 1)
            begin(pe, "wT_T")
            nc.tensor.transpose(small[0:O0, 0:2 * H0], att[:, :], ident[0:2 * H0, 0:2 * H0])
            nc.tensor.transpose(small[:, 64:64 + O0], w0[:, :], ident[0:O0, 0:O0]).then_inc(node_step, 1)

            layernorm("ln0", xT)
            dense("whT_mm", w0T[:, :], hT)
            table("ta", va[0:O0, :], attT[:, :])
            table("tw", hT, w0T[:, :], ROW["L0_gnn_b"])
            scatter("passA", counting, pA, windows_A)

            begin(pe, "passB")
            den_acc = acc[0:NB, 0, 0:NBLK * 3 * H0]
            mm(den_acc, zero_bf[:, 0:NB], zero_bf[:, 0:NBLK * 3 * H0], start=True, stop=False)
            pe.sem_inc(pB.oh_used, 2)
            with pe.Fori(0, ITERS) as i:
                for b in range(2):
                    pe.wait_ge(pB.oh_ready, i * 2 + (b + 1))
                    for k in range(G):
                        ins = mm(den_acc, onehot_low(b)[:, k, :], exp_by_block(b)[:, k, :, :].rearrange("p j s -> p (j s)"),
                                 start=False, stop=False)
                    ins.then_inc(pB.oh_used, 1)
            mm(den_acc, zero_bf[:, 0:NB], zero_bf[:, 0:NBLK * 3 * H0], start=False, stop=True).then_inc(node_step, 1)
            scatter("passC", wide, pC, lambda: in_windows(pC, wide))
            layernorm("ln1", xT)
            table("th", hT, None)
            scatter("passD", wide, pD, lambda: in_windows(pD, wide))
            layernorm("ln2", xT)
            table("t2", hT, w_in[:, :], ROW["L2_gnn_b_in"])

            begin(pe, "counts_mm")
            mm(small[:, 0:NBLK], before, counts[:, 0:NBLK], start=True, stop=True)
            mm(small[:, P:P + NBLK], avg[:, :], counts[:, 0:NBLK], start=True, stop=True).then_inc(node_step, 1)

            def attr_T(i, n, local):
                i, (b, s, k0, kn) = sub_at(i, n)
                if s == 0:
                    pe.wait_ge(attr_in[b], (i + 1) * (16 * (b + 1)))
                    if local:
                        pe.wait_ge(grp_hot, i * 2 + (b + 1 + GRP_M))
                if local:
                    for j in range(kn):
                        nc.tensor.transpose(turned_m(n % 2)[:, j * P:(j + 1) * P], onehot_grp(b)[:, k0 + j, :],
                                            ident_bf[:, :])
                nc.tensor.transpose(acc[0:kn * R, n % 2, 0:P], attrs[:, b, k0 * R:(k0 + kn) * R], ident[:, :])\
                    .then_inc(flt_T, 1)

            def attr_hidden(i, n):
                n1 = i * len(BODY_SUBS) + (n + 1)
                i, (b, s, k0, kn) = sub_at(i, n)
                pe.wait_ge(flt_Tc, n1)
                if s == NSUB - 1:
                    pe.sem_inc(attr_used, 1)
                for j, c in pairs(kn):
                    ins = mm(acc[0:c * F2, 2 + n % 2, j // 2 * P:(j // 2 + 1) * P],
                             w_f1_pairs[0:kn * R, j * F2:(j + c) * F2], attrT[n % 2][0:kn * R, 0:P],
                             start=True, stop=True)
                ins.then_inc(flt_h, 1)

            def attr_filter(i, n, local):
                b, s, k0, kn = BODY_SUBS[n]
                n1 = i * len(BODY_SUBS) + (n + 1)
                if local:
                    pe.wait_ge(flt_weighted, n1)
                    if s == 0:
                        pe.wait_ge(pM.rows_in[b], (i + 1) * 16)
                    for j in range(kn):
                        at = (n % 2 * SUB + j) * F2
                        ins = mm(small[:, at:at + F2], ohT_m[n % 4][:, j * P:(j + 1) * P], win_rows(b, F2, F2),
                                 start=True, stop=True)
                    if s == NSUB - 1:
                        ins.then_inc(pM.rows_used, 1)
                mm(acc[:, 4 + n % 2, 0:kn * F2], ones_row[0:1, :], b_f2_sub[:, 0:kn * F2], start=True, stop=False)
                pe.wait_ge(flt_hid, n1)
                for j, c in pairs(kn):
                    ins = mm(acc[:, 4 + n % 2, j * F2:(j + c) * F2], hid[n % 2][0:c * F2, j // 2 * P:(j // 2 + 1) * P],
                             w_f2_pair[0:c * F2, 0:c * F2], start=False, stop=j + c == kn)
                ins.then_inc(flt_W, 1)

            def filters(i, last, local):
                for n in range(len(BODY_SUBS)):
                    if not last or n + 1 < len(BODY_SUBS):
                        attr_hidden(i, n + 1)
                    if not last or n + 2 < len(BODY_SUBS):
                        attr_T(i, n + 2, local)
                    attr_filter(i, n, local)

            begin(pe, "filters")
            def all_filters(local):
                attr_T(0, 0, local)
                attr_hidden(0, 0)
                attr_T(0, 1, local)
                with pe.Fori(0, ITERS - 1) as i:
                    filters(i, False, local)
                filters(ITERS - 1, True, local)

            pe.wait_ge(pair_loaded, 16 * len(pair_loads))
            pe.sem_inc(pM.rows_used, 2)
            with pe.If(pe.value_load(covered[0:1, 0:1], min_val=0, max_val=1)):
                all_filters(True)
            with pe.Else():
                all_filters(False)

            begin(pe, "passE")
            open_acc(P)
            pe.sem_inc(pE.oh_used, CREDIT)
            with pe.If(pe.value_load(covered_s[0:1, 0:1], min_val=0, max_val=1)):
                with pe.Fori(0, ITERS) as i:
                    _, offs = nc.values_load_multi_w_load_instructions(
                        blk_offs[0:1, bass.ds(i * 4, 4)], engines=[PE_ENGINE], min_val=0, max_val=NCH * BPSUM - NB,
                        skip_runtime_bounds_check_because="blocks of nodes by their number")
                    for b in range(2):
                        pe.wait_ge(pE.oh_ready, i * 2 + (b + 1))
                        pe.wait_ge(pE.part3, i * 2 + (b + 1))
                        for k in range(G):
                            for st in narrow(b, k):
                                for w in range(2):
                                    ins = mm(acc_row[0:st.shape[1], bass.ds(offs[2 * b + w], NB)], st,
                                             onehot_blks(b, w)[:, k, :], start=False, stop=False)
                        ins.then_inc(pE.oh_used, G)
            with pe.Else():
                all_nodes(pE, narrow)
            close_acc(P)
            dense("o1_mm", w_o1[:, :], va)
            dense("o2_mm", w_o2[:, :], va)
            layernorm("ln3", xT)
            for n, name in ((0, "tq"), (1, "tk"), (2, "tv")):
                table(name, hT, wsq[:, n, :], ROW["L3_gnn_b" + "QKV"[n]])
            scatter("passF", wide, pF, windows_F)
            dense("wo_mm", wsq[:, 3, :], va)
            layernorm("ln4", hT)
            dense("w1_mm", wsq[:, 4, :], hT)
            dense("w2_mm", wsq[:, 5, :], va)
            layernorm("ln5", hT)
            table("fin", xT, None)


_INS = ['x', 'src', 'dst', 'edge_attr_32', 'edge_weight', 'L0_gnn_W', 'L0_gnn_b', 'L0_gnn_att_src', 'L0_gnn_att_dst',
 'L2_gnn_w_in', 'L2_gnn_b_in', 'L2_gnn_w_f1', 'L2_gnn_b_f1', 'L2_gnn_w_f2', 'L2_gnn_b_f2', 'L2_gnn_w_o1',
 'L2_gnn_b_o1', 'L2_gnn_w_o2', 'L2_gnn_b_o2', 'L3_gnn_WQ', 'L3_gnn_bQ', 'L3_gnn_WK', 'L3_gnn_bK', 'L3_gnn_WV',
 'L3_gnn_bV', 'L3_gnn_WO', 'L3_gnn_bO', 'L3_gnn_W1', 'L3_gnn_b1', 'L3_gnn_W2', 'L3_gnn_b2', 'L3_gnn_ln1_g',
 'L3_gnn_ln1_b', 'L3_gnn_ln2_g', 'L3_gnn_ln2_b']


def kernel(**inputs):
    import numpy as _np
    import concourse.bacc as _bacc
    from concourse import mybir as _mybir
    from concourse.bass_utils import run_bass_kernel_spmd as _run

    nc = _bacc.Bacc("TRN2", target_bir_lowering=False, num_devices=1)
    arrays, args = {}, {}
    for name in _INS:
        a = _np.ascontiguousarray(inputs[name])
        arrays[f"in_{name}_dram"] = a
        args[name] = nc.dram_tensor(f"in_{name}_dram", a.shape, _mybir.dt.from_np(a.dtype), kind="ExternalInput").ap()
    out = nc.dram_tensor("out_0_dram", (3125, 128), _mybir.dt.float32, kind="ExternalOutput").ap()
    build(nc, args, out)
    r = _run(nc, [arrays], core_ids=[0])
    return r.results[0]["out_0_dram"]
```
